# Optimizing a Trainium2 kernel written in Bass

```python
import numpy as np
import jax
import jax.numpy as jnp

def _softmax(x, axis=-1):
    return jax.nn.softmax(x, axis=axis)

def _gelu(x):
    return jax.nn.gelu(x, approximate=True)

def _silu(x):
    return jax.nn.silu(x)

def _sigmoid(x):
    return jax.nn.sigmoid(x)

def _layernorm(x, axis=-1, eps=1e-05):
    m = jnp.mean(x, axis=axis, keepdims=True)
    v = jnp.var(x, axis=axis, keepdims=True)
    return (x - m) / jnp.sqrt(v + eps)

def _scatter_add(tgt, idx, src, axis=0):
    return tgt.at[idx].add(src)

def _segment_sum(src, seg, n):
    return jax.ops.segment_sum(src, seg, n)
kernel_name = 'mk_gnn_ffn_d2_gnn_r32_990f7c'

def setup_inputs(seed: int=0):
    np.random.seed(seed)
    _w = jnp.asarray

    def _rec_inputs():
        import jax
        import jax.numpy as jnp
        _gk = jax.random.key(seed)
        x = -0.0002117 + 1 * jax.random.normal(jax.random.fold_in(_gk, 1), (3125, 256), jnp.float32)
        _s = jax.random.randint(jax.random.fold_in(_gk, 2), (25000,), 0, 3125, jnp.int32)
        _d = jax.random.randint(jax.random.fold_in(_gk, 3), (25000,), 0, 3125, jnp.int32)
        _loop = jnp.arange(3125, dtype=jnp.int32)
        src = jnp.concatenate([_s, _d, _loop])
        dst = jnp.concatenate([_d, _s, _loop])
        _o = jnp.argsort(dst, stable=True)
        src = src[_o]
        dst = dst[_o]
        edge_weight = jax.random.uniform(jax.random.fold_in(_gk, 13), (53125,), jnp.float32, 0.0, 0.999994)
        return (x, src, dst, edge_weight)
    x, src, dst, edge_weight = _rec_inputs()

    def _L0_gnn_setup():
        import jax, jax.numpy as jnp
        import numpy as np
        N_NODES = 3125
        N_EDGES = 10000
        D_IN, D_HID, D_OUT = (256, 1024, 256)
        BN_EPS = 1e-05
        key = jax.random.key(seed)
        ks = jax.random.split(key, 6)
        x = jax.random.normal(ks[0], (N_NODES, D_IN), dtype=jnp.float32)
        edge_index = jax.random.randint(ks[1], (2, N_EDGES), 0, N_NODES, dtype=jnp.int64)
        W1 = jax.random.normal(ks[2], (D_IN, D_HID), dtype=jnp.float32) * (1.0 / np.sqrt(D_IN))
        b1 = jnp.zeros((D_HID,), dtype=jnp.float32)
        gamma = jnp.ones((D_HID,), dtype=jnp.float32)
        beta = jnp.zeros((D_HID,), dtype=jnp.float32)
        W2 = jax.random.normal(ks[3], (D_HID, D_OUT), dtype=jnp.float32) * (1.0 / np.sqrt(D_HID))
        b2 = jnp.zeros((D_OUT,), dtype=jnp.float32)
        return {'x': x, 'edge_index': edge_index, 'W1': W1, 'b1': b1, 'gamma': gamma, 'beta': beta, 'W2': W2, 'b2': b2}
    _L0_gnn_all = _L0_gnn_setup()
    _L0_gnn_in = {k: v for k, v in _L0_gnn_all.items() if k in ('W1', 'b1', 'gamma', 'beta', 'W2', 'b2')}
    del _L0_gnn_all

    def _L0_ffn_setup():
        import jax, jax.numpy as jnp
        import numpy as np
        NUM_EXPERTS = 8
        TOP_K = 2
        B, S, D = (8, 256, 256)

        def _moe(tokens, router_w, w1, b1, w2, b2):
            N = tokens.shape[0]
            E = router_w.shape[0]
            logits = tokens.astype(jnp.float32) @ router_w.astype(jnp.float32).T
            probs = jax.nn.softmax(logits, axis=-1)
            rw, re = jax.lax.top_k(probs, TOP_K)
            if TOP_K > 1:
                rw = rw / jnp.maximum(rw.sum(-1, keepdims=True), 1e-12)
            rw = rw.astype(tokens.dtype)
            combine = jnp.zeros((N, E), tokens.dtype).at[jnp.arange(N)[:, None], re].set(rw)
            out = tokens
            for e in range(E):
                h = jax.nn.gelu(tokens @ w1[e] + b1[e], approximate=False)
                y = h @ w2[e] + b2[e]
                out = out + combine[:, e:e + 1] * y
            return out
        key = jax.random.key(seed)
        ks = jax.random.split(key, 4)
        scale = 1.0 / np.sqrt(D).astype(np.float32)
        return {'input_embeddings': jax.random.normal(ks[0], (B, S, D), jnp.float32), 'router_w': jax.random.normal(ks[1], (NUM_EXPERTS, D), jnp.float32) * scale, 'w1': jax.random.normal(ks[2], (NUM_EXPERTS, D, D), jnp.float32) * scale, 'b1': jnp.zeros((NUM_EXPERTS, D), jnp.float32), 'w2': jax.random.normal(ks[3], (NUM_EXPERTS, D, D), jnp.float32) * scale, 'b2': jnp.zeros((NUM_EXPERTS, D), jnp.float32)}
    _L0_ffn_all = _L0_ffn_setup()
    _L0_ffn_in = {k: v for k, v in _L0_ffn_all.items() if k in ('router_w', 'w1', 'b1', 'w2', 'b2')}
    del _L0_ffn_all

    def _L1_gnn_setup():
        import jax, jax.numpy as jnp
        import numpy as np
        N_NODES, N_EDGES, F_IN, F_OUT = (10000, 10000, 256, 256)
        key = jax.random.key(seed)
        k1, k2, k3, k4, k5, k6 = jax.random.split(key, 6)
        feature = jax.random.normal(k1, (N_NODES, F_IN), jnp.float32)
        ew = jax.random.uniform(k2, (N_EDGES,), jnp.float32)
        src = jax.random.randint(k3, (N_EDGES,), 0, N_NODES)
        dst = jax.random.randint(k4, (N_EDGES,), 0, N_NODES)
        W = jax.random.normal(k5, (F_OUT, 2 * F_IN), jnp.float32) / np.sqrt(2 * F_IN)
        b = jax.random.normal(k6, (F_OUT,), jnp.float32) * 0.01
        return {'feature': feature, 'ew': ew, 'src': src, 'dst': dst, 'W': W, 'b': b}
    _L1_gnn_all = _L1_gnn_setup()
    _L1_gnn_in = {k: v for k, v in _L1_gnn_all.items() if k in ('W', 'b')}
    del _L1_gnn_all

    def _L1_ffn_setup():
        import jax, jax.numpy as jnp
        import numpy as np
        B, S, H, F, E, K = (8, 128, 256, 512, 16, 2)
        EPS = 1e-05
        key = jax.random.key(seed)
        ks = jax.random.split(key, 9)
        sc = 0.02
        return {'x': jax.random.normal(ks[0], (B, S, H), dtype=jnp.float32), 'gate_w': jax.random.normal(ks[1], (H, E), dtype=jnp.float32) * sc, 'gate_b': jnp.zeros((E,), dtype=jnp.float32), 'w1': jax.random.normal(ks[2], (E, H, F), dtype=jnp.float32) * sc, 'b1': jnp.zeros((E, F), dtype=jnp.float32), 'w2': jax.random.normal(ks[3], (E, F, H), dtype=jnp.float32) * sc, 'b2': jnp.zeros((E, H), dtype=jnp.float32), 'gamma': jnp.ones((H,), dtype=jnp.float32), 'beta': jnp.zeros((H,), dtype=jnp.float32)}
    _L1_ffn_all = _L1_ffn_setup()
    _L1_ffn_in = {k: v for k, v in _L1_ffn_all.items() if k in ('gate_w', 'gate_b', 'w1', 'b1', 'w2', 'b2', 'gamma', 'beta')}
    del _L1_ffn_all
    return {'x': x, 'src': src, 'dst': dst, 'edge_weight': edge_weight, 'L0_gnn_W1': _L0_gnn_in['W1'], 'L0_gnn_b1': _L0_gnn_in['b1'], 'L0_gnn_gamma': _L0_gnn_in['gamma'], 'L0_gnn_beta': _L0_gnn_in['beta'], 'L0_gnn_W2': _L0_gnn_in['W2'], 'L0_gnn_b2': _L0_gnn_in['b2'], 'L0_ffn_router_w': _L0_ffn_in['router_w'], 'L0_ffn_w1': _L0_ffn_in['w1'], 'L0_ffn_b1': _L0_ffn_in['b1'], 'L0_ffn_w2': _L0_ffn_in['w2'], 'L0_ffn_b2': _L0_ffn_in['b2'], 'L1_gnn_W': _L1_gnn_in['W'], 'L1_gnn_b': _L1_gnn_in['b'], 'L1_ffn_gate_w': _L1_ffn_in['gate_w'], 'L1_ffn_gate_b': _L1_ffn_in['gate_b'], 'L1_ffn_w1': _L1_ffn_in['w1'], 'L1_ffn_b1': _L1_ffn_in['b1'], 'L1_ffn_w2': _L1_ffn_in['w2'], 'L1_ffn_b2': _L1_ffn_in['b2'], 'L1_ffn_gamma': _L1_ffn_in['gamma'], 'L1_ffn_beta': _L1_ffn_in['beta']}

def reference(x, src, dst, edge_weight, L0_gnn_W1, L0_gnn_b1, L0_gnn_gamma, L0_gnn_beta, L0_gnn_W2, L0_gnn_b2, L0_ffn_router_w, L0_ffn_w1, L0_ffn_b1, L0_ffn_w2, L0_ffn_b2, L1_gnn_W, L1_gnn_b, L1_ffn_gate_w, L1_ffn_gate_b, L1_ffn_w1, L1_ffn_b1, L1_ffn_w2, L1_ffn_b2, L1_ffn_gamma, L1_ffn_beta):
    import jax
    import jax.numpy as jnp

    def _L0_gnn_ref(x, edge_index, W1, b1, gamma, beta, W2, b2):
        import jax, jax.numpy as jnp
        import numpy as np
        N_NODES = 3125
        N_EDGES = 10000
        D_IN, D_HID, D_OUT = (256, 1024, 256)
        BN_EPS = 1e-05
        src, dst = (edge_index[0], edge_index[1])
        agg = jax.ops.segment_sum(x[src], dst, num_segments=x.shape[0])
        h = agg + x
        h1 = h @ W1 + b1
        mean = jnp.mean(h1, axis=0)
        var = jnp.mean(jnp.square(h1 - mean), axis=0)
        h1 = (h1 - mean) * jax.lax.rsqrt(var + BN_EPS) * gamma + beta
        h1 = jax.nn.relu(h1)
        out = jax.nn.relu(h1 @ W2 + b2)
        return out

    def _L0_ffn_ref(input_embeddings, router_w, w1, b1, w2, b2):
        import jax, jax.numpy as jnp
        import numpy as np
        NUM_EXPERTS = 8
        TOP_K = 2
        B, S, D = (8, 256, 256)

        def _moe(tokens, router_w, w1, b1, w2, b2):
            N = tokens.shape[0]
            E = router_w.shape[0]
            logits = tokens.astype(jnp.float32) @ router_w.astype(jnp.float32).T
            probs = jax.nn.softmax(logits, axis=-1)
            rw, re = jax.lax.top_k(probs, TOP_K)
            if TOP_K > 1:
                rw = rw / jnp.maximum(rw.sum(-1, keepdims=True), 1e-12)
            rw = rw.astype(tokens.dtype)
            combine = jnp.zeros((N, E), tokens.dtype).at[jnp.arange(N)[:, None], re].set(rw)
            out = tokens
            for e in range(E):
                h = jax.nn.gelu(tokens @ w1[e] + b1[e], approximate=False)
                y = h @ w2[e] + b2[e]
                out = out + combine[:, e:e + 1] * y
            return out
        b, s, d = input_embeddings.shape
        tokens = input_embeddings.reshape(b * s, d)
        return _moe(tokens, router_w, w1, b1, w2, b2).reshape(b, s, d)

    def _L1_gnn_ref(feature, ew, src, dst, W, b):
        import jax, jax.numpy as jnp
        import numpy as np
        N_NODES, N_EDGES, F_IN, F_OUT = (10000, 10000, 256, 256)
        n = feature.shape[0]
        msg = feature[src[0]] * feature[src] * ew[:, None]
        sums = jax.ops.segment_sum(msg, dst, num_segments=n)
        cnt = jax.ops.segment_sum(jnp.ones((msg.shape[0],), msg.dtype), dst, num_segments=n)
        hm_mean = sums / jnp.maximum(cnt, 1.0)[:, None]
        x = jnp.concatenate([feature, hm_mean], axis=1)
        return jax.nn.relu(x @ W.T + b)

    def _L1_ffn_ref(x, gate_w, gate_b, w1, b1, w2, b2, gamma, beta):
        import jax, jax.numpy as jnp
        import numpy as np
        B, S, H, F, E, K = (8, 128, 256, 512, 16, 2)
        EPS = 1e-05
        gate_logits = x @ gate_w + gate_b
        topk_vals, topk_idx = jax.lax.top_k(gate_logits, K)
        topk_w = jax.nn.softmax(topk_vals, axis=-1)
        h = jax.nn.relu(jnp.einsum('bsh,ehf->bsef', x, w1) + b1)
        expert_out = jnp.einsum('bsef,efh->bseh', h, w2) + b2
        sel = jnp.take_along_axis(expert_out, topk_idx[:, :, :, None], axis=2)
        moe = jnp.sum(topk_w[..., None] * sel, axis=2)
        y = x + moe
        mu = jnp.mean(y, axis=-1, keepdims=True)
        var = jnp.var(y, axis=-1, keepdims=True)
        return (y - mu) / jnp.sqrt(var + EPS) * gamma + beta
    edge_index = jnp.stack([src, dst])
    x = x + _L0_gnn_ref(_layernorm(x, axis=-1), edge_index, L0_gnn_W1, L0_gnn_b1, L0_gnn_gamma, L0_gnn_beta, L0_gnn_W2, L0_gnn_b2)
    x = x + _L0_ffn_ref(_layernorm(x, axis=-1)[None], L0_ffn_router_w, L0_ffn_w1, L0_ffn_b1, L0_ffn_w2, L0_ffn_b2)[0]
    x = x + _L1_gnn_ref(_layernorm(x, axis=-1), edge_weight, src, dst, L1_gnn_W, L1_gnn_b)
    x = x + _L1_ffn_ref(_layernorm(x, axis=-1)[None], L1_ffn_gate_w, L1_ffn_gate_b, L1_ffn_w1, L1_ffn_b1, L1_ffn_w2, L1_ffn_b2, L1_ffn_gamma, L1_ffn_beta)[0]
    return x

_drawn_inputs = setup_inputs


def setup_inputs(seed=0):
    import zlib

    import numpy as np

    out = dict(_drawn_inputs(seed))
    spreads = {'L0_gnn_b1': (0.0, 0.8),
     'L0_gnn_gamma': (1.0, 0.2),
     'L0_gnn_beta': (0.0, 0.1),
     'L0_gnn_b2': (0.0, 0.1),
     'L0_ffn_b1': (0.0, 0.335),
     'L0_ffn_b2': (0.0, 0.1),
     'L1_ffn_gate_b': (0.0, 0.418),
     'L1_ffn_b1': (0.0, 0.8),
     'L1_ffn_b2': (0.0, 0.359),
     'L1_ffn_gamma': (1.0, 0.2),
     'L1_ffn_beta': (0.0, 0.274)}
    factors = {'edge_weight': 3.367, 'L1_gnn_b': 8.0, 'L1_ffn_w1': 2.975}
    for name, (base, spread) in spreads.items():
        noise = np.random.default_rng([zlib.crc32(name.encode()), seed]).standard_normal(out[name].shape)
        drawn = base * np.exp(spread * noise) if base else spread * noise
        out[name] = jnp.asarray(drawn.astype(out[name].dtype))
    for name, factor in factors.items():
        out[name] = (out[name] * factor).astype(out[name].dtype)
    return out
```

```python
import concourse.bass as bass
from concourse import mybir
from contextlib import ExitStack

fp32 = mybir.dt.float32
i32 = mybir.dt.int32
u32 = mybir.dt.uint32
ALU = mybir.AluOpType
ACT = mybir.ActivationFunctionType
AX = mybir.AxisListType
ds = bass.ds

N = 3125
D = 256
NE = 53125
P = 125
T = N // P
DC = D // 128
HID = 1024
HC = HID // 128
KS = 18
WIN = KS * 128
GROUP = 6
GROUPS = KS // GROUP
ROUNDS = -(-NE // WIN)
NE_PAD = 25 * WIN
NE_LEN = NE_PAD + ROUNDS * WIN
NO_NODE = 1 << 20
U = 5
LN_EPS = 1e-5


def moe_tiles(experts):
    return (2 * N - experts) // 128 + experts


def gnn_moe(nc, x, src, dst, edge_weight, L0_gnn_W1, L0_gnn_b1, L0_gnn_gamma, L0_gnn_beta, L0_gnn_W2,
            L0_gnn_b2, L0_ffn_router_w, L0_ffn_w1, L0_ffn_b1, L0_ffn_w2, L0_ffn_b2, L1_gnn_W, L1_gnn_b,
            L1_ffn_gate_w, L1_ffn_gate_b, L1_ffn_w1, L1_ffn_b1, L1_ffn_w2, L1_ffn_b2, L1_ffn_gamma,
            L1_ffn_beta, out):
    E0, E1 = L0_ffn_w1.shape[0], L1_ffn_w1.shape[0]
    F0, F1 = L0_ffn_w1.shape[2], L1_ffn_w1.shape[2]
    SLOTS = 128 * max(moe_tiles(E0), moe_tiles(E1))

    ctx = ExitStack()
    with ctx:
        def sb(name, shape, dt=fp32):
            return ctx.enter_context(nc.sbuf_tensor(name, shape, dt))

        stage_sems = []

        def sem(name):
            s = nc.alloc_semaphore(name)
            stage_sems.append(s)
            return s

        def end_stage():
            nc.clear_and_free_semaphores(list(stage_sems))
            stage_sems.clear()
            nc.all_engine_barrier()

        def dram(name, shape, dt=fp32):
            return nc.dram_tensor(name, shape, dt, kind="Internal").ap()

        src_pad = dram("src_pad", [NE_LEN], i32)
        dst_pad = dram("dst_pad", [NE_LEN], i32)
        ew_pad = dram("ew_pad", [NE_LEN])
        xn_dram = dram("xn_dram", [N, D])
        slots_in = dram("slots_in", [SLOTS, D])
        slots_out = dram("slots_out", [SLOTS, D])

        xres = sb("xres", [P, T, D])
        tok = sb("tok", [P, T, D])
        arena = sb("arena", [128, 32768])
        work = sb("work", [128, 4096])

        def view(t, at, dims, parts=128):
            size = 1
            for d in dims:
                size *= d
            flat = t[0:parts, at:at + size]
            names = "abcd"[:len(dims)]
            if len(dims) == 1:
                return flat
            return flat.rearrange(f"p ({' '.join(names)}) -> p {' '.join(names)}",
                                  **{n: d for n, d in zip(names, dims)})

        h1T = view(arena, 0, [HC, N])
        ROWS = HC * N
        rows = view(arena, ROWS, [KS, D + 1])
        masks = view(arena, ROWS + KS * (D + 1), [KS, P])
        x3 = view(arena, 16384, [T, D], P)
        w1g = view(work, 0, [DC, HID])
        bn6 = view(work, 2048, [HC, T, 6])
        hT = view(work, 3248, [2 * DC, P])
        w2g = view(arena, ROWS, [HC, D])
        b2g_bc = view(arena, ROWS + HC * D, [D])
        gb_bc = view(work, 2304, [D])
        wT = view(arena, 16384 + T * D, [2 * DC, D])
        wraw = view(arena, ROWS, [DC, 2 * D])

        ident = sb("ident", [128, 128])
        ones = sb("ones", [128, 128])
        before = sb("before", [P, P])
        node_row = sb("node_row", [128, P])
        node_base = sb("node_base", [128, T])
        expert_row = sb("expert_row", [128, 16])
        tile_start = sb("tile_start", [1, 64])
        eps = sb("eps", [128, 1])
        pad_i = sb("pad_i", [25, 179], i32)
        pad_z = sb("pad_z", [25, 179])
        meta_src = sb("meta_src", [128, U, KS], i32)
        meta_dst = sb("meta_dst", [128, U, KS], i32)
        meta_ew = sb("meta_ew", [128, U, KS])
        dst_local = sb("dst_local", [128, U, KS])
        table = sb("table", [1, T + 2])
        gaps = sb("gaps", [1, T])
        scal = sb("scal", [1, 4])
        starts = sb("starts", [1, T + 2], i32)
        rounds = sb("rounds", [1, 1], i32)
        degree = sb("degree", [P, T])
        rdegree = sb("rdegree", [P, T])
        summed = sb("summed", [P, 2, D + 1])
        mean_v = sb("mean_v", [P, T])
        mv = sb("mv", [P, T, 2])
        st6 = sb("st6", [P, T, 6])
        rstd = sb("rstd", [P, T])
        bnmv = sb("bnmv", [128, HC, 2])
        bn_scale = sb("bn_scale", [128, HC])
        bn_shift = sb("bn_shift", [128, HC])
        VROWS = 3 * HC + E0 * F0 // 128 + E1 * F1 // 128
        vec_rows = view(arena, 4352, [128], VROWS)
        vecs = sb("vecs", [128, VROWS])
        b1g, gam, bet = (vecs[:, i * HC:(i + 1) * HC] for i in range(3))
        EB0, EB1 = 3 * HC, 3 * HC + E0 * F0 // 128
        gateb_bc = sb("gateb_bc", [128, E1])
        router = view(arena, 4608, [D], E0)
        gateT = [sb("gateT0", [128, DC, E0]), sb("gateT1", [128, DC, E1])]
        g_col = sb("g_col", [128, DC])
        i_first = sb("i_first", [1, 1], i32)

        psum = [ctx.enter_context(nc.psum_tensor(f"bank{i}", [128, 512], fp32)) for i in range(8)]

        s_x = sem("s_x"); s_w = sem("s_w"); s_const = sem("s_const"); s_pad = sem("s_pad")
        s_dst = sem("s_dst"); s_tr = sem("s_tr"); s_dve = sem("s_dve"); s_cnt = sem("s_cnt")
        s_zero = sem("s_zero"); s_wg = sem("s_wg")

        def chain(eng, s):
            n = [0]

            def link(ins):
                n[0] += 1
                ins.then_inc(s, 1)
                eng.wait_ge(s, n[0])
            link.count = n
            return link

        dst_a = view(arena, 2048, [NE // P], P).bitcast(i32)
        dst_b = view(arena, 2560, [NE // P], P).bitcast(i32)
        dst_f = view(arena, 3072, [NE // P], P)
        lt = view(arena, 3584, [NE // P], P)
        cols = view(arena, 4096, [T + 2], P)
        zeros = view(arena, 8192, [4096])

        with nc.Block() as block:
            @block.sync
            def _(sp):
                sp.dma_start(dst_pad[0:NE].rearrange("(p c) -> p c", p=P), dst.rearrange("(p c) -> p c", p=P)).then_inc(s_pad, 16)
                sp.dma_start(xres[:, :, :], x.rearrange("(t p) d -> p t d", p=P)).then_inc(s_x, 16)
                sp.dma_start(src_pad[0:NE].rearrange("(p c) -> p c", p=P), src.rearrange("(p c) -> p c", p=P)).then_inc(s_pad, 16)
                sp.dma_start(ew_pad[0:NE].rearrange("(p c) -> p c", p=P), edge_weight.rearrange("(p c) -> p c", p=P)).then_inc(s_pad, 16)
                sp.dma_start(dst_a, dst.rearrange("(p c) -> p c", p=P)).then_inc(s_dst, 16)
                sp.wait_ge(s_const, 3)
                tail = lambda a: a[NE:NE_PAD].rearrange("(p c) -> p c", p=25)
                sp.dma_start(tail(dst_pad), pad_i[:, :]).then_inc(s_pad, 16)
                sp.dma_start(tail(src_pad), pad_z[:, :].bitcast(i32)).then_inc(s_pad, 16)
                sp.dma_start(tail(ew_pad), pad_z[:, :]).then_inc(s_pad, 16)
                sp.wait_ge(s_pad, 16 * 6)
                sp.dma_start(dst_b, dst_pad[1:NE + 1].rearrange("(p c) -> p c", p=P)).then_inc(s_dst, 16)
                for n in range(SLOTS * D // (128 * 4096)):
                    sp.dma_start(slots_in[n * 2048:(n + 1) * 2048, :].rearrange("(p r) d -> p (r d)", p=128),
                                 zeros).then_inc(s_zero, 16)
                sp.wait_ge(s_x, 16)
                sp.wait_ge(s_dst, 32)
                sp.wait_ge(s_zero, 16 * (SLOTS * D // (128 * 4096)))

            @block.scalar
            def _(act):
                act.dma_start(vec_rows[0:HC, :], L0_gnn_b1.rearrange("(m p) -> m p", p=128)).then_inc(s_w, 16)
                act.dma_start(vec_rows[HC:2 * HC, :], L0_gnn_gamma.rearrange("(m p) -> m p", p=128)).then_inc(s_w, 16)
                act.dma_start(vec_rows[2 * HC:3 * HC, :], L0_gnn_beta.rearrange("(m p) -> m p", p=128)).then_inc(s_w, 16)
                act.dma_start(vec_rows[EB0:EB1, :], L0_ffn_b1.rearrange("e (c p) -> (e c) p", p=128)).then_inc(s_w, 16)
                act.dma_start(vec_rows[EB1:VROWS, :], L1_ffn_b1.rearrange("e (c p) -> (e c) p", p=128)).then_inc(s_w, 16)
                act.dma_start(router[:, :], L0_ffn_router_w).then_inc(s_w, 16)
                act.dma_start(w1g, L0_gnn_W1.rearrange("(c p) h -> p c h", p=128)).then_inc(s_wg, 16)
                act.dma_start(gateT[1][:, :, :], L1_ffn_gate_w.rearrange("(c p) e -> p c e", p=128)).then_inc(s_wg, 16)
                act.dma_start(gateb_bc[:, :], L1_ffn_gate_b.partition_broadcast(128)).then_inc(s_wg, 16)
                act.dma_start(i_first[:, :], src[0:1].rearrange("(a n) -> a n", a=1)).then_inc(s_wg, 16)
                act.wait_ge(s_wg, 16 * 4)

            @block.gpsimd
            def _(pool):
                pool.memset(pad_i[:, :], NO_NODE).then_inc(s_const, 1)
                pool.memset(pad_z[:, :], 0.0).then_inc(s_const, 1)
                pool.memset(zeros, 0.0).then_inc(s_const, 1)
                pool.memset(ident[:, :], 0.0).then_inc(s_const, 1)
                pool.memset(ones[:, :], 1.0).then_inc(s_const, 1)
                pool.memset(before[:, :], 1.0).then_inc(s_const, 1)
                pool.memset(eps[:, :], LN_EPS).then_inc(s_const, 1)
                pool.iota(node_row[:, :], [[1, P]], base=0, channel_multiplier=0,
                          allow_small_or_imprecise_dtypes=True).then_inc(s_const, 1)
                pool.iota(node_base[:, :], [[P, T]], base=0, channel_multiplier=0,
                          allow_small_or_imprecise_dtypes=True).then_inc(s_const, 1)
                pool.iota(expert_row[:, :], [[1, 16]], base=0, channel_multiplier=0,
                          allow_small_or_imprecise_dtypes=True).then_inc(s_const, 1)
                pool.iota(tile_start[:, :], [[128, 64]], base=0, channel_multiplier=0,
                          allow_small_or_imprecise_dtypes=True).then_inc(s_const, 1)
                pool.memset(degree[:, :], 0.0).then_inc(s_const, 1)
                pool.wait_ge(s_const, 12)
                pool.affine_select(out=ident[:, :], in_=ident[:, :], compare_op=ALU.not_equal, fill=1.0,
                                   base=0, pattern=[[-1, 128]], channel_multiplier=1).then_inc(s_const, 1)
                pool.affine_select(out=before[:, :], in_=before[:, :], compare_op=ALU.is_gt, fill=0.0,
                                   base=0, pattern=[[1, P]], channel_multiplier=-1).then_inc(s_const, 1)

            @block.tensor
            def _(pe):
                pe.wait_ge(s_const, 14)
                pe.wait_ge(s_w, 16 * 6)
                nc.tensor.transpose(psum[0][:, 0:VROWS], vec_rows[:, :], ident[0:VROWS, 0:VROWS])
                for c in range(DC):
                    last = nc.tensor.transpose(psum[1][:, c * E0:(c + 1) * E0], router[:, c * 128:(c + 1) * 128], ident[0:E0, 0:E0])
                last.then_inc(s_tr, 1)
                pe.wait_ge(s_cnt, 1)
                nc.tensor.matmul(psum[4][0:1, 0:T + 2], ones[0:P, 0:1], cols, start=True, stop=True).then_inc(s_tr, 1)

            @block.vector
            def _(dve):
                link = chain(dve, s_dve)
                dve.wait_ge(s_const, 14)
                link(nc.vector.memset(cols, 0.0))
                dve.wait_ge(s_dst, 32)
                link(nc.vector.tensor_copy(dst_f, dst_a))
                for t in range(1, T):
                    link(nc.vector.tensor_scalar(lt, dst_f, float(t * P), None, ALU.is_lt))
                    link(nc.vector.tensor_reduce(cols[:, t:t + 1], lt, AX.X, ALU.add))
                link(nc.vector.tensor_copy(lt, dst_b))
                link(nc.vector.tensor_tensor(lt, lt, dst_f, ALU.is_lt))
                nc.vector.tensor_reduce(cols[:, T + 1:T + 2], lt, AX.X, ALU.add).then_inc(s_cnt, 1)
                dve.wait_ge(s_tr, 2)
                nc.vector.tensor_copy(vecs[:, :], psum[0][:, 0:VROWS])
                nc.vector.tensor_copy(gateT[0][:, :, :], psum[1][:, 0:DC * E0].rearrange("p (c e) -> p c e", c=DC))
                link(nc.vector.tensor_copy(table[:, :], psum[4][0:1, 0:T + 2]))
                link(nc.vector.memset(table[:, T:T + 1], float(NE)))
                link(nc.vector.tensor_tensor(gaps[:, :], table[:, 1:T + 1], table[:, 0:T], ALU.subtract))
                link(nc.vector.tensor_reduce(scal[:, 0:1], gaps[:, :], AX.X, ALU.max))
                link(nc.vector.tensor_scalar(scal[:, 0:1], scal[:, 0:1], float(WIN), None, ALU.is_gt))
                link(nc.vector.tensor_scalar(scal[:, 1:2], table[:, T + 1:T + 2], 0.0, None, ALU.is_gt))
                link(nc.vector.tensor_tensor(scal[:, 2:3], scal[:, 0:1], scal[:, 1:2], ALU.max))
                link(nc.vector.tensor_scalar(rounds[:, :], scal[:, 2:3], float(ROUNDS - 1), 1.0, ALU.mult, ALU.add))
                link(nc.vector.tensor_scalar(scal[:, 3:4], scal[:, 2:3], -1.0, 1.0, ALU.mult, ALU.add))
                link(nc.vector.tensor_scalar(starts[:, :], table[:, :], scal[:, 3:4], None, ALU.mult))

        def layer_norm(tag, xin, xout, store, first=False, keep=None, affine=None):
            s_st = sem(f"s_st{tag}"); s_var = sem(f"s_var{tag}"); s_n = sem(f"s_n{tag}"); s_io = sem(f"s_io{tag}")
            with nc.Block() as block:
                @block.vector
                def _(dve):
                    for t in range(T):
                        nc.vector.bn_stats(st6[:, t, :], xin[:, t, :]).then_inc(s_st, 1)
                    for t in range(T):
                        dve.wait_ge(s_st, t + 1)
                        nc.vector.bn_aggr(mv[:, t, :], st6[:, t, :]).then_inc(s_st, 1)
                    dve.wait_ge(s_var, 1)
                    nc.vector.reciprocal(rstd[:, :], mean_v[:, :]).then_inc(s_st, 1)
                    dve.wait_ge(s_st, 2 * T + 1)
                    for t in range(T):
                        nc.vector.tensor_scalar(xout[:, t, :], xin[:, t, :], mv[:, t, 0:1], rstd[:, t:t + 1],
                                                ALU.subtract, ALU.mult).then_inc(s_n, 1)

                @block.scalar
                def _(act):
                    if keep is not None:
                        nc.scalar.copy(keep[:, :, :], xin[:, :, :])
                    act.wait_ge(s_st, 2 * T)
                    nc.scalar.activation(mean_v[:, :], mv[:, :, 1], ACT.Sqrt, bias=eps[0:P, :]).then_inc(s_var, 1)

                @block.sync
                def _(sp):
                    if store is not None:
                        dst_v = store.rearrange("(t p) d -> p t d", p=P)
                        for b in range(T // U):
                            sp.wait_ge(s_n, (b + 1) * U)
                            sp.dma_start(dst_v[:, b * U:(b + 1) * U, :], xout[:, b * U:(b + 1) * U, :]).then_inc(s_io, 16)
                        sp.wait_ge(s_io, 16 * (T // U))

        def graph(layer):
            weighted = layer == 1
            s_meta = [sem(f"s_meta{layer}_{w}") for w in range(U)]
            s_row = [sem(f"s_row{layer}_{j}") for j in range(KS)]
            s_local = sem(f"s_local{layer}"); s_mask = sem(f"s_mask{layer}"); s_used = sem(f"s_used{layer}")
            s_sum = sem(f"s_sum{layer}"); s_kept = sem(f"s_kept{layer}"); s_t = sem(f"s_t{layer}")
            s_ht = sem(f"s_ht{layer}"); s_proj = sem(f"s_proj{layer}"); s_post = sem(f"s_post{layer}")
            s_f = sem(f"s_f{layer}"); s_one = sem(f"s_one{layer}")
            s_nop = sem(f"s_nop{layer}"); s_nop2 = sem(f"s_nop2{layer}"); s_tmp = sem(f"s_tmp{layer}")
            W = D if weighted else D + 1
            META = 64 if weighted else 48
            TC = U if weighted else 0
            CREDIT = U * GROUPS
            fbuf = view(work, 0, [U, D], P)
            hm = view(work, U * D, [2, D], P)
            relu_in = view(work, (U + 2) * D, [2, D], P)
            with nc.Block() as block:
                def windows(eng, body):
                    n = eng.value_load(rounds[0:1, 0:1], min_val=1, max_val=ROUNDS)
                    with eng.Fori(0, n) as r:
                        with eng.Fori(0, T // U) as b:
                            for w in range(U):
                                body(r, r * T + b * U + w, b * U + w, w, r * (T // U) + b)

                @block.sync
                def _(sp):
                    def body(r, g, t, w, rb):
                        sp.wait_ge(s_used, CREDIT + (g - U + 1) * GROUPS)
                        if weighted:
                            sp.sem_inc(s_nop2, 1)
                            sp.wait_ge(s_t, U + g - U + 1)
                        sp.sem_inc(s_nop2, 1)
                        at = sp.value_load(starts[0:1, ds(t, 1)], min_val=0, max_val=NE)
                        at = sp.snap(at + r * WIN)
                        for to, frm in ((meta_src, src_pad), (meta_dst, dst_pad), (meta_ew, ew_pad)):
                            sp.dma_start(to[:, w, :], frm[ds(at, WIN)].rearrange("(p j) -> p j", j=KS)).then_inc(s_meta[w], 16)
                        if weighted:
                            sp.dma_start(fbuf[:, w, :], xn_dram[ds(t * P, P), :]).then_inc(s_meta[w], 16)
                    windows(sp, body)


                @block.gpsimd
                def _(pool):
                    nc.gpsimd.memset(rows[:, :, D:D + 1], 1.0).then_inc(s_one, 1)
                    nc.gpsimd.memset(tok[:, :, :], 0.0).then_inc(s_one, 1) if weighted else None

                    def body(r, g, t, w, rb):
                        pool.wait_ge(s_meta[w], (rb + 1) * META)
                        pool.sem_inc(s_nop, 1)
                        for j in range(KS):
                            if j % GROUP == 0:
                                pool.wait_ge(s_used, CREDIT + (g - 1) * GROUPS + j // GROUP + 1)
                                pool.sem_inc(s_nop, 1)
                            nc.gpsimd.indirect_dma_start(
                                out=rows[:, j, 0:D], out_offset=None, in_=xn_dram[:, :],
                                in_offset=bass.IndirectOffsetOnAxis(ap=meta_src[:, w, j:j + 1], axis=0)).then_inc(s_row[j], 16)
                    windows(pool, body)

                @block.vector
                def _(dve):
                    dve.wait_ge(s_one, 2 if weighted else 1)
                    LOCAL = 1

                    def body(r, g, t, w, rb):
                        dve.wait_ge(s_meta[w], (rb + 1) * META)
                        nc.vector.tensor_scalar(dst_local[:, w, :], meta_dst[:, w, :], node_base[:, ds(t, 1)], None,
                                                ALU.subtract).then_inc(s_local, 1)
                        dve.wait_ge(s_local, g + 1)
                        for j in range(KS):
                            if j % GROUP == 0:
                                dve.wait_ge(s_used, CREDIT + (g - 1) * GROUPS + j // GROUP + 1)
                            if weighted:
                                m = nc.vector.tensor_scalar(masks[:, j, :], node_row[:, :], dst_local[:, w, j:j + 1],
                                                            meta_ew[:, w, j:j + 1], ALU.is_equal, ALU.mult)
                            else:
                                m = nc.vector.tensor_scalar(masks[:, j, :], node_row[:, :], dst_local[:, w, j:j + 1],
                                                            None, ALU.is_equal)
                            if j % GROUP == GROUP - 1:
                                m.then_inc(s_mask, 1)
                        acc = psum[w % 2]
                        dve.wait_ge(s_used, CREDIT + (g + 1) * GROUPS)
                        last_use = g - 1 if w else g
                        dve.wait_ge(s_kept, last_use)
                        dve.wait_ge(s_t, last_use + TC)
                        nc.vector.tensor_tensor(summed[:, w % 2, 0:D], acc[0:P, 0:D], tok[:, ds(t, 1), :],
                                                ALU.add).then_inc(s_sum, 1)
                        if not weighted:
                            nc.vector.tensor_tensor(degree[:, ds(t, 1)], acc[0:P, D:D + 1], degree[:, ds(t, 1)],
                                                    ALU.add).then_inc(s_sum, 1)
                            for q in range(2):
                                dve.wait_ge(s_proj, 2 * g + q + 1)
                                nc.vector.tensor_tensor(
                                    h1T[:, 4 * q:4 * q + 4, ds(t * P, P)],
                                    psum[4 + q][:, 0:4 * P].rearrange("p (m n) -> p m n", m=4),
                                    b1g[:, 4 * q:4 * q + 4].unsqueeze(2).broadcast_to([128, 4, P]), ALU.add).then_inc(s_post, 1)
                            for m in range(HC):
                                if m % 4 == 0:
                                    dve.wait_ge(s_post, 2 * g + m // 4 + 1)
                                last = nc.vector.bn_stats(bn6[:, m, ds(t, 1), :], h1T[:, m, ds(t * P, P)])
                        else:
                            dve.wait_ge(s_sum, g + 1)
                            nc.vector.tensor_scalar(hm[:, w % 2, :], summed[:, w % 2, 0:D], rdegree[:, ds(t, 1)], None,
                                                    ALU.mult).then_inc(s_post, 1)
                            dve.wait_ge(s_proj, g + 1)
                            nc.vector.tensor_tensor(relu_in[:, w % 2, :], psum[4 + w % 2][0:P, 0:D], gb_bc[0:P, :],
                                                    ALU.add).then_inc(s_tmp, 1)
                            dve.wait_ge(s_tmp, g + 1)
                            nc.vector.scalar_tensor_tensor(x3[:, ds(t, 1), :], relu_in[:, w % 2:w % 2 + 1, :], 0.0,
                                                           xres[:, ds(t, 1), :], ALU.max, ALU.add)
                    windows(dve, body)

                @block.tensor
                def _(pe):
                    pe.sem_inc(s_used, CREDIT)
                    if weighted:
                        pe.sem_inc(s_t, TC)
                    pe.wait_ge(s_one, 1)
                    SUMS = 1 if weighted else 2

                    def body(r, g, t, w, rb):
                        acc = psum[w % 2]
                        if w >= 1:
                            pe.wait_ge(s_sum, (g - 1) * SUMS)
                        else:
                            pe.wait_ge(s_sum, g * SUMS)
                        for j in range(KS):
                            if j % GROUP == 0:
                                pe.wait_ge(s_mask, g * GROUPS + j // GROUP + 1)
                            pe.wait_ge(s_row[j], (g + 1) * 16)
                            m = nc.tensor.matmul(acc[0:P, 0:W], masks[:, j, :], rows[:, j, 0:W], start=(j == 0), stop=(j == KS - 1))
                            if j % GROUP == GROUP - 1:
                                m.then_inc(s_used, 1)
                        pe.wait_ge(s_sum, (g + 1) * SUMS)
                        if not weighted:
                            for c in range(DC):
                                last = nc.tensor.transpose(psum[2][:, c * P:(c + 1) * P], summed[:, w % 2, c * 128:(c + 1) * 128],
                                                           ident[0:P, 0:P])
                            last.then_inc(s_t, 1)
                            pe.wait_ge(s_ht, g + 1)
                            pe.wait_ge(s_post, 2 * g)
                            for q in range(2):
                                for m in range(4):
                                    for c in range(DC):
                                        last = nc.tensor.matmul(psum[4 + q][:, m * P:(m + 1) * P],
                                                                w1g[:, c, (4 * q + m) * 128:(4 * q + m + 1) * 128],
                                                                hT[:, c, :], start=(c == 0), stop=(c == DC - 1))
                                last.then_inc(s_proj, 1)
                        else:
                            pe.wait_ge(s_post, g + 1)
                            pe.wait_ge(s_meta[w], (rb + 1) * META)
                            for c in range(2 * DC):
                                frm = fbuf[:, w, c * 128:(c + 1) * 128] if c < DC else hm[:, w % 2, (c - DC) * 128:(c - DC + 1) * 128]
                                last = nc.tensor.transpose(psum[2][:, c * P:(c + 1) * P], frm, ident[0:P, 0:P])
                            last.then_inc(s_t, 1)
                            pe.wait_ge(s_ht, g + 1)
                            pe.wait_ge(s_tmp, g - 1 if w >= 1 else g)
                            for c in range(2 * DC):
                                last = nc.tensor.matmul(psum[4 + w % 2][0:P, 0:D], hT[:, c, :], wT[:, c, :],
                                                        start=(c == 0), stop=(c == 2 * DC - 1))
                            last.then_inc(s_proj, 1)
                    windows(pe, body)

                @block.scalar
                def _(act):
                    if weighted:
                        first = act.value_load(i_first[0:1, 0:1], min_val=0, max_val=N - 1)
                        act.dma_start(g_col[:, :], xn_dram[ds(first, 1), :].rearrange("a (c p) -> p (a c)", p=128),
                                      allow_slow_non_contiguous=True).then_inc(s_f, 16)
                        act.wait_ge(s_f, 16)

                    def body(r, g, t, w, rb):
                        act.wait_ge(s_sum, (g + 1) * (1 if weighted else 2))
                        nc.scalar.copy(tok[:, ds(t, 1), :], summed[:, w % 2:w % 2 + 1, 0:D]).then_inc(s_kept, 1)
                        if not weighted:
                            act.wait_ge(s_t, g + 1)
                            nc.scalar.copy(hT[:, 0:DC, :], psum[2][:, 0:DC * P].rearrange("p (c n) -> p c n", c=DC)).then_inc(s_ht, 1)
                        else:
                            act.wait_ge(s_t, g + 1 + TC)
                            nc.scalar.copy(hT[:, 0:DC, :], psum[2][:, 0:DC * P].rearrange("p (c n) -> p c n", c=DC))
                            for c in range(DC):
                                a = nc.scalar.activation(hT[:, DC + c, :], psum[2][:, (DC + c) * P:(DC + c + 1) * P], ACT.Copy,
                                                         scale=g_col[:, c:c + 1])
                            a.then_inc(s_ht, 1)
                    windows(act, body)

        def first_layer_end():
            s_w2 = sem("s_w2"); s_bn = sem("s_bn"); s_bns = sem("s_bns"); s_norm = sem("s_norm")
            s_y = sem("s_y"); s_ycopy = sem("s_ycopy"); s_yx = sem("s_yx")
            ysum = view(work, 0, [2, D], P)
            with nc.Block() as block:
                @block.sync
                def _(sp):
                    sp.dma_start(w2g, L0_gnn_W2.rearrange("(m p) d -> p m d", p=128)).then_inc(s_w2, 16)
                    sp.dma_start(b2g_bc, L0_gnn_b2.partition_broadcast(128)).then_inc(s_w2, 16)
                    sp.wait_ge(s_w2, 32)

                @block.vector
                def _(dve):
                    link = chain(dve, s_bn)
                    for m in range(HC):
                        nc.vector.bn_aggr(bnmv[:, m, :], bn6[:, m, :, :].rearrange("p t s -> p (t s)")).then_inc(s_bn, 1)
                    dve.wait_ge(s_bns, 1)
                    link.count[0] = HC
                    link(nc.vector.reciprocal(bn_scale[:, :], bn_shift[:, :]))
                    link(nc.vector.tensor_tensor(bn_scale[:, :], bn_scale[:, :], gam, ALU.mult))
                    link(nc.vector.tensor_tensor(bn_shift[:, :], bnmv[:, :, 0], bn_scale[:, :], ALU.mult))
                    link(nc.vector.tensor_tensor(bn_shift[:, :], bet, bn_shift[:, :], ALU.subtract))
                    dve.wait_ge(s_w2, 32)
                    for t in range(T):
                        dve.wait_ge(s_y, t + 1)
                        nc.vector.tensor_tensor(ysum[:, t % 2, :], psum[t % 2][0:P, 0:D], b2g_bc[0:P, :], ALU.add).then_inc(s_ycopy, 1)
                        dve.wait_ge(s_ycopy, t + 1)
                        nc.vector.scalar_tensor_tensor(xres[:, t, :], ysum[:, t % 2, :], 0.0, xres[:, t, :],
                                                       ALU.max, ALU.add).then_inc(s_yx, 1)

                @block.scalar
                def _(act):
                    act.wait_ge(s_bn, HC)
                    nc.scalar.activation(bn_shift[:, :], bnmv[:, :, 1], ACT.Sqrt, bias=eps[:, :]).then_inc(s_bns, 1)
                    act.wait_ge(s_bn, HC + 4)
                    for b in range(T // U):
                        for m in range(HC):
                            part = h1T[:, m, b * U * P:(b + 1) * U * P]
                            nc.scalar.activation(part, part, ACT.Relu, bias=bn_shift[:, m:m + 1],
                                                 scale=bn_scale[:, m:m + 1]).then_inc(s_norm, 1)

                @block.tensor
                def _(pe):
                    pe.wait_ge(s_w2, 32)
                    for t in range(T):
                        if t >= 2:
                            pe.wait_ge(s_ycopy, t - 1)
                        for m in range(HC):
                            if t % U == 0:
                                pe.wait_ge(s_norm, t // U * HC + m + 1)
                            last = nc.tensor.matmul(psum[t % 2][0:P, 0:D], h1T[:, m, t * P:(t + 1) * P], w2g[:, m, :],
                                                    start=(m == 0), stop=(m == HC - 1))
                        last.then_inc(s_y, 1)

        def moe(layer, E, F, w1, w2, b2, act_fn, softmax_first):
            NT = moe_tiles(E)
            FC = F // 128
            eb = EB0 if layer == 0 else EB1
            TE = T * E
            at = [0]

            def small(dims, parts=P, dt=fp32):
                v = view(arena, 16384 + at[0], dims, parts)
                size = 1
                for d in dims:
                    size *= d
                at[0] += size + size % 2
                return v if dt is fp32 else v.bitcast(dt)
            W1AT, W2AT = 0, E * DC * F
            w1s = view(arena, W1AT, [E * DC * F])
            w2s = view(arena, W2AT, [E * FC * D])
            tT = view(work, 0, [4, DC, P])
            lg = small([T, E]); v8 = small([T, 8]); i8 = small([T, 8], dt=u32); ex = small([T, 8]); zs = small([T])
            idf = small([T, 2]); sel = [small([T, E]), small([T, E])]; both = small([T, E]); tot = small([T, E])
            pp = [small([T, E]), small([T, E])]; posf = small([T, E])
            cf = small([E]); ci = small([E], dt=i32); padded = small([E]); ends = [small([E]), small([E])]
            base = small([E]); tcmp = small([NT, E], 1); tcount = small([NT], 1)
            wts, pos, comb, tile_expert = moe_keep[layer]
            s_lt = sem(f"s_lt{layer}"); s_lc = sem(f"s_lc{layer}"); s_lg = sem(f"s_lg{layer}"); s_top = sem(f"s_top{layer}")
            s_ex = sem(f"s_ex{layer}"); s_pre = sem(f"s_pre{layer}"); s_sc = sem(f"s_sc{layer}"); s_wl = sem(f"s_wl{layer}")
            s_bth = sem(f"s_bth{layer}")

            def steps(r):
                s = 1
                while s < r:
                    yield s
                    s *= 2

            with nc.Block() as block:
                POS = {}

                def logits(pe, t):
                    pe.wait_ge(s_lc, t + 1)
                    for c in range(DC):
                        last = nc.tensor.matmul(psum[2][0:P, t * E:(t + 1) * E], tT[:, t % 4, c, :], gateT[layer][:, c, :],
                                                start=(c == 0), stop=(c == DC - 1))
                    last.then_inc(s_lg, 1)

                @block.sync
                def _(sp):
                    if layer == 0:
                        for e in range(E):
                            sp.dma_start(w1s[:, e * DC * F:(e + 1) * DC * F].rearrange("p (c f) -> p c f", c=DC),
                                         w1[e].rearrange("(c p) f -> p c f", p=128)).then_inc(s_wl, 16)
                            sp.dma_start(w2s[:, e * FC * D:(e + 1) * FC * D].rearrange("p (c d) -> p c d", c=FC),
                                         w2[e].rearrange("(c p) d -> p c d", p=128)).then_inc(s_wl, 16)
                        sp.wait_ge(s_wl, 32 * E)
                    else:
                        for e in range(E):
                            sp.dma_start(w1s[:, e * DC * F:(e + 1) * DC * F].rearrange("p (c f) -> p c f", c=DC),
                                         w1[e].rearrange("(c p) f -> p c f", p=128)).then_inc(s_wl, 16)
                        sp.wait_ge(s_wl, 16 * E)

                @block.tensor
                def _(pe):
                    for t in range(T):
                        if t >= 2:
                            pe.wait_ge(s_lc, t - 1)
                        for c in range(DC):
                            last = nc.tensor.transpose(psum[t % 2][:, c * P:(c + 1) * P], tok[:, t, c * 128:(c + 1) * 128],
                                                       ident[0:P, 0:P])
                        last.then_inc(s_lt, 1)
                        if t >= 1:
                            logits(pe, t - 1)
                    logits(pe, T - 1)
                    pe.wait_ge(s_bth, 1)
                    bf = both.rearrange("p t e -> p (t e)")
                    nc.tensor.matmul(psum[3][0:P, 0:TE], before[:, :], bf, start=True, stop=True).then_inc(s_pre, 1)
                    nc.tensor.matmul(psum[4][0:P, 0:TE], ones[0:P, 0:P], bf, start=True, stop=True).then_inc(s_pre, 1)

                @block.vector
                def _(dve):
                    link = chain(dve, s_top)
                    pt = psum[2][0:P, 0:TE].rearrange("p (t e) -> p t e", e=E)

                    def spread(a, n):
                        return a.unsqueeze(2).broadcast_to([P, T, n])

                    def over(a, n=T, p=P):
                        return a.unsqueeze(1).broadcast_to([p, n, E])

                    dve.wait_ge(s_lg, T)
                    if layer == 0:
                        link(nc.vector.tensor_copy(lg, pt))
                    else:
                        link(nc.vector.tensor_tensor(lg, pt, over(gateb_bc[0:P, 0:E]), ALU.add))
                    for t in range(T):
                        nc.vector.max(v8[:, t, :], lg[:, t, :]).then_inc(s_top, 1)
                    for t in range(T):
                        dve.wait_ge(s_top, 1 + t + 1)
                        nc.vector.max_index(i8[:, t, :], v8[:, t, :], lg[:, t, :]).then_inc(s_top, 1)
                    link.count[0] += 2 * T
                    dve.wait_ge(s_top, link.count[0])
                    n = 8 if softmax_first else 2
                    link(nc.vector.tensor_tensor(ex[:, :, 0:n], v8[:, :, 0:n], v8[:, :, 0:1].broadcast_to([P, T, n]), ALU.subtract))
                    POS["shifted"] = link.count[0]
                    link(nc.vector.tensor_copy(idf, i8[:, :, 0:2]))
                    for k in range(2):
                        link(nc.vector.tensor_tensor(sel[k], over(expert_row[0:P, 0:E]), spread(idf[:, :, k], E), ALU.is_equal))
                    nc.vector.tensor_tensor(both, sel[0], sel[1], ALU.add).then_inc(s_bth, 1)
                    dve.wait_ge(s_ex, 1)
                    if softmax_first:
                        link(nc.vector.tensor_reduce(zs, ex, AX.X, ALU.add))
                        link(nc.vector.reciprocal(zs, zs))
                        link(nc.vector.tensor_tensor(ex[:, :, 0:2], ex[:, :, 0:2], spread(zs, 2), ALU.mult))
                    link(nc.vector.tensor_tensor(zs, ex[:, :, 0], ex[:, :, 1], ALU.add))
                    if softmax_first:
                        link(nc.vector.tensor_scalar(zs, zs, 1e-12, None, ALU.max))
                    link(nc.vector.reciprocal(zs, zs))
                    link(nc.vector.tensor_tensor(wts[:, :, :], ex[:, :, 0:2], spread(zs, 2), ALU.mult))
                    link(nc.vector.tensor_tensor(comb, sel[0], spread(wts[:, :, 0], E), ALU.mult))
                    link(nc.vector.tensor_tensor(posf, sel[1], spread(wts[:, :, 1], E), ALU.mult))
                    link(nc.vector.tensor_tensor(comb, comb, posf, ALU.add))
                    dve.wait_ge(s_pre, 2)
                    link(nc.vector.tensor_copy(tot, psum[4][0:P, 0:TE].rearrange("p (t e) -> p t e", e=E)))
                    a = tot
                    for n, s in enumerate(steps(T)):
                        b = pp[n % 2]
                        nc.vector.tensor_copy(b[:, 0:s, :], a[:, 0:s, :])
                        link(nc.vector.tensor_tensor(b[:, s:T, :], a[:, s:T, :], a[:, 0:T - s, :], ALU.add))
                        a = b
                    link(nc.vector.tensor_scalar(cf, a[:, T - 1, :], 127.0, None, ALU.add))
                    link(nc.vector.tensor_copy(ci, cf))
                    link(nc.vector.tensor_scalar(ci, ci, 7, 7, ALU.logical_shift_right, ALU.logical_shift_left))
                    link(nc.vector.tensor_copy(padded, ci))
                    q = padded
                    for n, s in enumerate(steps(E)):
                        b = ends[n % 2]
                        nc.vector.tensor_copy(b[:, 0:s], q[:, 0:s])
                        link(nc.vector.tensor_tensor(b[:, s:E], q[:, s:E], q[:, 0:E - s], ALU.add))
                        q = b
                    link(nc.vector.tensor_tensor(base, q, padded, ALU.subtract))
                    link(nc.vector.tensor_tensor(posf, a, tot, ALU.subtract))
                    link(nc.vector.tensor_tensor(posf, posf, psum[3][0:P, 0:TE].rearrange("p (t e) -> p t e", e=E), ALU.add))
                    link(nc.vector.tensor_tensor(posf, posf, over(base), ALU.add))
                    for k in range(2):
                        link(nc.vector.tensor_tensor(both if k else tot, sel[k], posf, ALU.mult))
                        link(nc.vector.tensor_reduce(zs, both if k else tot, AX.X, ALU.add))
                        link(nc.vector.tensor_copy(pos[:, k, :], zs))
                    POS["pos"] = link.count[0]
                    link(nc.vector.tensor_tensor(tcmp, over(q[0:1, :], NT, 1),
                                                 tile_start[:, 0:NT].unsqueeze(2).broadcast_to([1, NT, E]), ALU.is_le))
                    link(nc.vector.tensor_reduce(tcount, tcmp, AX.X, ALU.add))
                    link(nc.vector.tensor_scalar(tile_expert[:, 0:NT], tcount, float(E - 1), None, ALU.min))

                @block.scalar
                def _(act):
                    for t in range(T):
                        act.wait_ge(s_lt, t + 1)
                        if t >= 4:
                            act.wait_ge(s_lg, t - 3)
                        nc.scalar.copy(tT[:, t % 4, :, :], psum[t % 2][:, 0:DC * P].rearrange("p (c n) -> p c n", c=DC)).then_inc(s_lc, 1)
                    act.wait_ge(s_top, POS["shifted"])
                    n = 8 if softmax_first else 2
                    nc.scalar.activation(ex[:, :, 0:n], ex[:, :, 0:n], ACT.Exp).then_inc(s_ex, 1)

                @block.gpsimd
                def _(pool):
                    pool.wait_ge(s_top, POS["pos"])
                    for t in range(T):
                        for k in range(2):
                            nc.gpsimd.indirect_dma_start(
                                out=slots_in[:, :], out_offset=bass.IndirectOffsetOnAxis(ap=pos[:, k, t:t + 1], axis=0),
                                in_=tok[:, t, :], in_offset=None).then_inc(s_sc, 16)
                    pool.wait_ge(s_sc, 16 * 2 * T)

            G = 4
            xin = view(work, 0, [G, D])
            xT = view(work, G * D, [2, D])
            s_xi = [sem(f"s_xi{layer}_{w}") for w in range(G)]
            s_yo = sem(f"s_yo{layer}")
            s_xt = sem(f"s_xt{layer}"); s_xc = sem(f"s_xc{layer}"); s_h = sem(f"s_h{layer}"); s_hc = sem(f"s_hc{layer}")
            s_g = sem(f"s_g{layer}"); s_gc = sem(f"s_gc{layer}"); s_o2 = sem(f"s_o2{layer}"); s_oc = sem(f"s_oc{layer}")
            s_w2l = sem(f"s_w2l{layer}")
            hN, hTt, yo = moe_bufs
            s_nopp = sem(f"s_nopp{layer}"); s_nopq = sem(f"s_nopq{layer}")
            with nc.Block() as block:
                def groups(eng, body, experts=True):
                    with eng.Fori(0, NT // G) as i:
                        es = []
                        if experts:
                            es = [eng.value_load(tile_expert[0:1, ds(i * G + w, 1)], min_val=0, max_val=E - 1) for w in range(G)]
                        body(i, es)

                @block.sync
                def _(sp):
                    if layer == 1:
                        for e in range(E):
                            sp.dma_start(w2s[:, e * FC * D:(e + 1) * FC * D].rearrange("p (c d) -> p c d", c=FC),
                                         w2[e].rearrange("(c p) d -> p c d", p=128)).then_inc(s_w2l, 16)

                    def body(i, es):
                        for w in range(G):
                            sp.wait_ge(s_xt, i * G + w + 1)
                            sp.sem_inc(s_nopq, 1)
                            sp.dma_start(xin[:, w, :], slots_in[ds((i * G + w) * 128, 128), :]).then_inc(s_xi[w], 16)
                    groups(sp, body, False)
                    if layer == 1:
                        sp.wait_ge(s_w2l, 16 * E)

                @block.tensor
                def _(pe):
                    pe.sem_inc(s_xt, G)
                    if layer == 1:
                        pe.wait_ge(s_w2l, 16 * E)

                    def body(i, es):
                        for w in range(G):
                            pe.wait_ge(s_xi[w], (i + 1) * 16)
                            for c in range(DC):
                                at = (w % 2) * D + c * 128
                                last = nc.tensor.transpose(psum[4 + w // 2][:, at:at + 128], xin[:, w, c * 128:(c + 1) * 128], ident[:, :])
                            last.then_inc(s_xt, 1)
                        for w in range(G):
                            pe.wait_ge(s_xc, i * 2 + w // 2 + 1)
                            pe.wait_ge(s_gc, (i * G) * 1)
                            for c in range(DC):
                                last = nc.tensor.matmul(psum[w][:, 0:F], xT[:, w % 2, c * 128:(c + 1) * 128],
                                                        w1s[:, ds(es[w] * (DC * F) + c * F, F)], start=(c == 0), stop=(c == DC - 1))
                            last.then_inc(s_h, 1)
                        for w in range(G):
                            pe.wait_ge(s_hc, i * G + w + 1)
                            for c in range(FC):
                                last = nc.tensor.transpose(psum[w][:, c * 128:(c + 1) * 128], hN[:, w % 2, c * 128:(c + 1) * 128], ident[:, :])
                            last.then_inc(s_g, 1)
                        for w in range(G):
                            pe.wait_ge(s_gc, i * G + w + 1)
                            if w == 0:
                                pe.wait_ge(s_oc, i * 2)
                            for c in range(FC):
                                last = nc.tensor.matmul(psum[6 + w // 2][:, (w % 2) * D:(w % 2) * D + D],
                                                        hTt[:, w % 2, c * 128:(c + 1) * 128],
                                                        w2s[:, ds(es[w] * (FC * D) + c * D, D)], start=(c == 0), stop=(c == FC - 1))
                            last.then_inc(s_o2, 1)
                    groups(pe, body)

                @block.scalar
                def _(act):
                    def body(i, es):
                        for q in range(2):
                            act.wait_ge(s_xt, G + i * G + 2 * q + 2)
                            act.wait_ge(s_h, i * G + 2 * q)
                            nc.scalar.copy(xT[:, :, :], psum[4 + q][:, :].rearrange("p (w d) -> p w d", w=2)).then_inc(s_xc, 1)
                        for w in range(G):
                            act.wait_ge(s_g, i * G + w + 1)
                            act.wait_ge(s_o2, i * G + w - 1 if w >= 2 else i * G)
                            for c in range(FC):
                                last = nc.scalar.activation(hTt[:, w % 2, c * 128:(c + 1) * 128], psum[w][:, c * 128:(c + 1) * 128], act_fn,
                                                            bias=vecs[:, ds(es[w] * FC + (eb + c), 1)])
                            last.then_inc(s_gc, 1)
                    groups(act, body)

                @block.vector
                def _(dve):
                    def body(i, es):
                        for w in range(G):
                            dve.wait_ge(s_h, i * G + w + 1)
                            if w >= 2:
                                dve.wait_ge(s_g, i * G + w - 1)
                            else:
                                dve.wait_ge(s_g, i * G)
                            nc.vector.tensor_copy(hN[:, w % 2, 0:F], psum[w][:, 0:F]).then_inc(s_hc, 1)
                        for q in range(2):
                            dve.wait_ge(s_o2, i * G + 2 * q + 2)
                            dve.wait_ge(s_yo, (i * 2 + q) * 16)
                            nc.vector.tensor_copy(yo[:, :, :], psum[6 + q][:, :].rearrange("p (w d) -> p w d", w=2)).then_inc(s_oc, 1)
                    groups(dve, body, False)

                @block.gpsimd
                def _(pool):
                    def body(i, es):
                        for q in range(2):
                            pool.wait_ge(s_oc, i * 2 + q + 1)
                            pool.sem_inc(s_nopp, 1)
                            pool.dma_start(slots_out[ds((i * 2 + q) * 256, 256), :].rearrange("(w p) d -> p w d", w=2),
                                           yo[:, :, :]).then_inc(s_yo, 16)
                    groups(pool, body, False)
                    pool.wait_ge(s_yo, NT // 2 * 16)

            NQ = 10
            ygath = view(arena, 0, [NQ, D], P)
            b2e = view(work, 0, [D], E)
            combT = view(work, D, [4, P], 16)
            s_b2 = sem(f"s_b2{layer}"); s_yg = [sem(f"s_yg{layer}_{n}") for n in range(NQ)]
            s_ct = sem(f"s_ct{layer}"); s_cc = sem(f"s_cc{layer}"); s_bb = sem(f"s_bb{layer}"); s_c = sem(f"s_c{layer}")
            s_fin = sem(f"s_fin{layer}")
            with nc.Block() as block:
                @block.sync
                def _(sp):
                    sp.dma_start(b2e, b2).then_inc(s_b2, 16)
                    sp.wait_ge(s_b2, 16)

                @block.gpsimd
                def _(pool):
                    for t in range(T):
                        for k in range(2):
                            n = 2 * t + k
                            if n >= NQ:
                                pool.wait_ge(s_c, (t - NQ // 2) * 3 + k + 1)
                            nc.gpsimd.indirect_dma_start(
                                out=ygath[:, n % NQ, :], out_offset=None, in_=slots_out[0:NT * 128, :],
                                in_offset=bass.IndirectOffsetOnAxis(ap=pos[:, k, t:t + 1], axis=0)).then_inc(s_yg[n % NQ], 16)

                @block.tensor
                def _(pe):
                    pe.wait_ge(s_b2, 16)
                    for t in range(T):
                        if t >= 2:
                            pe.wait_ge(s_cc, t - 1)
                        nc.tensor.transpose(psum[t % 2][0:E, 0:P], comb[:, t, :], ident[0:P, 0:P]).then_inc(s_ct, 1)
                        pe.wait_ge(s_cc, t + 1)
                        if t >= 2:
                            pe.wait_ge(s_c, (t - 2) * 3 + 3)
                        nc.tensor.matmul(psum[2 + t % 2][0:P, 0:D], combT[0:E, t % 4, :], b2e, start=True, stop=True).then_inc(s_bb, 1)

                @block.scalar
                def _(act):
                    for t in range(T):
                        act.wait_ge(s_ct, t + 1)
                        if t >= 4:
                            act.wait_ge(s_bb, t - 3)
                        nc.scalar.copy(combT[0:E, t % 4, :], psum[t % 2][0:E, 0:P]).then_inc(s_cc, 1)

                @block.vector
                def _(dve):
                    for t in range(T):
                        prev = tok[:, t, :]
                        for k in range(2):
                            n = 2 * t + k
                            dve.wait_ge(s_yg[n % NQ], 16 * (n // NQ + 1))
                            if k:
                                dve.wait_ge(s_c, 3 * t + 1)
                            nc.vector.scalar_tensor_tensor(tok[:, t, :], ygath[:, n % NQ, :], wts[:, t, k:k + 1], prev,
                                                           ALU.mult, ALU.add).then_inc(s_c, 1)
                        dve.wait_ge(s_bb, t + 1)
                        dve.wait_ge(s_c, 3 * t + 2)
                        nc.vector.tensor_tensor(tok[:, t, :], psum[2 + t % 2][0:P, 0:D], tok[:, t, :], ALU.add).then_inc(s_c, 1)
                        if layer == 0:
                            dve.wait_ge(s_c, 3 * t + 3)
                            nc.vector.tensor_tensor(xres[:, t, :], tok[:, t, :], xres[:, t, :], ALU.add).then_inc(s_fin, 1)

        def second_layer_start():
            s_v = sem("s_v"); s_vt = sem("s_vt"); s_vd = sem("s_vd")
            with nc.Block() as block:
                @block.sync
                def _(sp):
                    sp.dma_start(wraw, L1_gnn_W.rearrange("(o p) i -> p o i", p=128)).then_inc(s_v, 16)
                    sp.dma_start(gb_bc, L1_gnn_b.partition_broadcast(128)).then_inc(s_v, 16)
                    sp.wait_ge(s_v, 32)

                @block.tensor
                def _(pe):
                    pe.wait_ge(s_v, 32)
                    for i in range(2 * DC):
                        for o in range(DC):
                            at = (i % 2) * D + o * 128
                            last = nc.tensor.transpose(psum[2 + i // 2][:, at:at + 128], wraw[:, o, i * 128:(i + 1) * 128], ident[:, :])
                    last.then_inc(s_vt, 1)

                @block.vector
                def _(dve):
                    nc.vector.tensor_scalar(rdegree[:, :], degree[:, :], 1.0, None, ALU.max).then_inc(s_vd, 1)
                    dve.wait_ge(s_vd, 1)
                    nc.vector.reciprocal(rdegree[:, :], rdegree[:, :]).then_inc(s_vd, 1)
                    dve.wait_ge(s_vt, 1)
                    for b in range(DC):
                        nc.vector.tensor_copy(wT[:, 2 * b:2 * b + 2, :], psum[2 + b][:, :].rearrange("p (i o) -> p i o", i=2))

        def finish():
            fgam_bc = view(work, 0, [D]); fbet_bc = view(work, D, [D])
            s_g1 = sem("s_gain"); s_fo = sem("s_fo"); s_out = sem("s_out")
            with nc.Block() as block:
                @block.sync
                def _(sp):
                    sp.dma_start(fgam_bc, L1_ffn_gamma.partition_broadcast(128)).then_inc(s_g1, 16)
                    sp.dma_start(fbet_bc, L1_ffn_beta.partition_broadcast(128)).then_inc(s_g1, 16)
                    out_v = out.rearrange("(t p) d -> p t d", p=P)
                    for b in range(T // U):
                        sp.wait_ge(s_fo, (b + 1) * U * 3)
                        sp.dma_start(out_v[:, b * U:(b + 1) * U, :], xres[:, b * U:(b + 1) * U, :]).then_inc(s_out, 16)
                    sp.wait_ge(s_out, 16 * (T // U))

                @block.vector
                def _(dve):
                    dve.wait_ge(s_g1, 32)
                    for b in range(T // U):
                        for step in range(3):
                            for w in range(U):
                                t = b * U + w
                                if step:
                                    dve.wait_ge(s_fo, (3 * b + step - 1) * U + w + 1)
                                if step == 0:
                                    i = nc.vector.tensor_tensor(tok[:, t, :], tok[:, t, :], fgam_bc[0:P, :], ALU.mult)
                                elif step == 1:
                                    i = nc.vector.tensor_tensor(tok[:, t, :], tok[:, t, :], fbet_bc[0:P, :], ALU.add)
                                else:
                                    i = nc.vector.tensor_tensor(xres[:, t, :], tok[:, t, :], xres[:, t, :], ALU.add)
                                i.then_inc(s_fo, 1)

        moe_keep = [(sb(f"wts{l}", [P, T, 2]), sb(f"pos{l}", [P, 2, T], i32), None, sb(f"tile_expert{l}", [1, 64], i32)) for l in range(1)]
        comb_all = sb("comb_all", [P, T * 16])
        keep = moe_keep[0]
        moe_keep = [(keep[0], keep[1], comb_all[:, 0:T * E].rearrange("p (t e) -> p t e", e=E), keep[3]) for E in (E0, E1)]
        moe_bufs = (view(work, 1536, [2, 512]), view(work, 3072, [2, 512]), view(work, 2560, [2, D]))
        end_stage()
        layer_norm("a", xres, tok, xn_dram)
        end_stage()
        graph(0)
        end_stage()
        first_layer_end()
        end_stage()
        layer_norm("b", xres, tok, None)
        end_stage()
        moe(0, E0, F0, L0_ffn_w1, L0_ffn_w2, L0_ffn_b2, ACT.Gelu, True)
        end_stage()
        layer_norm("c", xres, tok, xn_dram)
        end_stage()
        second_layer_start()
        end_stage()
        graph(1)
        end_stage()
        layer_norm("d", x3, tok, None, keep=xres)
        end_stage()
        moe(1, E1, F1, L1_ffn_w1, L1_ffn_w2, L1_ffn_b2, ACT.Relu, False)
        end_stage()
        layer_norm("e", tok, tok, None)
        end_stage()
        finish()


_INS = ['x', 'src', 'dst', 'edge_weight', 'L0_gnn_W1', 'L0_gnn_b1', 'L0_gnn_gamma', 'L0_gnn_beta', 'L0_gnn_W2', 'L0_gnn_b2',
        'L0_ffn_router_w', 'L0_ffn_w1', 'L0_ffn_b1', 'L0_ffn_w2', 'L0_ffn_b2', 'L1_gnn_W', 'L1_gnn_b', 'L1_ffn_gate_w',
        'L1_ffn_gate_b', 'L1_ffn_w1', 'L1_ffn_b1', 'L1_ffn_w2', 'L1_ffn_b2', 'L1_ffn_gamma', 'L1_ffn_beta']


def kernel(**inputs):
    import numpy as _np
    import concourse.bacc as _bacc
    from concourse import mybir as _mybir
    from concourse.bass_utils import run_bass_kernel_spmd as _run

    nc = _bacc.Bacc("TRN2", target_bir_lowering=False, num_devices=1)
    arrays, args = {}, []
    for name in _INS:
        a = _np.ascontiguousarray(inputs[name])
        arrays[f"in_{name}_dram"] = a
        args.append(nc.dram_tensor(f"in_{name}_dram", a.shape, _mybir.dt.from_np(a.dtype), kind="ExternalInput").ap())
    args.append(nc.dram_tensor("out_0_dram", (N, D), _mybir.dt.float32, kind="ExternalOutput").ap())
    gnn_moe(nc, *args)
    r = _run(nc, [arrays], core_ids=[0])
    return r.results[0]["out_0_dram"]
```

```python
import concourse.bass as bass
from concourse import mybir
from contextlib import ExitStack

fp32 = mybir.dt.float32
fp16 = mybir.dt.float16
i32 = mybir.dt.int32
u32 = mybir.dt.uint32
ALU = mybir.AluOpType
ACT = mybir.ActivationFunctionType
AX = mybir.AxisListType
ds = bass.ds

N = 3125
D = 256
NE = 53125
P = 125
T = N // P
DC = D // 128
HID = 1024
HC = HID // 128
KS = 18
WIN = KS * 128
GROUP = 6
GROUPS = KS // GROUP
ROUNDS = -(-NE // WIN)
NE_PAD = 25 * WIN
NE_LEN = NE_PAD + ROUNDS * WIN
NO_NODE = 1 << 20
REGION = -(-N // 128) * 128 + 128
U = 5
LN_EPS = 1e-5
SUB = 25
SUBS = P // SUB
SUB_TILES = 4
DENSE = (1, 3)
HALF = (0, 13, T)
BUILD = (3, 6, 7)


def moe_tiles(experts):
    return (2 * N - experts) // 128 + experts


def gnn_moe(nc, x, src, dst, edge_weight, L0_gnn_W1, L0_gnn_b1, L0_gnn_gamma, L0_gnn_beta, L0_gnn_W2,
            L0_gnn_b2, L0_ffn_router_w, L0_ffn_w1, L0_ffn_b1, L0_ffn_w2, L0_ffn_b2, L1_gnn_W, L1_gnn_b,
            L1_ffn_gate_w, L1_ffn_gate_b, L1_ffn_w1, L1_ffn_b1, L1_ffn_w2, L1_ffn_b2, L1_ffn_gamma,
            L1_ffn_beta, out):
    E0, E1 = L0_ffn_w1.shape[0], L1_ffn_w1.shape[0]
    F0, F1 = L0_ffn_w1.shape[2], L1_ffn_w1.shape[2]
    SLOTS = 128 * max(moe_tiles(E0), moe_tiles(E1))

    ctx = ExitStack()
    with ctx:
        def sb(name, shape, dt=fp32):
            return ctx.enter_context(nc.sbuf_tensor(name, shape, dt))

        stage_sems = []
        stage = [0]

        def sem(name):
            s = nc.alloc_semaphore(f"{name}_{stage[0]}")
            stage_sems.append(s)
            return s

        def end_stage():
            nc.clear_and_free_semaphores(list(stage_sems))
            stage_sems.clear()
            stage[0] += 1
            nc.all_engine_barrier()

        def dram(name, shape, dt=fp32):
            return nc.dram_tensor(name, shape, dt, kind="Internal").ap()

        src_pad = dram("src_pad", [NE_LEN], i32)
        dst_pad = dram("dst_pad", [NE_LEN], i32)
        ew_pad = dram("ew_pad", [NE_LEN])
        xn16_dram = dram("xn16_dram", [N, 2 * D], fp16)
        xn_dram = dram("xn_dram", [N, D])
        slots_in = dram("slots_in", [max(E0, E1) * REGION, D])
        slots_out = dram("slots_out", [SLOTS, D])

        xres = sb("xres", [P, T, D])
        tok = sb("tok", [P, T, D])
        arena = sb("arena", [128, 32768])
        work = sb("work", [128, 4096])

        def view(t, at, dims, parts=128, half=False):
            size = 1
            for d in dims:
                size *= d
            flat = t[0:parts, at:at + size // 2].bitcast(fp16) if half else t[0:parts, at:at + size]
            names = "abcd"[:len(dims)]
            if len(dims) == 1:
                return flat
            return flat.rearrange(f"p ({' '.join(names)}) -> p {' '.join(names)}",
                                  **{n: d for n, d in zip(names, dims)})

        h1T = view(arena, 0, [HC, N])
        ROWS = HC * N
        rows = view(arena, ROWS, [KS, D + 1])
        masks = view(arena, ROWS + KS * (D + 1), [KS, P])
        rows16 = view(arena, ROWS, [KS, 2 * D + 2], half=True)
        masks16 = view(arena, ROWS + KS * (D + 1), [9, P + 1], half=True)[:, :, 0:P]
        MATRIX = ROWS + KS * (D + 1) + 9 * (P + 1) // 2
        adjacency = view(arena, MATRIX, [T, P + 1], P, half=True)[:, :, 0:P]
        col_hot = view(arena, MATRIX + T * (P + 1) // 2, [3, T * SUB + 1], half=True)[:, :, 0:T * SUB]
        x16 = xres[:, :, :].bitcast(fp16)
        x3 = view(arena, 16384, [T, D], P)
        w1g = view(work, 0, [DC, HID])
        bn6 = view(work, 2048, [HC, T, 6])
        hT = view(work, 3248, [2 * DC, P])
        w2g = view(arena, ROWS, [HC, D])
        b2g_bc = view(arena, ROWS + HC * D, [D])
        gb_bc = view(work, 2304, [D])
        wT = view(arena, 16384 + T * D, [2 * DC, D])
        wraw = view(arena, ROWS, [DC, 2 * D])

        ident = sb("ident", [128, 128])
        ones = sb("ones", [128, 128])
        before = sb("before", [P, P])
        node_row = sb("node_row", [128, P])
        node_base = sb("node_base", [128, T])
        expert_row = sb("expert_row", [128, 16])
        region_row = sb("region_row", [128, 16])
        zero_rows = sb("zero_rows", [128, D])
        row_hot = view(zero_rows, 0, [4, P + 1], half=True)[:, :, 0:P]
        comb_all = sb("comb_all", [128, T * 16])
        col_row = view(comb_all, 0, [T * SUB + 1], half=True)[:, 0:T * SUB]
        sub_base = sb("sub_base", [128, SUBS])
        dense_meta = sb("dense_meta", [128, len(DENSE), 2, SUBS, SUB_TILES], i32)
        dense_starts = sb("dense_starts", [1, (T // U) * len(DENSE) * SUBS], i32)
        fgam_bc = zero_rows
        tile_start = sb("tile_start", [1, 64])
        eps = sb("eps", [128, 1])
        pad_i = view(arena, 5120, [179], 25).bitcast(i32)
        pad_z = view(arena, 5376, [179], 25)
        shared = sb("shared", [128, 4 * D])
        meta_src = view(shared, 0, [U, KS]).bitcast(i32)
        meta_dst = view(shared, U * KS, [U, KS]).bitcast(i32)
        meta_ew = view(shared, 2 * U * KS, [U, KS])
        dst_local = view(shared, 3 * U * KS, [U, KS])
        summed = view(shared, 4 * U * KS, [2, D + 1], P)
        CALC = 4 * U * KS + 2 * (D + 1)
        LIST = SUBS * SUB_TILES
        meta_f = view(shared, CALC, [2, SUBS, SUB_TILES])
        beyond = meta_f[:, 1, :, :]
        block_of = view(shared, CALC + 2 * LIST, [SUBS, SUB_TILES])
        row_of, col_of = ([view(shared, CALC + (i + k) * LIST, [SUBS, SUB_TILES]) for k in range(2)] for i in (3, 5))
        y_out = view(shared, 0, [2, 2, D])
        fbet_bc = view(shared, 0, [D])
        NL = (T // U) * len(DENSE) * SUBS
        table = view(arena, 7424, [T + 2 + NL], 1)
        gaps = view(arena, 7552, [T + NL], 1)
        scal = sb("scal", [1, 4])
        starts = sb("starts", [1, T + 2], i32)
        rounds = sb("rounds", [1, 3], i32)
        degree = sb("degree", [P, T])
        rdegree = sb("rdegree", [P, T])
        mean_v = sb("mean_v", [P, T])
        mv = sb("mv", [P, T, 2])
        st6 = sb("st6", [P, T, 6])
        rstd = sb("rstd", [P, T])
        bnmv = sb("bnmv", [128, HC, 2])
        bn_scale = sb("bn_scale", [128, HC])
        bn_shift = sb("bn_shift", [128, HC])
        VROWS = 3 * HC + E0 * F0 // 128 + E1 * F1 // 128
        vec_rows = view(arena, 4352, [128], VROWS)
        vecs = sb("vecs", [128, VROWS])
        b1g, gam, bet = (vecs[:, i * HC:(i + 1) * HC] for i in range(3))
        EB0, EB1 = 3 * HC, 3 * HC + E0 * F0 // 128
        gateb_bc = sb("gateb_bc", [128, E1])
        router = view(arena, 4608, [D], E0)
        gateT = [sb("gateT0", [128, DC, E0]), sb("gateT1", [128, DC, E1])]
        g_col = sb("g_col", [128, DC])
        i_first = sb("i_first", [1, 1], i32)

        psum = [ctx.enter_context(nc.psum_tensor(f"bank{i}", [128, 512], fp32)) for i in range(8)]

        s_x = sem("s_x"); s_w = sem("s_w"); s_const = sem("s_const"); s_pad = sem("s_pad")
        s_dst = sem("s_dst"); s_tr = sem("s_tr"); s_dve = sem("s_dve"); s_cnt = sem("s_cnt")
        s_wg = sem("s_wg"); s_next = sem("s_next"); s_dstb = sem("s_dstb")
        s_st = sem("s_st"); s_var = sem("s_var"); s_sq = sem("s_sq"); s_n = sem("s_n"); s_xn = sem("s_xn")
        s_hi = sem("s_hi"); s_rs = sem("s_rs"); s_lo = sem("s_lo")

        def chain(eng, s):
            n = [0]

            def link(ins):
                n[0] += 1
                ins.then_inc(s, 1)
                eng.wait_ge(s, n[0])
            link.count = n
            return link

        dst_a = view(arena, 2048, [NE // P], P).bitcast(i32)
        dst_b = view(arena, 2560, [NE // P], P).bitcast(i32)
        dst_f = view(arena, 3072, [NE // P], P)
        lt = view(arena, 6144, [2, NE // P], P)
        cols = view(arena, 4096, [T + 2 + NL], P)
        dst_16 = view(arena, 7680, [NE // P + 1], P, half=True)[:, 0:NE // P]
        lt16 = view(arena, 7936, [2, NE // P + 1], P, half=True)[:, :, 0:NE // P]

        with nc.Block() as block:
            @block.sync
            def _(sp):
                sp.dma_start(dst_a, dst.rearrange("(p c) -> p c", p=P)).then_inc(s_dst, 16)
                sp.wait_ge(s_next, 1)
                sp.dma_start(dst_b[0:P - 1, :], dst[1:1 + (P - 1) * (NE // P)].rearrange("(p c) -> p c", p=P - 1)).then_inc(s_dstb, 16)
                sp.dma_start(dst_b[P - 1:P, 0:NE // P - 1], dst[1 + (P - 1) * (NE // P):NE].rearrange("(p c) -> p c", p=1)).then_inc(s_dstb, 16)
                sp.dma_start(xres[:, :, :], x.rearrange("(t p) d -> p t d", p=P)).then_inc(s_x, 16)
                sp.dma_start(dst_pad[0:NE].rearrange("(p c) -> p c", p=P), dst.rearrange("(p c) -> p c", p=P)).then_inc(s_pad, 16)
                sp.dma_start(src_pad[0:NE].rearrange("(p c) -> p c", p=P), src.rearrange("(p c) -> p c", p=P)).then_inc(s_pad, 16)
                sp.dma_start(ew_pad[0:NE].rearrange("(p c) -> p c", p=P), edge_weight.rearrange("(p c) -> p c", p=P)).then_inc(s_pad, 16)
                sp.wait_ge(s_const, 2)
                tail = lambda a: a[NE:NE_PAD].rearrange("(p c) -> p c", p=25)
                sp.dma_start(tail(dst_pad), pad_i[:, :]).then_inc(s_pad, 16)
                sp.dma_start(tail(src_pad), pad_z[:, :].bitcast(i32)).then_inc(s_pad, 16)
                sp.dma_start(tail(ew_pad), pad_z[:, :]).then_inc(s_pad, 16)
                xn_rows = xn16_dram.rearrange("(t p) d -> p t d", p=P)
                for b in range(T // U):
                    sp.wait_ge(s_lo, (b + 1) * U)
                    sp.dma_start(xn_rows[:, b * U:(b + 1) * U, :], x16[:, b * U:(b + 1) * U, :]).then_inc(s_xn, 16)
                sp.wait_ge(s_pad, 16 * 6)
                sp.wait_ge(s_xn, 16 * (T // U))

            @block.scalar
            def _(act):
                act.dma_start(vec_rows[0:HC, :], L0_gnn_b1.rearrange("(m p) -> m p", p=128)).then_inc(s_w, 16)
                act.dma_start(vec_rows[HC:2 * HC, :], L0_gnn_gamma.rearrange("(m p) -> m p", p=128)).then_inc(s_w, 16)
                act.dma_start(vec_rows[2 * HC:3 * HC, :], L0_gnn_beta.rearrange("(m p) -> m p", p=128)).then_inc(s_w, 16)
                act.dma_start(vec_rows[EB0:EB1, :], L0_ffn_b1.rearrange("e (c p) -> (e c) p", p=128)).then_inc(s_w, 16)
                act.dma_start(vec_rows[EB1:VROWS, :], L1_ffn_b1.rearrange("e (c p) -> (e c) p", p=128)).then_inc(s_w, 16)
                act.dma_start(router[:, :], L0_ffn_router_w).then_inc(s_w, 16)
                act.dma_start(w1g, L0_gnn_W1.rearrange("(c p) h -> p c h", p=128)).then_inc(s_wg, 16)
                act.dma_start(gateT[1][:, :, :], L1_ffn_gate_w.rearrange("(c p) e -> p c e", p=128)).then_inc(s_wg, 16)
                act.dma_start(gateb_bc[:, :], L1_ffn_gate_b.partition_broadcast(128)).then_inc(s_wg, 16)
                act.dma_start(i_first[:, :], src[0:1].rearrange("(a n) -> a n", a=1)).then_inc(s_wg, 16)
                act.wait_ge(s_var, T)
                nc.scalar.activation(mean_v[:, :], mv[:, :, 1], ACT.Sqrt, bias=eps[0:P, :]).then_inc(s_sq, 1)
                for t in range(T):
                    act.wait_ge(s_n, t + 1)
                    nc.scalar.copy(x16[:, t, 0:D], tok[:, t, :]).then_inc(s_hi, 1)
                act.wait_ge(s_wg, 16 * 4)

            @block.gpsimd
            def _(pool):
                pool.memset(dst_b, NO_NODE).then_inc(s_next, 1)
                pool.memset(pad_i[:, :], NO_NODE).then_inc(s_const, 1)
                pool.memset(pad_z[:, :], 0.0).then_inc(s_const, 1)
                pool.memset(ident[:, :], 0.0).then_inc(s_const, 1)
                pool.memset(ones[:, :], 1.0).then_inc(s_const, 1)
                pool.memset(before[:, :], 1.0).then_inc(s_const, 1)
                pool.memset(eps[:, :], LN_EPS).then_inc(s_const, 1)
                pool.iota(node_row[:, :], [[1, P]], base=0, channel_multiplier=0,
                          allow_small_or_imprecise_dtypes=True).then_inc(s_const, 1)
                pool.iota(node_base[:, :], [[P, T]], base=0, channel_multiplier=0,
                          allow_small_or_imprecise_dtypes=True).then_inc(s_const, 1)
                pool.iota(expert_row[:, :], [[1, 16]], base=0, channel_multiplier=0,
                          allow_small_or_imprecise_dtypes=True).then_inc(s_const, 1)
                pool.iota(region_row[:, :], [[REGION, 16]], base=0, channel_multiplier=0,
                          allow_small_or_imprecise_dtypes=True).then_inc(s_const, 1)
                pool.iota(tile_start[:, :], [[128, 64]], base=0, channel_multiplier=0,
                          allow_small_or_imprecise_dtypes=True).then_inc(s_const, 1)
                pool.memset(degree[:, :], 0.0).then_inc(s_const, 1)
                pool.iota(col_row, [[1, T * SUB]], base=0, channel_multiplier=0,
                          allow_small_or_imprecise_dtypes=True).then_inc(s_const, 1)
                pool.iota(sub_base[:, :], [[SUB, SUBS]], base=0, channel_multiplier=0,
                          allow_small_or_imprecise_dtypes=True).then_inc(s_const, 1)
                pool.wait_ge(s_const, 14)
                pool.affine_select(out=ident[:, :], in_=ident[:, :], compare_op=ALU.not_equal, fill=1.0,
                                   base=0, pattern=[[-1, 128]], channel_multiplier=1).then_inc(s_const, 1)
                pool.affine_select(out=before[:, :], in_=before[:, :], compare_op=ALU.is_gt, fill=0.0,
                                   base=0, pattern=[[1, P]], channel_multiplier=-1).then_inc(s_const, 1)
                for t in range(T):
                    pool.wait_ge(s_hi, t + 1)
                    pool.tensor_tensor(x16[:, t, D:2 * D], tok[:, t, :], x16[:, t, 0:D], ALU.subtract).then_inc(s_lo, 1)

            @block.tensor
            def _(pe):
                pe.wait_ge(s_const, 16)
                pe.wait_ge(s_w, 16 * 6)
                nc.tensor.transpose(psum[0][:, 0:VROWS], vec_rows[:, :], ident[0:VROWS, 0:VROWS])
                for c in range(DC):
                    last = nc.tensor.transpose(psum[1][:, c * E0:(c + 1) * E0], router[:, c * 128:(c + 1) * 128], ident[0:E0, 0:E0])
                last.then_inc(s_tr, 1)
                pe.wait_ge(s_cnt, 1)
                nc.tensor.matmul(psum[4][0:1, 0:T + 2 + NL], ones[0:P, 0:1], cols, start=True, stop=True).then_inc(s_tr, 1)

            @block.vector
            def _(dve):
                link = chain(dve, s_dve)
                dve.wait_ge(s_const, 16)
                link(nc.vector.memset(cols, 0.0))
                dve.wait_ge(s_dst, 16)
                link(nc.vector.tensor_copy(dst_f, dst_a))
                link(nc.vector.tensor_scalar(dst_16, dst_f, float(N // 2), None, ALU.subtract))
                firsts = {t: t * P for t in range(1, T)}
                for i in range(NL):
                    b, w, k = i // (len(DENSE) * SUBS), DENSE[i // SUBS % len(DENSE)], i % SUBS
                    firsts[T + 2 + i] = (b * U + w) * P + k * SUB
                for n, (column, node) in enumerate(firsts.items()):
                    dve.wait_ge(s_dve, max(link.count[0] - 1, 3))
                    nc.vector.tensor_scalar(lt16[:, n % 2, :], dst_16, float(node - N // 2), 0.0, ALU.is_lt, ALU.add,
                                            accum_out=cols[:, column:column + 1]).then_inc(s_dve, 1)
                    link.count[0] += 1
                dve.wait_ge(s_dstb, 32)
                dve.wait_ge(s_dve, link.count[0])
                link(nc.vector.tensor_copy(lt[:, 0, :], dst_b))
                link(nc.vector.tensor_tensor(lt[:, 1, :], lt[:, 0, :], dst_f, ALU.is_lt))
                nc.vector.tensor_reduce(cols[:, T + 1:T + 2], lt[:, 1, :], AX.X, ALU.add).then_inc(s_cnt, 1)
                dve.wait_ge(s_x, 16)
                for t in range(T):
                    nc.vector.bn_stats(st6[:, t, :], xres[:, t, :]).then_inc(s_st, 1)
                for t in range(T):
                    dve.wait_ge(s_st, t + 1)
                    nc.vector.bn_aggr(mv[:, t, :], st6[:, t, :]).then_inc(s_var, 1)
                dve.wait_ge(s_sq, 1)
                nc.vector.reciprocal(rstd[:, :], mean_v[:, :]).then_inc(s_rs, 1)
                dve.wait_ge(s_rs, 1)
                for t in range(T):
                    nc.vector.tensor_scalar(tok[:, t, :], xres[:, t, :], mv[:, t, 0:1], rstd[:, t:t + 1],
                                            ALU.subtract, ALU.mult).then_inc(s_n, 1)
                dve.wait_ge(s_tr, 2)
                nc.vector.tensor_copy(vecs[:, :], psum[0][:, 0:VROWS])
                nc.vector.tensor_copy(gateT[0][:, :, :], psum[1][:, 0:DC * E0].rearrange("p (c e) -> p c e", c=DC))
                link(nc.vector.tensor_copy(table, psum[4][0:1, 0:T + 2 + NL]))
                lists = table[:, T + 2:T + 2 + NL].rearrange("p (b w k) -> p b w k", b=T // U, k=SUBS)
                list_gaps = gaps[:, T:T + NL].rearrange("p (b w k) -> p b w k", b=T // U, k=SUBS)
                link(nc.vector.memset(table[:, T:T + 1], float(NE)))
                link(nc.vector.tensor_tensor(gaps[:, 0:T], table[:, 1:T + 1], table[:, 0:T], ALU.subtract))
                for w in range(len(DENSE)):
                    link(nc.vector.tensor_tensor(list_gaps[:, :, w, 0:SUBS - 1], lists[:, :, w, 1:SUBS], lists[:, :, w, 0:SUBS - 1], ALU.subtract))
                    nexts = table[:, 1:T + 1].rearrange("p (b w) -> p b w", w=U)[:, :, DENSE[w]]
                    link(nc.vector.tensor_tensor(list_gaps[:, :, w, SUBS - 1], nexts, lists[:, :, w, SUBS - 1], ALU.subtract))
                link(nc.vector.tensor_reduce(scal[:, 0:1], gaps[:, 0:T], AX.X, ALU.max))
                link(nc.vector.tensor_scalar(scal[:, 0:1], scal[:, 0:1], float(WIN), None, ALU.is_gt))
                link(nc.vector.tensor_scalar(scal[:, 1:2], table[:, T + 1:T + 2], 0.0, None, ALU.is_gt))
                link(nc.vector.tensor_reduce(scal[:, 2:3], gaps[:, T:T + NL], AX.X, ALU.max))
                link(nc.vector.tensor_scalar(scal[:, 2:3], scal[:, 2:3], float(SUB_TILES * 128), None, ALU.is_gt))
                link(nc.vector.tensor_tensor(scal[:, 0:1], scal[:, 0:1], scal[:, 1:2], ALU.max))
                link(nc.vector.tensor_tensor(scal[:, 2:3], scal[:, 0:1], scal[:, 2:3], ALU.max))
                link(nc.vector.tensor_scalar(rounds[:, 0:1], scal[:, 2:3], float(ROUNDS - 1), 1.0, ALU.mult, ALU.add))
                link(nc.vector.tensor_scalar(scal[:, 3:4], scal[:, 2:3], -1.0, 1.0, ALU.mult, ALU.add))
                link(nc.vector.tensor_copy(rounds[:, 1:2], scal[:, 3:4]))
                link(nc.vector.tensor_scalar(rounds[:, 2:3], scal[:, 2:3], float(ROUNDS), None, ALU.mult))
                link(nc.vector.tensor_scalar(starts[:, :], table[:, 0:T + 2], scal[:, 3:4], None, ALU.mult))
                link(nc.vector.tensor_copy(dense_starts[:, :], table[:, T + 2:T + 2 + NL]))

        def first_graph(dense):
            kinds = "GDGDG" if dense else "GGGGG"
            G_SLOT = [kinds[:w].count("G") for w in range(U)]
            D_SLOT = [kinds[:w].count("D") for w in range(U)]
            NG, ND = kinds.count("G"), kinds.count("D")
            GROUP = 3
            KG = KS // GROUP
            RING = 3
            s_meta = [sem(f"s_meta{w}") for w in range(U)]
            s_row = [sem(f"s_row{j}") for j in range(KS)]
            s_local = sem("s_local"); s_mask = sem("s_mask"); s_used = sem("s_used"); s_sum = sem("s_sum")
            s_kept = sem("s_kept"); s_t = sem("s_t"); s_ht = sem("s_ht"); s_proj = sem("s_proj"); s_post = sem("s_post")
            s_one = sem("s_one"); s_went = sem("s_went"); s_went_sp = sem("s_went_sp")
            s_calc = sem("s_calc"); s_taken = sem("s_taken"); s_hot = sem("s_hot"); s_tile = sem("s_tile")
            s_evac = sem("s_evac"); s_dense = sem("s_dense")
            FREE = NG * KG
            TILES = 4
            HALVES = 3
            with nc.Block() as block:
                def windows(eng, body):
                    n = eng.value_load(rounds[0:1, 1:2] if dense else rounds[0:1, 2:3], min_val=0, max_val=1 if dense else ROUNDS)
                    with eng.If(n > 0):
                        with eng.Fori(0, n) as r:
                            with eng.Fori(0, T // U) as b:
                                body(r, b, r * (T // U) + b)

                @block.sync
                def _(sp):
                    def body(r, b, rb):
                        for w in range(U):
                            t = b * U + w
                            if kinds[w] == "G":
                                sp.wait_ge(s_used, (rb * NG + G_SLOT[w] + 1) * KG)
                                sp.sem_inc(s_went_sp, 1)
                                at = sp.value_load(starts[0:1, ds(t, 1)], min_val=0, max_val=NE)
                                if not dense:
                                    at = sp.snap(at + r * WIN)
                                for to, frm in ((meta_src, src_pad), (meta_dst, dst_pad)):
                                    sp.dma_start(to[:, w, :], frm[ds(at, WIN)].rearrange("(p j) -> p j", j=KS)).then_inc(s_meta[w], 16)
                            else:
                                sp.wait_ge(s_taken, rb * ND + D_SLOT[w] + 1)
                                sp.sem_inc(s_went_sp, 1)
                                for s in range(SUBS):
                                    at = sp.value_load(dense_starts[0:1, ds((b * ND + D_SLOT[w]) * SUBS + s, 1)], min_val=0, max_val=NE)
                                    for i, frm in enumerate((src_pad, dst_pad)):
                                        sp.dma_start(dense_meta[:, D_SLOT[w], i, s, :],
                                                     frm[ds(at, SUB_TILES * 128)].rearrange("(p j) -> p j", j=SUB_TILES)).then_inc(s_meta[w], 16)
                    windows(sp, body)

                @block.gpsimd
                def _(pool):
                    nc.gpsimd.memset(rows16[:, :, 2 * D:2 * D + 1], 1.0).then_inc(s_one, 1)

                    def body(r, b, rb):
                        for w in range(U):
                            if kinds[w] == "G":
                                x = rb * NG + G_SLOT[w]
                                pool.wait_ge(s_meta[w], (rb + 1) * 32)
                                pool.sem_inc(s_went, 1)
                                for j in range(KS):
                                    if j % GROUP == 0:
                                        pool.wait_ge(s_used, FREE + (x - 1) * KG + j // GROUP + 1)
                                        pool.sem_inc(s_went, 1)
                                    nc.gpsimd.indirect_dma_start(
                                        out=rows16[:, j, 0:2 * D], out_offset=None, in_=xn16_dram[:, :],
                                        in_offset=bass.IndirectOffsetOnAxis(ap=meta_src[:, w, j:j + 1], axis=0)).then_inc(s_row[j], 16)
                    windows(pool, body)

                @block.vector
                def _(dve):
                    dve.sem_inc(s_sum, 1)
                    dve.sem_inc(s_post, 1)
                    if dense:
                        dve.sem_inc(s_taken, ND)

                    def body(r, b, rb):
                        def masks(w, q):
                            x = rb * NG + G_SLOT[w]
                            if q == 0:
                                dve.wait_ge(s_meta[w], (rb + 1) * 32)
                                nc.vector.tensor_scalar(dst_local[:, w, :], meta_dst[:, w, :], node_base[:, ds(b * U + w, 1)], None,
                                                        ALU.subtract).then_inc(s_local, 1)
                                dve.wait_ge(s_local, x + 1)
                            dve.wait_ge(s_used, FREE + x * KG + q - RING + 1)
                            for j in range(q * GROUP, (q + 1) * GROUP):
                                m = nc.vector.tensor_scalar(masks16[:, j % (RING * GROUP), :], col_row[:, 0:P],
                                                            dst_local[:, w, j:j + 1], None, ALU.is_equal)
                            m.then_inc(s_mask, 1)

                        def columns(w):
                            d = rb * ND + D_SLOT[w]
                            n = [0]

                            def link(ins):
                                n[0] += 1
                                ins.then_inc(s_calc, 1)
                                dve.wait_ge(s_calc, d * 8 + n[0])
                            dve.wait_ge(s_meta[w], (rb + 1) * 16 * 2 * SUBS)
                            nc.vector.tensor_copy(meta_f, dense_meta[:, D_SLOT[w], :, :, :]).then_inc(s_taken, 1)
                            dve.wait_ge(s_taken, ND + d + 1)
                            link(nc.vector.tensor_scalar(block_of, meta_f[:, 0, :, :], 1.0 / P, -(P // 2) / P, ALU.mult, ALU.add))
                            link(nc.vector.tensor_scalar(block_of, block_of, float(3 << 22), None, ALU.add))
                            link(nc.vector.tensor_scalar(block_of, block_of, float(3 << 22), None, ALU.subtract))
                            link(nc.vector.scalar_tensor_tensor(row_of[D_SLOT[w]], block_of, -float(P), meta_f[:, 0, :, :], ALU.mult, ALU.add))
                            link(nc.vector.scalar_tensor_tensor(col_of[D_SLOT[w]], meta_f[:, 1, :, :], node_base[:, ds(b * U + w, 1)],
                                                                sub_base[:, :].unsqueeze(2).broadcast_to([128, SUBS, SUB_TILES]),
                                                                ALU.subtract, ALU.subtract))
                            link(nc.vector.tensor_scalar(beyond, col_of[D_SLOT[w]], float(SUB), float(1 << 16), ALU.is_ge, ALU.mult))
                            link(nc.vector.scalar_tensor_tensor(col_of[D_SLOT[w]], block_of, float(SUB), col_of[D_SLOT[w]], ALU.mult, ALU.add))
                            link(nc.vector.tensor_tensor(col_of[D_SLOT[w]], col_of[D_SLOT[w]], beyond, ALU.add))

                        def hots(w, lo, hi):
                            d = rb * ND + D_SLOT[w]
                            for k in range(lo, hi):
                                dve.wait_ge(s_tile, TILES + d * (SUBS * SUB_TILES) + (k - 2 if k >= 3 else 0))
                                at = (slice(None), k // SUB_TILES, slice(k % SUB_TILES, k % SUB_TILES + 1))
                                nc.vector.tensor_scalar(row_hot[:, k % 4, :], col_row[:, 0:P], row_of[D_SLOT[w]][at], None, ALU.is_equal)
                                nc.vector.tensor_scalar(col_hot[:, k % 3, :], col_row[:, :], col_of[D_SLOT[w]][at], None, ALU.is_equal).then_inc(s_hot, 1)

                        def add(w):
                            g = rb * U + w
                            acc = psum[w % 2]
                            if kinds[w] == "G":
                                dve.wait_ge(s_used, FREE + (rb * NG + G_SLOT[w] + 1) * KG)
                            else:
                                dve.wait_ge(s_dense, rb * ND + D_SLOT[w] + 1)
                            last_use = g - 1 if w else g
                            if not dense:
                                dve.wait_ge(s_kept, 1 + last_use)
                            dve.wait_ge(s_t, 1 + last_use)
                            nc.vector.tensor_tensor(summed[:, w % 2, 0:D], acc[0:P, 0:D], tok[:, ds(b * U + w, 1), :],
                                                    ALU.add).then_inc(s_sum, 1)
                            nc.vector.tensor_tensor(degree[:, ds(b * U + w, 1)], acc[0:P, D:D + 1], degree[:, ds(b * U + w, 1)],
                                                    ALU.add).then_inc(s_sum, 1)

                        def bias(w):
                            g = rb * U + w
                            for q in range(2):
                                dve.wait_ge(s_proj, 2 * g + q + 1)
                                nc.vector.tensor_tensor(
                                    h1T[:, 4 * q:4 * q + 4, ds((b * U + w) * P, P)],
                                    psum[4 + q][:, 0:4 * P].rearrange("p (m n) -> p m n", m=4),
                                    b1g[:, 4 * q:4 * q + 4].unsqueeze(2).broadcast_to([128, 4, P]), ALU.add).then_inc(s_post, 1)

                        def statistics(w):
                            for m in range(HC):
                                if m % 4 == 0:
                                    dve.wait_ge(s_post, 1 + 2 * (rb * U + w) + m // 4 + 1)
                                nc.vector.bn_stats(bn6[:, m, ds(b * U + w, 1), :], h1T[:, m, ds((b * U + w) * P, P)])

                        if not dense:
                            for w in range(U):
                                for q in range(KG):
                                    masks(w, q)
                                add(w)
                                bias(w)
                                statistics(w)
                            return
                        masks(0, 0)
                        masks(0, 1)
                        columns(1)
                        for k in range(SUBS):
                            hots(1, k * SUB_TILES, (k + 1) * SUB_TILES)
                            if k + 2 < KG:
                                masks(0, k + 2)
                        columns(3)
                        add(0)
                        hots(3, 0, 3)
                        masks(2, 0)
                        add(1)
                        masks(2, 1)
                        bias(0)
                        hots(3, 3, 7)
                        masks(2, 2)
                        statistics(0)
                        bias(1)
                        hots(3, 7, 8)
                        masks(2, 3)
                        hots(3, 8, 12)
                        statistics(1)
                        masks(2, 4)
                        hots(3, 12, 16)
                        masks(2, 5)
                        hots(3, 16, 20)
                        add(2)
                        masks(4, 0)
                        masks(4, 1)
                        add(3)
                        masks(4, 2)
                        bias(2)
                        for q in range(3, KG):
                            masks(4, q)
                        statistics(2)
                        add(4)
                        bias(3)
                        statistics(3)
                        bias(4)
                        statistics(4)
                    windows(dve, body)

                @block.tensor
                def _(pe):
                    pe.sem_inc(s_used, FREE)
                    pe.sem_inc(s_t, 1)
                    if dense:
                        pe.sem_inc(s_tile, TILES)
                    pe.wait_ge(s_one, 1)

                    def body(r, b, rb):
                        def bank_free(w):
                            g = rb * U + w
                            pe.wait_ge(s_sum, 1 + ((g - 1) * 2 if w else g * 2))

                        def gathered(w, q):
                            x = rb * NG + G_SLOT[w]
                            if q == 0:
                                bank_free(w)
                            pe.wait_ge(s_mask, x * KG + q + 1)
                            for j in range(q * GROUP, (q + 1) * GROUP):
                                pe.wait_ge(s_row[j], (x + 1) * 16)
                                mask = masks16[:, j % (RING * GROUP), :]
                                nc.tensor.matmul(psum[w % 2][0:P, 0:D + 1], mask, rows16[:, j, D:2 * D + 1], start=(j == 0), stop=False)
                                last = nc.tensor.matmul(psum[w % 2][0:P, 0:D], mask, rows16[:, j, 0:D], start=False, stop=(j == KS - 1))
                            last.then_inc(s_used, 1)

                        def build(w, s):
                            d = rb * ND + D_SLOT[w]
                            first = 2 * s
                            for k in range(SUB_TILES):
                                pe.wait_ge(s_hot, d * (SUBS * SUB_TILES) + s * SUB_TILES + k + 1)
                                for half in range(2):
                                    if k == 0:
                                        pe.wait_ge(s_evac, HALVES + d * (2 * SUBS) + (first + half - 2 if s else 0))
                                    lo, hi = HALF[half] * SUB, HALF[half + 1] * SUB
                                    n = s * SUB_TILES + k
                                    last = nc.tensor.matmul(psum[BUILD[(first + half) % 3]][0:P, 0:hi - lo], row_hot[:, n % 4, :],
                                                            col_hot[:, n % 3, lo:hi], start=(k == 0), stop=(k == SUB_TILES - 1))
                                last.then_inc(s_tile, 1)

                        def multiply(w, lo, hi):
                            if lo == 0:
                                bank_free(w)
                                pe.wait_ge(s_evac, HALVES + (rb * ND + D_SLOT[w] + 1) * (2 * SUBS))
                            for k in range(lo, hi):
                                for part in range(2):
                                    nc.tensor.matmul(psum[w % 2][0:P, 0:D], adjacency[:, k, :], x16[:, k, part * D:(part + 1) * D],
                                                     start=(k == 0 and part == 0), stop=(k == T - 1 and part == 1))
                            if hi == T:
                                for k in range(T):
                                    last = nc.tensor.matmul(psum[w % 2][0:P, D:D + 1], adjacency[:, k, :], rows16[0:P, 0, 2 * D:2 * D + 1],
                                                            start=(k == 0), stop=(k == T - 1))
                                last.then_inc(s_dense, 1)

                        def turn(w):
                            g = rb * U + w
                            pe.wait_ge(s_sum, 1 + (g + 1) * 2)
                            for c in range(DC):
                                last = nc.tensor.transpose(psum[2][:, c * P:(c + 1) * P], summed[:, w % 2, c * 128:(c + 1) * 128],
                                                           ident[0:P, 0:P])
                            last.then_inc(s_t, 1)

                        def project(w):
                            g = rb * U + w
                            pe.wait_ge(s_ht, g + 1)
                            pe.wait_ge(s_post, 1 + 2 * g)
                            for q in range(2):
                                for m in range(4):
                                    for c in range(DC):
                                        last = nc.tensor.matmul(psum[4 + q][:, m * P:(m + 1) * P],
                                                                w1g[:, c, (4 * q + m) * 128:(4 * q + m + 1) * 128],
                                                                hT[:, c, :], start=(c == 0), stop=(c == DC - 1))
                                last.then_inc(s_proj, 1)

                        if not dense:
                            for w in range(U):
                                for q in range(KG):
                                    gathered(w, q)
                                turn(w)
                                project(w)
                            return
                        for w in (0, 2):
                            gathered(w, 0)
                            if w == 0:
                                gathered(w, 1)
                            build(w + 1, 0)
                            if w:
                                project(w - 1)
                                gathered(w, 1)
                            for k in range(1, SUBS):
                                if w:
                                    build(w + 1, k)
                                    gathered(w, k + 1)
                                else:
                                    gathered(w, k + 1)
                                    build(w + 1, k)
                            multiply(w + 1, 0, T // 2)
                            turn(w)
                            multiply(w + 1, T // 2, T)
                            project(w)
                            turn(w + 1)
                        for q in range(KG):
                            gathered(4, q)
                        project(3)
                        turn(4)
                        project(4)
                    windows(pe, body)

                @block.scalar
                def _(act):
                    if dense:
                        act.sem_inc(s_evac, HALVES)
                    else:
                        act.sem_inc(s_kept, 1)

                    def body(r, b, rb):
                        def copies(w):
                            g = rb * U + w
                            if not dense:
                                act.wait_ge(s_sum, 1 + (g + 1) * 2)
                                nc.scalar.copy(tok[:, ds(b * U + w, 1), :], summed[:, w % 2:w % 2 + 1, 0:D]).then_inc(s_kept, 1)
                            act.wait_ge(s_t, 1 + g + 1)
                            nc.scalar.copy(hT[:, 0:DC, :], psum[2][:, 0:DC * P].rearrange("p (c n) -> p c n", c=DC)).then_inc(s_ht, 1)

                        def matrix(w):
                            d = rb * ND + D_SLOT[w]
                            for s in range(SUBS):
                                act.wait_ge(s_tile, TILES + d * (SUBS * SUB_TILES) + (s + 1) * SUB_TILES)
                                for half in range(2):
                                    lo, hi = HALF[half], HALF[half + 1]
                                    nc.scalar.copy(adjacency[:, lo:hi, s * SUB:(s + 1) * SUB],
                                                   psum[BUILD[(2 * s + half) % 3]][0:P, 0:(hi - lo) * SUB].rearrange(
                                                       "p (k n) -> p k n", n=SUB)).then_inc(s_evac, 1)

                        if not dense:
                            for w in range(U):
                                copies(w)
                            return
                        for w in (0, 2):
                            matrix(w + 1)
                            copies(w)
                            copies(w + 1)
                        copies(4)
                    windows(act, body)

        def graph(layer):
            weighted = layer == 1
            s_meta = [sem(f"s_meta{layer}_{w}") for w in range(U)]
            s_row = [sem(f"s_row{layer}_{j}") for j in range(KS)]
            s_local = sem(f"s_local{layer}"); s_mask = sem(f"s_mask{layer}"); s_used = sem(f"s_used{layer}")
            s_sum = sem(f"s_sum{layer}"); s_kept = sem(f"s_kept{layer}"); s_t = sem(f"s_t{layer}")
            s_ht = sem(f"s_ht{layer}"); s_proj = sem(f"s_proj{layer}"); s_post = sem(f"s_post{layer}")
            s_f = sem(f"s_f{layer}"); s_one = sem(f"s_one{layer}")
            s_nop = sem(f"s_nop{layer}"); s_nop2 = sem(f"s_nop2{layer}"); s_tmp = sem(f"s_tmp{layer}")
            W = D if weighted else D + 1
            META = 64 if weighted else 48
            TC = U if weighted else 1
            ONE = 1
            CREDIT = U * GROUPS
            fbuf = view(work, 0, [U, D], P)
            hm = view(work, U * D, [2, D], P)
            relu_in = view(work, (U + 2) * D, [2, D], P)
            with nc.Block() as block:
                def windows(eng, body):
                    n = eng.value_load(rounds[0:1, 0:1], min_val=1, max_val=ROUNDS)
                    with eng.Fori(0, n) as r:
                        with eng.Fori(0, T // U) as b:
                            for w in range(U):
                                body(r, r * T + b * U + w, b * U + w, w, r * (T // U) + b)

                @block.sync
                def _(sp):
                    def body(r, g, t, w, rb):
                        sp.wait_ge(s_used, CREDIT + (g - U + 1) * GROUPS)
                        if weighted:
                            sp.sem_inc(s_nop2, 1)
                            sp.wait_ge(s_t, U + g - U + 1)
                        sp.sem_inc(s_nop2, 1)
                        at = sp.value_load(starts[0:1, ds(t, 1)], min_val=0, max_val=NE)
                        at = sp.snap(at + r * WIN)
                        for to, frm in ((meta_src, src_pad), (meta_dst, dst_pad), (meta_ew, ew_pad)):
                            sp.dma_start(to[:, w, :], frm[ds(at, WIN)].rearrange("(p j) -> p j", j=KS)).then_inc(s_meta[w], 16)
                        if weighted:
                            sp.dma_start(fbuf[:, w, :], xn_dram[ds(t * P, P), :]).then_inc(s_meta[w], 16)
                    windows(sp, body)


                @block.gpsimd
                def _(pool):
                    nc.gpsimd.memset(rows[:, :, D:D + 1], 1.0).then_inc(s_one, 1)
                    nc.gpsimd.memset(tok[:, :, :], 0.0).then_inc(s_one, 1) if weighted else None

                    def body(r, g, t, w, rb):
                        pool.wait_ge(s_meta[w], (rb + 1) * META)
                        pool.sem_inc(s_nop, 1)
                        for j in range(KS):
                            if j % GROUP == 0:
                                pool.wait_ge(s_used, CREDIT + (g - 1) * GROUPS + j // GROUP + 1)
                                pool.sem_inc(s_nop, 1)
                            nc.gpsimd.indirect_dma_start(
                                out=rows[:, j, 0:D], out_offset=None, in_=xn_dram[:, :],
                                in_offset=bass.IndirectOffsetOnAxis(ap=meta_src[:, w, j:j + 1], axis=0)).then_inc(s_row[j], 16)
                    windows(pool, body)

                @block.vector
                def _(dve):
                    dve.wait_ge(s_one, 2 if weighted else 1)
                    dve.sem_inc(s_sum, ONE)
                    dve.sem_inc(s_post, ONE)
                    dve.sem_inc(s_tmp, ONE)

                    def body(r, g, t, w, rb):
                        dve.wait_ge(s_meta[w], (rb + 1) * META)
                        nc.vector.tensor_scalar(dst_local[:, w, :], meta_dst[:, w, :], node_base[:, ds(t, 1)], None,
                                                ALU.subtract).then_inc(s_local, 1)
                        dve.wait_ge(s_local, g + 1)
                        for j in range(KS):
                            if j % GROUP == 0:
                                dve.wait_ge(s_used, CREDIT + (g - 1) * GROUPS + j // GROUP + 1)
                            if weighted:
                                m = nc.vector.tensor_scalar(masks[:, j, :], node_row[:, :], dst_local[:, w, j:j + 1],
                                                            meta_ew[:, w, j:j + 1], ALU.is_equal, ALU.mult)
                            else:
                                m = nc.vector.tensor_scalar(masks[:, j, :], node_row[:, :], dst_local[:, w, j:j + 1],
                                                            None, ALU.is_equal)
                            if j % GROUP == GROUP - 1:
                                m.then_inc(s_mask, 1)
                        acc = psum[w % 2]
                        dve.wait_ge(s_used, CREDIT + (g + 1) * GROUPS)
                        last_use = g - 1 if w else g
                        dve.wait_ge(s_kept, ONE + last_use)
                        dve.wait_ge(s_t, last_use + TC)
                        nc.vector.tensor_tensor(summed[:, w % 2, 0:D], acc[0:P, 0:D], tok[:, ds(t, 1), :],
                                                ALU.add).then_inc(s_sum, 1)
                        if not weighted:
                            nc.vector.tensor_tensor(degree[:, ds(t, 1)], acc[0:P, D:D + 1], degree[:, ds(t, 1)],
                                                    ALU.add).then_inc(s_sum, 1)
                            for q in range(2):
                                dve.wait_ge(s_proj, 2 * g + q + 1)
                                nc.vector.tensor_tensor(
                                    h1T[:, 4 * q:4 * q + 4, ds(t * P, P)],
                                    psum[4 + q][:, 0:4 * P].rearrange("p (m n) -> p m n", m=4),
                                    b1g[:, 4 * q:4 * q + 4].unsqueeze(2).broadcast_to([128, 4, P]), ALU.add).then_inc(s_post, 1)
                            for m in range(HC):
                                if m % 4 == 0:
                                    dve.wait_ge(s_post, ONE + 2 * g + m // 4 + 1)
                                last = nc.vector.bn_stats(bn6[:, m, ds(t, 1), :], h1T[:, m, ds(t * P, P)])
                        else:
                            dve.wait_ge(s_sum, ONE + g + 1)
                            nc.vector.tensor_scalar(hm[:, w % 2, :], summed[:, w % 2, 0:D], rdegree[:, ds(t, 1)], None,
                                                    ALU.mult).then_inc(s_post, 1)
                            dve.wait_ge(s_proj, g + 1)
                            nc.vector.tensor_tensor(relu_in[:, w % 2, :], psum[4 + w % 2][0:P, 0:D], gb_bc[0:P, :],
                                                    ALU.add).then_inc(s_tmp, 1)
                            dve.wait_ge(s_tmp, ONE + g + 1)
                            nc.vector.scalar_tensor_tensor(x3[:, ds(t, 1), :], relu_in[:, w % 2:w % 2 + 1, :], 0.0,
                                                           xres[:, ds(t, 1), :], ALU.max, ALU.add)
                    windows(dve, body)

                @block.tensor
                def _(pe):
                    pe.sem_inc(s_used, CREDIT)
                    pe.sem_inc(s_t, TC)
                    pe.wait_ge(s_one, 1)
                    SUMS = 1 if weighted else 2

                    def body(r, g, t, w, rb):
                        acc = psum[w % 2]
                        if w >= 1:
                            pe.wait_ge(s_sum, ONE + (g - 1) * SUMS)
                        else:
                            pe.wait_ge(s_sum, ONE + g * SUMS)
                        for j in range(KS):
                            if j % GROUP == 0:
                                pe.wait_ge(s_mask, g * GROUPS + j // GROUP + 1)
                            pe.wait_ge(s_row[j], (g + 1) * 16)
                            m = nc.tensor.matmul(acc[0:P, 0:W], masks[:, j, :], rows[:, j, 0:W], start=(j == 0), stop=(j == KS - 1))
                            if j % GROUP == GROUP - 1:
                                m.then_inc(s_used, 1)
                        pe.wait_ge(s_sum, ONE + (g + 1) * SUMS)
                        if not weighted:
                            for c in range(DC):
                                last = nc.tensor.transpose(psum[2][:, c * P:(c + 1) * P], summed[:, w % 2, c * 128:(c + 1) * 128],
                                                           ident[0:P, 0:P])
                            last.then_inc(s_t, 1)
                            pe.wait_ge(s_ht, g + 1)
                            pe.wait_ge(s_post, ONE + 2 * g)
                            for q in range(2):
                                for m in range(4):
                                    for c in range(DC):
                                        last = nc.tensor.matmul(psum[4 + q][:, m * P:(m + 1) * P],
                                                                w1g[:, c, (4 * q + m) * 128:(4 * q + m + 1) * 128],
                                                                hT[:, c, :], start=(c == 0), stop=(c == DC - 1))
                                last.then_inc(s_proj, 1)
                        else:
                            pe.wait_ge(s_post, ONE + g + 1)
                            pe.wait_ge(s_meta[w], (rb + 1) * META)
                            for c in range(2 * DC):
                                frm = fbuf[:, w, c * 128:(c + 1) * 128] if c < DC else hm[:, w % 2, (c - DC) * 128:(c - DC + 1) * 128]
                                last = nc.tensor.transpose(psum[2][:, c * P:(c + 1) * P], frm, ident[0:P, 0:P])
                            last.then_inc(s_t, 1)
                            pe.wait_ge(s_ht, g + 1)
                            pe.wait_ge(s_tmp, ONE + (g - 1 if w >= 1 else g))
                            for c in range(2 * DC):
                                last = nc.tensor.matmul(psum[4 + w % 2][0:P, 0:D], hT[:, c, :], wT[:, c, :],
                                                        start=(c == 0), stop=(c == 2 * DC - 1))
                            last.then_inc(s_proj, 1)
                    windows(pe, body)

                @block.scalar
                def _(act):
                    if weighted:
                        first = act.value_load(i_first[0:1, 0:1], min_val=0, max_val=N - 1)
                        act.dma_start(g_col[:, :], xn_dram[ds(first, 1), :].rearrange("a (c p) -> p (a c)", p=128),
                                      allow_slow_non_contiguous=True).then_inc(s_f, 16)
                        act.wait_ge(s_f, 16)

                    act.sem_inc(s_kept, ONE)

                    def body(r, g, t, w, rb):
                        act.wait_ge(s_sum, ONE + (g + 1) * (1 if weighted else 2))
                        nc.scalar.copy(tok[:, ds(t, 1), :], summed[:, w % 2:w % 2 + 1, 0:D]).then_inc(s_kept, 1)
                        if not weighted:
                            act.wait_ge(s_t, g + 1 + TC)
                            nc.scalar.copy(hT[:, 0:DC, :], psum[2][:, 0:DC * P].rearrange("p (c n) -> p c n", c=DC)).then_inc(s_ht, 1)
                        else:
                            act.wait_ge(s_t, g + 1 + TC)
                            nc.scalar.copy(hT[:, 0:DC, :], psum[2][:, 0:DC * P].rearrange("p (c n) -> p c n", c=DC))
                            for c in range(DC):
                                a = nc.scalar.activation(hT[:, DC + c, :], psum[2][:, (DC + c) * P:(DC + c + 1) * P], ACT.Copy,
                                                         scale=g_col[:, c:c + 1])
                            a.then_inc(s_ht, 1)
                    windows(act, body)

        def dispatch(layer, E, F, w1, w2, softmax_first):
            NT = moe_tiles(E)
            FC = F // 128
            B = T // U
            first = layer == 0
            w1s, w2s, early = expert_weights(layer, E, F)
            pools = [[work, 1600, 4096], [arena, 31400, 32768]] if first else [[arena, 26624, 32768]]

            def small(dims, parts=P, dt=fp32):
                size = 1
                for d in dims:
                    size *= d
                size += size % 2
                pool = next(p for p in pools if p[1] + size <= p[2])
                v = view(pool[0], pool[1], dims, parts)
                pool[1] += size
                return v if dt is fp32 else v.bitcast(dt)

            ysum = view(work, 0, [2, D], P)
            tT = view(work, 2 * D, [4, DC, P])
            lg = small([T, E]); v8 = small([T, 8]); i8 = small([T, 8], dt=u32); ex = small([T, 8]); zs = small([T])
            idf = small([T, 2]); sel = small([T, 2, E]); both = small([T, E]); rank = small([T, E])
            picked = small([T, 2, E]); posf = small([T, E]); place = small([T, 2])
            cum = small([T + 1, E]); cf = small([E]); ci = small([E], dt=i32); padded = small([E])
            ends = [small([E]), small([E])]; base = small([E]); adj = small([E], 1)
            tcmp = small([NT, E], 1); tcount = small([NT], 1); valid = small([NT], 1)
            wts, pos, pos_in, comb, tile_expert, tile_row, pad_row = routing(E)

            def over(a, n=T, p=P):
                return a.unsqueeze(1).broadcast_to([p, n, E])

            s_w2 = sem("s_w2"); s_wl = sem("s_wl"); s_bn = sem("s_bn"); s_bns = sem("s_bns"); s_norm = sem("s_norm")
            s_y = sem("s_y"); s_ycopy = sem("s_ycopy"); s_x = sem("s_x"); s_st = sem("s_st"); s_var = sem("s_var")
            s_sq = sem("s_sq"); s_rs = sem("s_rs"); s_tok = sem("s_tok"); s_lt = sem("s_lt"); s_lc = sem("s_lc")
            s_lg = sem("s_lg"); s_lgr = sem("s_lgr"); s_both = sem("s_both"); s_rank = sem("s_rank"); s_rkr = sem("s_rkr")
            s_pos = sem("s_pos"); s_total = sem("s_total"); s_own = sem("s_own"); s_top = sem("s_top"); s_shift = sem("s_shift")
            s_ex = sem("s_ex"); s_sc = sem("s_sc"); s_pad = sem("s_pad"); s_padrow = sem("s_padrow"); s_cum = sem("s_cum"); s_xl = sem("s_xl"); s_zero = sem("s_zero")

            with nc.Block() as block:
                @block.sync
                def _(sp):
                    if first:
                        sp.dma_start(w2g, L0_gnn_W2.rearrange("(m p) d -> p m d", p=128)).then_inc(s_w2, 16)
                        sp.dma_start(b2g_bc, L0_gnn_b2.partition_broadcast(128)).then_inc(s_w2, 16)
                        sp.dma_start(xres[:, :, :], x.rearrange("(t p) d -> p t d", p=P)).then_inc(s_xl, 16)
                        sp.wait_ge(s_w2, 32)
                    for e in range(E):
                        sp.dma_start(w1s[:, e * DC * F:(e + 1) * DC * F].rearrange("p (c f) -> p c f", c=DC),
                                     w1[e].rearrange("(c p) f -> p c f", p=128)).then_inc(s_wl, 16)
                    if not first:
                        sp.wait_ge(s_x, T)
                    for e in range(early):
                        sp.dma_start(w2s[:, e * FC * D:(e + 1) * FC * D].rearrange("p (c d) -> p c d", c=FC),
                                     w2[e].rearrange("(c p) d -> p c d", p=128)).then_inc(s_wl, 16)
                    sp.wait_ge(s_wl, 16 * (E + early))
                    if first:
                        sp.wait_ge(s_xl, 16)
                        sp.wait_ge(s_zero, 1)
                    sp.wait_ge(s_padrow, 1)
                    for e in range(E):
                        row = sp.value_load(pad_row[0:1, e:e + 1], min_val=e * REGION, max_val=e * REGION + N)
                        sp.dma_start(slots_in[ds(row, 128), :], zero_rows[:, :]).then_inc(s_pad, 16)
                    sp.wait_ge(s_pad, 16 * E)

                @block.scalar
                def _(act):
                    def batch_norm(b):
                        for m in range(HC):
                            part = h1T[:, m, b * U * P:(b + 1) * U * P]
                            nc.scalar.activation(part, part, ACT.Relu, bias=bn_shift[:, m:m + 1],
                                                 scale=bn_scale[:, m:m + 1]).then_inc(s_norm, 1)

                    if first:
                        act.wait_ge(s_bn, HC)
                        nc.scalar.activation(bn_shift[:, :], bnmv[:, :, 1], ACT.Sqrt, bias=eps[:, :]).then_inc(s_bns, 1)
                        act.wait_ge(s_bn, HC + 4)
                        batch_norm(0)
                        batch_norm(1)
                    else:
                        for t in range(T):
                            nc.scalar.copy(xres[:, t, :], x3[:, t, :]).then_inc(s_x, 1)
                    def roots(b):
                        act.wait_ge(s_var, (b + 1) * U)
                        nc.scalar.activation(mean_v[:, b * U:(b + 1) * U], mv[:, b * U:(b + 1) * U, 1], ACT.Sqrt,
                                             bias=eps[0:P, :]).then_inc(s_sq, 1)

                    def copies(b):
                        for t in range(b * U, (b + 1) * U):
                            act.wait_ge(s_lt, t + 1)
                            if t >= 4:
                                act.wait_ge(s_lg, t - 3)
                            nc.scalar.copy(tT[:, t % 4, :, :], psum[2 + t % 2][:, 0:DC * P].rearrange("p (c n) -> p c n", c=DC)).then_inc(s_lc, 1)

                    if first:
                        for b in range(B):
                            roots(b)
                            if b + 2 < B:
                                batch_norm(b + 2)
                            copies(b)
                    else:
                        roots(0)
                        roots(1)
                        for b in range(B):
                            copies(b)
                            if b + 2 < B:
                                roots(b + 2)
                    n = 8 if softmax_first else 2
                    act.wait_ge(s_shift, 1)
                    nc.scalar.activation(ex[:, :, 0:n], ex[:, :, 0:n], ACT.Exp).then_inc(s_ex, 1)

                @block.gpsimd
                def _(pool):
                    if first:
                        pool.memset(zero_rows[:, :], 0.0).then_inc(s_zero, 1)
                    for t in range(T):
                        if t % U == 0:
                            pool.wait_ge(s_pos, t // U + 1)
                        for k in range(2):
                            nc.gpsimd.indirect_dma_start(
                                out=slots_in[:, :], out_offset=bass.IndirectOffsetOnAxis(ap=pos_in[:, t, k:k + 1], axis=0),
                                in_=tok[:, t, :], in_offset=None).then_inc(s_sc, 16)
                    pool.wait_ge(s_sc, 16 * 2 * T)

                @block.tensor
                def _(pe):
                    def product(t):
                        if t >= 2:
                            pe.wait_ge(s_ycopy, t - 1)
                        for m in range(HC):
                            if t % U == 0:
                                pe.wait_ge(s_norm, t // U * HC + m + 1)
                            last = nc.tensor.matmul(psum[t % 2][0:P, 0:D], h1T[:, m, t * P:(t + 1) * P], w2g[:, m, :],
                                                    start=(m == 0), stop=(m == HC - 1))
                        last.then_inc(s_y, 1)

                    def logits(t):
                        b = t // U
                        pe.wait_ge(s_lc, t + 1)
                        if t % U == 0 and b >= 2:
                            pe.wait_ge(s_lgr, b - 1)
                        for c in range(DC):
                            last = nc.tensor.matmul(psum[4 + b % 2][0:P, (t % U) * E:(t % U + 1) * E], tT[:, t % 4, c, :],
                                                    gateT[layer][:, c, :], start=(c == 0), stop=(c == DC - 1))
                        last.then_inc(s_lg, 1)

                    def transposes_and_logits(b):
                        for t in range(b * U, (b + 1) * U):
                            pe.wait_ge(s_tok, t + 1)
                            if t >= 2:
                                pe.wait_ge(s_lc, t - 1)
                            for c in range(DC):
                                last = nc.tensor.transpose(psum[2 + t % 2][:, c * P:(c + 1) * P], tok[:, t, c * 128:(c + 1) * 128],
                                                           ident[0:P, 0:P])
                            last.then_inc(s_lt, 1)
                            if t % U:
                                logits(t - 1)
                        logits((b + 1) * U - 1)

                    def ranks(b):
                        pe.wait_ge(s_cum, (b + 1) * U)
                        if b >= 2:
                            pe.wait_ge(s_rkr, b - 1)
                        to = psum[6 + b % 2][0:P, 0:U * E]
                        nc.tensor.matmul(to, before[:, :], both[:, b * U:(b + 1) * U, :].rearrange("p t e -> p (t e)"), start=True, stop=False)
                        last = nc.tensor.matmul(to, ones[0:P, 0:P], cum[:, b * U:(b + 1) * U, :].rearrange("p t e -> p (t e)"), start=False, stop=True)
                        last.then_inc(s_rank, 1)

                    if first:
                        pe.wait_ge(s_w2, 32)
                    if first:
                        for b in range(B + 2):
                            if b < B:
                                product(b * U)
                                product(b * U + 1)
                            if b >= 2:
                                ranks(b - 2)
                            if b < B:
                                for t in range(b * U + 2, (b + 1) * U):
                                    product(t)
                            if 1 <= b <= B:
                                transposes_and_logits(b - 1)
                    else:
                        transposes_and_logits(0)
                        transposes_and_logits(1)
                        for b in range(B):
                            ranks(b)
                            if b + 2 < B:
                                transposes_and_logits(b + 2)
                    pe.wait_ge(s_cum, T)
                    nc.tensor.matmul(psum[0][0:P, 0:E], ones[0:P, 0:P], cum[:, T, :], start=True, stop=True).then_inc(s_total, 1)

                @block.vector
                def _(dve):
                    link = chain(dve, s_own)

                    def residual(t):
                        if first:
                            dve.wait_ge(s_y, t + 1)
                            nc.vector.tensor_tensor(ysum[:, t % 2, :], psum[t % 2][0:P, 0:D], b2g_bc[0:P, :], ALU.add).then_inc(s_ycopy, 1)
                            dve.wait_ge(s_ycopy, t + 1)
                            nc.vector.scalar_tensor_tensor(xres[:, t, :], ysum[:, t % 2, :], 0.0, xres[:, t, :],
                                                           ALU.max, ALU.add).then_inc(s_x, 1)
                        dve.wait_ge(s_x, t + 1)
                        nc.vector.bn_stats(st6[:, t, :], xres[:, t, :]).then_inc(s_st, 1)

                    def variances(b):
                        for t in range(b * U, (b + 1) * U):
                            dve.wait_ge(s_st, t + 1)
                            nc.vector.bn_aggr(mv[:, t, :], st6[:, t, :]).then_inc(s_var, 1)

                    def normalise(b):
                        dve.wait_ge(s_sq, b + 1)
                        nc.vector.reciprocal(rstd[:, b * U:(b + 1) * U], mean_v[:, b * U:(b + 1) * U]).then_inc(s_rs, 1)
                        dve.wait_ge(s_rs, b + 1)
                        for t in range(b * U, (b + 1) * U):
                            nc.vector.tensor_scalar(tok[:, t, :], xres[:, t, :], mv[:, t, 0:1], rstd[:, t:t + 1],
                                                    ALU.subtract, ALU.mult).then_inc(s_tok, 1)

                    def choose(b):
                        r = slice(b * U, (b + 1) * U)
                        dve.wait_ge(s_lg, (b + 1) * U)
                        pt = psum[4 + b % 2][0:P, 0:U * E].rearrange("p (t e) -> p t e", e=E)
                        if first:
                            nc.vector.tensor_copy(lg[:, r, :], pt).then_inc(s_lgr, 1)
                        else:
                            nc.vector.tensor_tensor(lg[:, r, :], pt, over(gateb_bc[0:P, 0:E], U), ALU.add).then_inc(s_lgr, 1)
                        dve.wait_ge(s_lgr, b + 1)
                        for t in range(b * U, (b + 1) * U):
                            nc.vector.max(v8[:, t, :], lg[:, t, :]).then_inc(s_top, 1)
                        for n, t in enumerate(range(b * U, (b + 1) * U)):
                            dve.wait_ge(s_top, 2 * b * U + n + 1)
                            nc.vector.max_index(i8[:, t, :], v8[:, t, :], lg[:, t, :]).then_inc(s_top, 1)
                        dve.wait_ge(s_top, 2 * (b + 1) * U)
                        link(nc.vector.tensor_copy(idf[:, r, :], i8[:, r, 0:2]))
                        link(nc.vector.tensor_tensor(sel[:, r, :, :], expert_row[0:P, 0:E].unsqueeze(1).unsqueeze(1).broadcast_to([P, U, 2, E]),
                                                     idf[:, r, :].unsqueeze(3).broadcast_to([P, U, 2, E]), ALU.is_equal))
                        nc.vector.tensor_tensor(both[:, r, :], sel[:, r, 0, :], sel[:, r, 1, :], ALU.add).then_inc(s_both, 1)
                        dve.wait_ge(s_both, b + 1)
                        for t in range(b * U, (b + 1) * U):
                            nc.vector.tensor_tensor(cum[:, t + 1, :], cum[:, t, :], both[:, t, :], ALU.add).then_inc(s_cum, 1)
                            dve.wait_ge(s_cum, t + 1)

                    def places(b):
                        r = slice(b * U, (b + 1) * U)
                        dve.wait_ge(s_rank, b + 1)
                        nc.vector.tensor_copy(rank[:, r, :], psum[6 + b % 2][0:P, 0:U * E].rearrange("p (t e) -> p t e", e=E)).then_inc(s_rkr, 1)
                        dve.wait_ge(s_rkr, b + 1)
                        link(nc.vector.tensor_tensor(posf[:, r, :], rank[:, r, :], over(region_row[0:P, 0:E], U), ALU.add))
                        link(nc.vector.tensor_tensor(picked[:, r, :, :], sel[:, r, :, :],
                                                     posf[:, r, :].unsqueeze(2).broadcast_to([P, U, 2, E]), ALU.mult))
                        link(nc.vector.tensor_reduce(place[:, r, :], picked[:, r, :, :], AX.X, ALU.add))
                        nc.vector.tensor_copy(pos_in[:, r, :], place[:, r, :]).then_inc(s_pos, 1)

                    if first:
                        for m in range(HC):
                            nc.vector.bn_aggr(bnmv[:, m, :], bn6[:, m, :, :].rearrange("p t s -> p (t s)")).then_inc(s_bn, 1)
                        dve.wait_ge(s_bns, 1)
                        scale = chain(dve, s_bn)
                        scale.count[0] = HC
                        scale(nc.vector.reciprocal(bn_scale[:, :], bn_shift[:, :]))
                        scale(nc.vector.tensor_tensor(bn_scale[:, :], bn_scale[:, :], gam, ALU.mult))
                        scale(nc.vector.tensor_tensor(bn_shift[:, :], bnmv[:, :, 0], bn_scale[:, :], ALU.mult))
                        scale(nc.vector.tensor_tensor(bn_shift[:, :], bet, bn_shift[:, :], ALU.subtract))
                        dve.wait_ge(s_w2, 32)
                        dve.wait_ge(s_xl, 16)
                    link(nc.vector.memset(cum[:, 0, :], 0.0))
                    if first:
                        for b in range(B + 2):
                            if b < B:
                                for t in range(b * U, b * U + 3):
                                    residual(t)
                            if b >= 2:
                                places(b - 2)
                            if b < B:
                                for t in range(b * U + 3, (b + 1) * U):
                                    residual(t)
                                variances(b)
                                if b:
                                    choose(b - 1)
                                normalise(b)
                            elif b == B:
                                choose(b - 1)
                    else:
                        def statistics(b):
                            if b < B:
                                for t in range(b * U, (b + 1) * U):
                                    residual(t)
                                variances(b)

                        statistics(0)
                        statistics(1)
                        normalise(0)
                        statistics(2)
                        normalise(1)
                        for b in range(B):
                            choose(b)
                            statistics(b + 3)
                            places(b)
                            if b + 2 < B:
                                normalise(b + 2)

                    dve.wait_ge(s_total, 1)
                    total = psum[0][0:P, 0:E]
                    nc.vector.tensor_tensor(pad_row[0:1, 0:E], total[0:1, :], region_row[0:1, 0:E], ALU.add).then_inc(s_padrow, 1)
                    link(nc.vector.tensor_scalar(cf, total, 127.0, None, ALU.add))
                    link(nc.vector.tensor_copy(ci, cf))
                    link(nc.vector.tensor_scalar(ci, ci, 7, 7, ALU.logical_shift_right, ALU.logical_shift_left))
                    link(nc.vector.tensor_copy(padded, ci))
                    n = 8 if softmax_first else 2
                    nc.vector.tensor_tensor(ex[:, :, 0:n], v8[:, :, 0:n], v8[:, :, 0:1].broadcast_to([P, T, n]), ALU.subtract).then_inc(s_shift, 1)
                    q = padded
                    s = 1
                    while s < E:
                        to = ends[s.bit_length() % 2]
                        nc.vector.tensor_copy(to[:, 0:s], q[:, 0:s]).then_inc(s_own, 1)
                        link.count[0] += 1
                        link(nc.vector.tensor_tensor(to[:, s:E], q[:, s:E], q[:, 0:E - s], ALU.add))
                        q = to
                        s *= 2
                    link(nc.vector.tensor_tensor(base, q, padded, ALU.subtract))
                    link(nc.vector.tensor_tensor(posf, rank, over(base), ALU.add))
                    link(nc.vector.tensor_tensor(picked, sel, posf.unsqueeze(2).broadcast_to([P, T, 2, E]), ALU.mult))
                    link(nc.vector.tensor_reduce(place, picked, AX.X, ALU.add))
                    link(nc.vector.tensor_copy(pos[:, :, :], place))
                    link(nc.vector.tensor_tensor(adj, region_row[0:1, 0:E], base[0:1, :], ALU.subtract))
                    link(nc.vector.tensor_tensor(tcmp, over(q[0:1, :], NT, 1),
                                                 tile_start[:, 0:NT].unsqueeze(2).broadcast_to([1, NT, E]), ALU.is_le))
                    link(nc.vector.tensor_reduce(tcount, tcmp, AX.X, ALU.add))
                    link(nc.vector.tensor_scalar(tile_expert[:, 0:NT], tcount, float(E - 1), None, ALU.min))
                    link(nc.vector.tensor_tensor(tcmp, over(expert_row[0:1, 0:E], NT, 1), tcount.unsqueeze(2).broadcast_to([1, NT, E]), ALU.is_equal))
                    link(nc.vector.tensor_tensor(tcmp, tcmp, over(adj, NT, 1), ALU.mult))
                    link(nc.vector.tensor_scalar(valid, tcount, float(E), None, ALU.is_lt))
                    link(nc.vector.tensor_reduce(tcount, tcmp, AX.X, ALU.add))
                    link(nc.vector.tensor_tensor(tcount, tcount, tile_start[:, 0:NT], ALU.add))
                    link(nc.vector.tensor_tensor(tile_row[:, 0:NT], tcount, valid, ALU.mult))
                    dve.wait_ge(s_ex, 1)
                    if softmax_first:
                        link(nc.vector.tensor_reduce(zs, ex, AX.X, ALU.add))
                        link(nc.vector.reciprocal(zs, zs))
                        link(nc.vector.tensor_tensor(ex[:, :, 0:2], ex[:, :, 0:2], zs.unsqueeze(2).broadcast_to([P, T, 2]), ALU.mult))
                    link(nc.vector.tensor_tensor(zs, ex[:, :, 0], ex[:, :, 1], ALU.add))
                    if softmax_first:
                        link(nc.vector.tensor_scalar(zs, zs, 1e-12, None, ALU.max))
                    link(nc.vector.reciprocal(zs, zs))
                    link(nc.vector.tensor_tensor(wts[:, :, :], ex[:, :, 0:2], zs.unsqueeze(2).broadcast_to([P, T, 2]), ALU.mult))
                    link(nc.vector.tensor_tensor(picked, sel, wts[:, :, :].unsqueeze(3).broadcast_to([P, T, 2, E]), ALU.mult))
                    link(nc.vector.tensor_tensor(comb, picked[:, :, 0, :], picked[:, :, 1, :], ALU.add))

        def experts_stage(layer, E, F, w1, w2, act_fn):
            NT = moe_tiles(E)
            FC = F // 128
            eb = EB0 if layer == 0 else EB1
            w1s, w2s, early = expert_weights(layer, E, F)
            _, _, _, _, tile_expert, tile_row, _ = routing(E)
            G = 8
            S = 4
            assert NT % G == 0 and G % S == 0
            xin = view(work, 0, [S, D])
            xT = view(work, 1024, [S, D])
            hN = view(work, 2048, [2, 512])
            hTt = view(work, 3072, [2, 512])
            s_xi = [sem(f"s_xi{layer}_{w}") for w in range(S)]
            s_yo = [sem(f"s_yo{layer}_{q}") for q in range(2)]
            s_xt = sem(f"s_xt{layer}"); s_xc = sem(f"s_xc{layer}"); s_h = sem(f"s_h{layer}"); s_hc = sem(f"s_hc{layer}")
            s_g = sem(f"s_g{layer}"); s_gc = sem(f"s_gc{layer}"); s_o2 = sem(f"s_o2{layer}"); s_oc = sem(f"s_oc{layer}")
            s_gb = sem("s_gb"); s_w2l = sem(f"s_w2l{layer}"); s_went = sem(f"s_went{layer}"); s_stored = sem(f"s_stored{layer}")
            with nc.Block() as block:
                def groups(eng, body, engine=None):
                    def step(i, more):
                        experts = []
                        if engine is not None:
                            _, experts = nc.values_load_multi_w_load_instructions(
                                tile_expert[0:1, ds(i * G, G)], engines=(engine,), min_val=0, max_val=E - 1)
                        body(i, experts, more)

                    with eng.Fori(0, NT // G - 1) as i:
                        step(i, True)
                    step(NT // G - 1, False)

                @block.sync
                def _(sp):
                    def load(n, slot):
                        row = sp.value_load(tile_row[0:1, ds(n, 1)], min_val=0, max_val=E * REGION - 128)
                        sp.dma_start(xin[:, slot, :], slots_in[ds(row, 128), :]).then_inc(s_xi[slot], 16)

                    for w in range(S):
                        load(w, w)
                    if layer == 1:
                        sp.dma_start(fbet_bc, L1_ffn_beta.partition_broadcast(128)).then_inc(s_gb, 16)
                        sp.dma_start(fgam_bc[:, :], L1_ffn_gamma.partition_broadcast(128)).then_inc(s_gb, 16)
                    for e in range(early, E):
                        sp.dma_start(w2s[:, e * FC * D:(e + 1) * FC * D].rearrange("p (c d) -> p c d", c=FC),
                                     w2[e].rearrange("(c p) d -> p c d", p=128)).then_inc(s_w2l, 16)

                    def body(i, experts, more):
                        for w in range(G):
                            if more or w + S < G:
                                sp.wait_ge(s_xt, i * G + w + 1)
                                sp.sem_inc(s_went, 1)
                                load(i * G + w + S, w % S)
                    groups(sp, body)
                    sp.wait_ge(s_w2l, 16 * (E - early))
                    if layer == 1:
                        sp.wait_ge(s_gb, 32)

                @block.tensor
                def _(pe):
                    def x_transposes(i, w):
                        pe.wait_ge(s_xi[w % S], (i * (G // S) + w // S + 1) * 16)
                        for c in range(DC):
                            at = (w % 2) * D + c * 128
                            last = nc.tensor.transpose(psum[4 + w % S // 2][:, at:at + 128], xin[:, w % S, c * 128:(c + 1) * 128], ident[:, :])
                        last.then_inc(s_xt, 1)

                    pe.sem_inc(s_h, S)
                    pe.sem_inc(s_g, 2)
                    pe.sem_inc(s_o2, 2)
                    for w in range(S):
                        x_transposes(0, w)

                    def body(i, experts, more):
                        def first_product(w):
                            pe.wait_ge(s_xc, i * (G // 2) + w // 2 + 1)
                            pe.wait_ge(s_gc, i * G + w + 1)
                            for c in range(DC):
                                last = nc.tensor.matmul(psum[w % S][:, 0:F], xT[:, w % S, c * 128:(c + 1) * 128],
                                                        w1s[:, ds(experts[w] * (DC * F) + c * F, F)], start=(c == 0), stop=(c == DC - 1))
                            last.then_inc(s_h, 1)

                        def hidden_transposes(w):
                            pe.wait_ge(s_hc, i * G + w + 1)
                            for c in range(FC):
                                last = nc.tensor.transpose(psum[w % S][:, c * 128:(c + 1) * 128], hN[:, w % 2, c * 128:(c + 1) * 128], ident[:, :])
                            last.then_inc(s_g, 1)

                        def second_product(w):
                            pe.wait_ge(s_gc, S + i * G + w + 1)
                            pe.wait_ge(s_oc, i * (G // 2) + w // 2 + 1)
                            for c in range(FC):
                                last = nc.tensor.matmul(psum[6 + w % S // 2][:, (w % 2) * D:(w % 2) * D + D],
                                                        hTt[:, w % 2, c * 128:(c + 1) * 128],
                                                        w2s[:, ds(experts[w] * (FC * D) + c * D, D)], start=(c == 0), stop=(c == FC - 1))
                            last.then_inc(s_o2, 1)

                        first_product(0)
                        first_product(1)
                        hidden_transposes(0)
                        for w in range(G):
                            if w + 2 < G:
                                first_product(w + 2)
                            if w + 1 < G:
                                hidden_transposes(w + 1)
                            if w == 0:
                                pe.wait_ge(s_w2l, 16 * (E - early))
                            second_product(w)
                            if w % 2 == 0 and (more or w + S < G):
                                x_transposes(i, w + S)
                                x_transposes(i, w + S + 1)
                    groups(pe, body, mybir.EngineType.PE)

                @block.scalar
                def _(act):
                    act.sem_inc(s_gc, S)

                    def body(i, experts, more):
                        for w in range(G):
                            act.wait_ge(s_g, 2 + i * G + w + 1)
                            act.wait_ge(s_o2, i * G + w + 1)
                            for c in range(FC):
                                last = nc.scalar.activation(hTt[:, w % 2, c * 128:(c + 1) * 128], psum[w % S][:, c * 128:(c + 1) * 128], act_fn,
                                                            bias=vecs[:, ds(experts[w] * FC + (eb + c), 1)])
                            last.then_inc(s_gc, 1)
                    groups(act, body, mybir.EngineType.Activation)

                @block.vector
                def _(dve):
                    dve.sem_inc(s_oc, 2)
                    if layer == 1:
                        dve.wait_ge(s_gb, 32)
                        nc.vector.tensor_tensor(xres[:, :, :], xres[:, :, :], fbet_bc[0:P, :].unsqueeze(1).broadcast_to([P, T, D]), ALU.add)

                    def xT_copy(i, w):
                        dve.wait_ge(s_xt, i * G + w + 2)
                        dve.wait_ge(s_h, i * G + w + 2)
                        nc.vector.tensor_copy(xT[:, w % S:w % S + 2, :],
                                              psum[4 + w % S // 2][:, :].rearrange("p (w d) -> p w d", w=2)).then_inc(s_xc, 1)

                    for w in range(0, S, 2):
                        xT_copy(0, w)

                    def body(i, experts, more):
                        def hidden_copy(w):
                            dve.wait_ge(s_h, S + i * G + w + 1)
                            dve.wait_ge(s_g, i * G + w + 1)
                            nc.vector.tensor_copy(hN[:, w % 2, 0:F], psum[w % S][:, 0:F]).then_inc(s_hc, 1)

                        def result_copy(q):
                            dve.wait_ge(s_o2, 2 + i * G + 2 * q + 2)
                            dve.wait_ge(s_stored, i * (G // 2) + q + 1)
                            nc.vector.tensor_copy(y_out[:, q % 2, :, :], psum[6 + q % 2][:, :].rearrange("p (w d) -> p w d", w=2)).then_inc(s_oc, 1)

                        hidden_copy(0)
                        hidden_copy(1)
                        for w in range(G):
                            if w + 2 < G:
                                hidden_copy(w + 2)
                            if w % 2:
                                result_copy(w // 2)
                            elif more or w + S < G:
                                xT_copy(i, w + S)
                    groups(dve, body)

                @block.gpsimd
                def _(pool):
                    pool.sem_inc(s_stored, 2)

                    def body(i, experts, more):
                        for q in range(G // 2):
                            pool.wait_ge(s_oc, 2 + i * (G // 2) + q + 1)
                            pool.sem_inc(s_went, 1)
                            pool.dma_start(slots_out[ds((i * (G // 2) + q) * 256, 256), :].rearrange("(w p) d -> p w d", w=2),
                                           y_out[:, q % 2, :, :]).then_inc(s_yo[q % 2], 16)
                            if q:
                                pool.wait_ge(s_yo[(q - 1) % 2], (i * (G // 4) + (q - 1) // 2 + 1) * 16)
                                pool.sem_inc(s_stored, 1)
                        pool.wait_ge(s_yo[1], (i + 1) * (G // 4) * 16)
                        pool.sem_inc(s_stored, 1)
                    groups(pool, body)

        def combine(layer, E, NT, b2):
            NQ = 10
            B = T // U
            first = layer == 0
            ygath = view(arena, 0, [NQ, D], P)
            part = view(arena, NQ * D, [2, D], P)
            b2e = view(work, 0, [D], E)
            combT = view(work, D, [4, P], 16)
            wts, pos, _, comb, _, _, _ = routing(E)
            s_b2 = sem("s_b2"); s_yg = [sem(f"s_yg{n}") for n in range(NQ)]
            s_ct = sem("s_ct"); s_cc = sem("s_cc"); s_bb = sem("s_bb"); s_c = sem("s_c")
            s_st = sem("s_st"); s_var = sem("s_var"); s_sq = sem("s_sq"); s_rs = sem("s_rs")
            s_n = sem("s_n"); s_gain = sem("s_gain"); s_io = sem("s_io")
            s_v = sem("s_v"); s_vt = sem("s_vt"); s_vd = sem("s_vd")
            result = xres if first else tok
            with nc.Block() as block:
                @block.sync
                def _(sp):
                    sp.dma_start(b2e, b2).then_inc(s_b2, 16)
                    if first:
                        sp.dma_start(wraw, L1_gnn_W.rearrange("(o p) i -> p o i", p=128)).then_inc(s_v, 16)
                        sp.dma_start(gb_bc, L1_gnn_b.partition_broadcast(128)).then_inc(s_v, 16)
                        sp.wait_ge(s_v, 32)
                    sp.wait_ge(s_b2, 16)
                    to = (xn_dram if first else out).rearrange("(t p) d -> p t d", p=P)
                    for b in range(B):
                        sp.wait_ge(s_n, (b + 1) * U)
                        sp.dma_start(to[:, b * U:(b + 1) * U, :], tok[:, b * U:(b + 1) * U, :]).then_inc(s_io, 16)
                    sp.wait_ge(s_io, 16 * B)

                @block.gpsimd
                def _(pool):
                    for t in range(T):
                        for k in range(2):
                            n = 2 * t + k
                            if n >= NQ:
                                pool.wait_ge(s_c, (t - NQ // 2) * 2 + k + 1)
                            nc.gpsimd.indirect_dma_start(
                                out=ygath[:, n % NQ, :], out_offset=None, in_=slots_out[0:NT * 128, :],
                                in_offset=bass.IndirectOffsetOnAxis(ap=pos[:, t, k:k + 1], axis=0)).then_inc(s_yg[n % NQ], 16)

                @block.tensor
                def _(pe):
                    if first:
                        pe.wait_ge(s_v, 32)
                        for i in range(2 * DC):
                            for o in range(DC):
                                at = (i % 2) * D + o * 128
                                last = nc.tensor.transpose(psum[6 + i // 2][:, at:at + 128], wraw[:, o, i * 128:(i + 1) * 128], ident[:, :])
                        last.then_inc(s_vt, 1)
                    pe.wait_ge(s_b2, 16)
                    for t in range(T):
                        if t >= 2:
                            pe.wait_ge(s_cc, t - 1)
                        nc.tensor.transpose(psum[t % 2][0:E, 0:P], comb[:, t, :], ident[0:P, 0:P]).then_inc(s_ct, 1)
                        if t >= 4:
                            pe.wait_ge(s_c, (t - 4) * 2 + 1)
                        to = psum[2 + t % 4][0:P, 0:D]
                        nc.tensor.matmul(to, ident[0:P, 0:P], tok[:, t, :], start=True, stop=False)
                        if first:
                            nc.tensor.matmul(to, ident[0:P, 0:P], xres[:, t, :], start=False, stop=False)
                        pe.wait_ge(s_cc, t + 1)
                        nc.tensor.matmul(to, combT[0:E, t % 4, :], b2e, start=False, stop=True).then_inc(s_bb, 1)

                @block.scalar
                def _(act):
                    def copies(b):
                        for t in range(b * U, (b + 1) * U):
                            act.wait_ge(s_ct, t + 1)
                            if t >= 4:
                                act.wait_ge(s_bb, t - 3)
                            nc.scalar.copy(combT[0:E, t % 4, :], psum[t % 2][0:E, 0:P]).then_inc(s_cc, 1)

                    copies(0)
                    for b in range(B):
                        if b + 1 < B:
                            copies(b + 1)
                        act.wait_ge(s_var, (b + 1) * U)
                        nc.scalar.activation(mean_v[:, b * U:(b + 1) * U], mv[:, b * U:(b + 1) * U, 1], ACT.Sqrt,
                                             bias=eps[0:P, :]).then_inc(s_sq, 1)

                @block.vector
                def _(dve):
                    def add_rows(t):
                        for k in range(2):
                            n = 2 * t + k
                            dve.wait_ge(s_yg[n % NQ], 16 * (n // NQ + 1))
                            if k:
                                dve.wait_ge(s_c, 2 * t + 1)
                            else:
                                dve.wait_ge(s_bb, t + 1)
                            nc.vector.scalar_tensor_tensor(result[:, t, :] if k else part[:, t % 2, :], ygath[:, n % NQ, :],
                                                           wts[:, t, k:k + 1], part[:, t % 2, :] if k else psum[2 + t % 4][0:P, 0:D],
                                                           ALU.mult, ALU.add).then_inc(s_c, 1)
                        dve.wait_ge(s_c, 2 * t + 2)
                        nc.vector.bn_stats(st6[:, t, :], result[:, t, :]).then_inc(s_st, 1)
                        dve.wait_ge(s_st, t + 1)
                        nc.vector.bn_aggr(mv[:, t, :], st6[:, t, :]).then_inc(s_var, 1)

                    def normalise(b):
                        dve.wait_ge(s_sq, b + 1)
                        nc.vector.reciprocal(rstd[:, b * U:(b + 1) * U], mean_v[:, b * U:(b + 1) * U]).then_inc(s_rs, 1)
                        dve.wait_ge(s_rs, b + 1)
                        for n, t in enumerate(range(b * U, (b + 1) * U)):
                            if first:
                                nc.vector.tensor_scalar(tok[:, t, :], xres[:, t, :], mv[:, t, 0:1], rstd[:, t:t + 1],
                                                        ALU.subtract, ALU.mult).then_inc(s_n, 1)
                            else:
                                nc.vector.scalar_tensor_tensor(tok[:, t, :], tok[:, t, :], mv[:, t, 0:1], fgam_bc[0:P, :],
                                                               ALU.subtract, ALU.mult).then_inc(s_gain, 1)
                        if not first:
                            for t in range(b * U, (b + 1) * U):
                                dve.wait_ge(s_gain, t + 1)
                                nc.vector.scalar_tensor_tensor(tok[:, t, :], tok[:, t, :], rstd[:, t:t + 1], xres[:, t, :],
                                                               ALU.mult, ALU.add).then_inc(s_n, 1)

                    if first:
                        nc.vector.tensor_scalar(rdegree[:, :], degree[:, :], 1.0, None, ALU.max).then_inc(s_vd, 1)
                        dve.wait_ge(s_vd, 1)
                        nc.vector.reciprocal(rdegree[:, :], rdegree[:, :])
                        dve.wait_ge(s_vt, 1)
                        for i in range(DC):
                            nc.vector.tensor_copy(wT[:, 2 * i:2 * i + 2, :], psum[6 + i][:, :].rearrange("p (i o) -> p i o", i=2))
                    for b in range(B):
                        for t in range(b * U, b * U + 3):
                            add_rows(t)
                        if b:
                            normalise(b - 1)
                        for t in range(b * U + 3, (b + 1) * U):
                            add_rows(t)
                    normalise(B - 1)

        wts_all = sb("wts", [P, T, 2]); pos_all = sb("pos", [P, T, 2], i32); pos_in_all = sb("pos_in", [P, T, 2], i32)
        tile_expert_all = sb("tile_expert", [1, 64], i32); tile_row_all = sb("tile_row", [1, 64], i32)
        pad_row_all = sb("pad_row", [1, 16], i32)

        def routing(E):
            return (wts_all, pos_all, pos_in_all, comb_all[0:P, 0:T * E].rearrange("p (t e) -> p t e", e=E),
                    tile_expert_all, tile_row_all, pad_row_all)

        def expert_weights(layer, E, F):
            if layer == 0:
                return view(arena, 27304, [E * DC * F]), view(arena, 0, [E * (F // 128) * D]), 0
            return view(arena, 0, [E * DC * F]), view(arena, E * DC * F, [E * (F // 128) * D]), 10

        end_stage()
        first_graph(True)
        end_stage()
        first_graph(False)
        end_stage()
        dispatch(0, E0, F0, L0_ffn_w1, L0_ffn_w2, True)
        end_stage()
        experts_stage(0, E0, F0, L0_ffn_w1, L0_ffn_w2, ACT.Gelu)
        end_stage()
        combine(0, E0, moe_tiles(E0), L0_ffn_b2)
        end_stage()
        graph(1)
        end_stage()
        dispatch(1, E1, F1, L1_ffn_w1, L1_ffn_w2, False)
        end_stage()
        experts_stage(1, E1, F1, L1_ffn_w1, L1_ffn_w2, ACT.Relu)
        end_stage()
        combine(1, E1, moe_tiles(E1), L1_ffn_b2)
        end_stage()


_INS = ['x', 'src', 'dst', 'edge_weight', 'L0_gnn_W1', 'L0_gnn_b1', 'L0_gnn_gamma', 'L0_gnn_beta', 'L0_gnn_W2', 'L0_gnn_b2',
        'L0_ffn_router_w', 'L0_ffn_w1', 'L0_ffn_b1', 'L0_ffn_w2', 'L0_ffn_b2', 'L1_gnn_W', 'L1_gnn_b', 'L1_ffn_gate_w',
        'L1_ffn_gate_b', 'L1_ffn_w1', 'L1_ffn_b1', 'L1_ffn_w2', 'L1_ffn_b2', 'L1_ffn_gamma', 'L1_ffn_beta']


def kernel(**inputs):
    import numpy as _np
    import concourse.bacc as _bacc
    from concourse import mybir as _mybir
    from concourse.bass_utils import run_bass_kernel_spmd as _run

    nc = _bacc.Bacc("TRN2", target_bir_lowering=False, num_devices=1)
    arrays, args = {}, []
    for name in _INS:
        a = _np.ascontiguousarray(inputs[name])
        arrays[f"in_{name}_dram"] = a
        args.append(nc.dram_tensor(f"in_{name}_dram", a.shape, _mybir.dt.from_np(a.dtype), kind="ExternalInput").ap())
    args.append(nc.dram_tensor("out_0_dram", (N, D), _mybir.dt.float32, kind="ExternalOutput").ap())
    gnn_moe(nc, *args)
    r = _run(nc, [arrays], core_ids=[0])
    return r.results[0]["out_0_dram"]
```

```python
import concourse.bass as bass
from concourse import mybir
from contextlib import ExitStack

fp32 = mybir.dt.float32
fp16 = mybir.dt.float16
i32 = mybir.dt.int32
u32 = mybir.dt.uint32
ALU = mybir.AluOpType
ACT = mybir.ActivationFunctionType
AX = mybir.AxisListType
ds = bass.ds

N = 3125
D = 256
NE = 53125
P = 125
T = N // P
DC = D // 128
HID = 1024
HC = HID // 128
KS = 18
WIN = KS * 128
GROUP = 6
GROUPS = KS // GROUP
ROUNDS = -(-NE // WIN)
NE_PAD = 25 * WIN
NE_LEN = NE_PAD + ROUNDS * WIN
NO_NODE = 1 << 20
REGION = -(-N // 128) * 128 + 128
U = 5
LN_EPS = 1e-5
SUB = 25
SUBS = P // SUB
SUB_TILES = 4
DENSE = (1, 3)
HALF = (0, 13, T)
BUILD = (3, 6, 7)
GROUP_TILES = 8


def tail_tiles(experts):
    usual = 2 * N // 128 + experts // 2
    return min((4, 8), key=lambda tail: -(-(usual + 1 - tail) // GROUP_TILES) * GROUP_TILES + tail)


def moe_tiles(experts):
    most = (2 * N - experts) // 128 + experts
    tail = tail_tiles(experts)
    return -(-(most - tail) // GROUP_TILES) * GROUP_TILES + tail


def gnn_moe(nc, x, src, dst, edge_weight, L0_gnn_W1, L0_gnn_b1, L0_gnn_gamma, L0_gnn_beta, L0_gnn_W2,
            L0_gnn_b2, L0_ffn_router_w, L0_ffn_w1, L0_ffn_b1, L0_ffn_w2, L0_ffn_b2, L1_gnn_W, L1_gnn_b,
            L1_ffn_gate_w, L1_ffn_gate_b, L1_ffn_w1, L1_ffn_b1, L1_ffn_w2, L1_ffn_b2, L1_ffn_gamma,
            L1_ffn_beta, out):
    E0, E1 = L0_ffn_w1.shape[0], L1_ffn_w1.shape[0]
    F0, F1 = L0_ffn_w1.shape[2], L1_ffn_w1.shape[2]
    MOST_TILES = max(moe_tiles(E0), moe_tiles(E1))
    SLOTS = 128 * MOST_TILES

    ctx = ExitStack()
    with ctx:
        def sb(name, shape, dt=fp32):
            return ctx.enter_context(nc.sbuf_tensor(name, shape, dt))

        stage_sems = []
        stage = [0]

        def sem(name):
            s = nc.alloc_semaphore(f"{name}_{stage[0]}")
            stage_sems.append(s)
            return s

        def end_stage():
            nc.clear_and_free_semaphores(list(stage_sems))
            stage_sems.clear()
            stage[0] += 1
            nc.all_engine_barrier()

        def dram(name, shape, dt=fp32):
            return nc.dram_tensor(name, shape, dt, kind="Internal").ap()

        src_pad = dram("src_pad", [NE_LEN], i32)
        dst_pad = dram("dst_pad", [NE_LEN], i32)
        ew_pad = dram("ew_pad", [NE_LEN])
        xn16_dram = dram("xn16_dram", [N, 2 * D], fp16)
        xn_dram = dram("xn_dram", [N, D])
        slots_in = dram("slots_in", [max(E0, E1) * REGION, D])
        slots_out = dram("slots_out", [SLOTS, D])

        xres = sb("xres", [P, T, D])
        tok = sb("tok", [P, T, D])
        arena = sb("arena", [128, 32768])
        work = sb("work", [128, 4096])

        def view(t, at, dims, parts=128, half=False):
            size = 1
            for d in dims:
                size *= d
            flat = t[0:parts, at:at + size // 2].bitcast(fp16) if half else t[0:parts, at:at + size]
            names = "abcd"[:len(dims)]
            if len(dims) == 1:
                return flat
            return flat.rearrange(f"p ({' '.join(names)}) -> p {' '.join(names)}",
                                  **{n: d for n, d in zip(names, dims)})

        h1T = view(arena, 0, [HC, N])
        ROWS = HC * N
        rows = view(arena, ROWS, [KS, D])
        masks = view(arena, ROWS + KS * D, [KS, P])
        rows16 = view(arena, ROWS, [KS, 2 * D + 2], half=True)
        masks16 = view(arena, ROWS + KS * (D + 1), [9, P + 1], half=True)[:, :, 0:P]
        MATRIX = ROWS + KS * (D + 1) + 9 * (P + 1) // 2
        adjacency = view(arena, MATRIX, [T, P + 1], P, half=True)[:, :, 0:P]
        col_hot = view(arena, MATRIX + T * (P + 1) // 2, [3, T * SUB + 1], half=True)[:, :, 0:T * SUB]
        x16 = xres[:, :, :].bitcast(fp16)
        x3 = view(arena, 16384, [T, D], P)
        w1g = view(work, 0, [DC, HID])
        bn6 = view(work, 2048, [HC, T, 6])
        hT = view(work, 3248, [2 * DC, P])
        w2g = view(arena, ROWS, [HC, D])
        b2g_bc = view(arena, ROWS + HC * D, [D])
        gb_bc = view(work, 2304, [D])
        wT = view(arena, 16384 + T * D, [2 * DC, D])
        wraw = view(arena, ROWS, [DC, 2 * D])

        ident = sb("ident", [128, 128])
        ones = sb("ones", [128, 128])
        before = sb("before", [P, P])
        node_row = sb("node_row", [128, P])
        node_base = sb("node_base", [128, T])
        expert_row = sb("expert_row", [128, 16])
        region_row = sb("region_row", [128, 16])
        nibble_row = sb("nibble_row", [1, MOST_TILES])
        zero_rows = sb("zero_rows", [128, D])
        row_hot = view(zero_rows, 0, [4, P + 1], half=True)[:, :, 0:P]
        comb_all = sb("comb_all", [128, T * 16])
        col_row = view(comb_all, 0, [T * SUB + 1], half=True)[:, 0:T * SUB]
        sub_base = sb("sub_base", [128, SUBS])
        dense_meta = sb("dense_meta", [128, len(DENSE), 2, SUBS, SUB_TILES], i32)
        dense_starts = sb("dense_starts", [1, (T // U) * len(DENSE) * SUBS], i32)
        fgam_bc = zero_rows
        tile_start = sb("tile_start", [1, MOST_TILES])
        eps = sb("eps", [128, 1])
        pad_i = view(arena, 5120, [179], 25).bitcast(i32)
        pad_z = view(arena, 5376, [179], 25)
        shared = sb("shared", [128, 4 * D])
        meta_src = view(shared, 0, [U, KS]).bitcast(i32)
        meta_dst = view(shared, U * KS, [U, KS]).bitcast(i32)
        meta_ew = view(shared, 2 * U * KS, [U, KS])
        dst_local = view(shared, 3 * U * KS, [U, KS])
        summed = view(shared, 4 * U * KS, [2, D + 1], P)
        CALC = 4 * U * KS + 2 * (D + 1)
        LIST = SUBS * SUB_TILES
        meta_f = view(shared, CALC, [2, SUBS, SUB_TILES])
        beyond = meta_f[:, 1, :, :]
        block_of = view(shared, CALC + 2 * LIST, [SUBS, SUB_TILES])
        row_of, col_of = ([view(shared, CALC + (i + k) * LIST, [SUBS, SUB_TILES]) for k in range(2)] for i in (3, 5))
        y_out = view(shared, 0, [2, 2, D])
        fbet_bc = view(shared, 0, [D])
        NL = (T // U) * len(DENSE) * SUBS
        table = view(arena, 7424, [T + 2 + NL], 1)
        gaps = view(arena, 7552, [T + NL], 1)
        scal = sb("scal", [1, 4])
        starts = sb("starts", [1, T + 2], i32)
        rounds = sb("rounds", [1, 3], i32)
        degree = sb("degree", [P, T])
        rdegree = sb("rdegree", [P, T])
        mean_v = sb("mean_v", [P, T])
        mv = sb("mv", [P, T, 2])
        st6 = sb("st6", [P, T, 6])
        rstd = sb("rstd", [P, T])
        bnmv = sb("bnmv", [128, HC, 2])
        bn_scale = sb("bn_scale", [128, HC])
        bn_shift = sb("bn_shift", [128, HC])
        VROWS = 3 * HC + E0 * F0 // 128 + E1 * F1 // 128
        vec_rows = view(arena, 4352, [128], VROWS)
        vecs = sb("vecs", [128, VROWS])
        b1g, gam, bet = (vecs[:, i * HC:(i + 1) * HC] for i in range(3))
        EB0, EB1 = 3 * HC, 3 * HC + E0 * F0 // 128
        gateb_bc = sb("gateb_bc", [128, E1])
        router = view(arena, 4608, [D], E0)
        gateT = [sb("gateT0", [128, DC, E0]), sb("gateT1", [128, DC, E1])]
        g_col = sb("g_col", [128, DC])
        i_first = sb("i_first", [1, 1], i32)

        psum = [ctx.enter_context(nc.psum_tensor(f"bank{i}", [128, 512], fp32)) for i in range(8)]

        s_x = sem("s_x"); s_w = sem("s_w"); s_const = sem("s_const"); s_pad = sem("s_pad")
        s_dst = sem("s_dst"); s_tr = sem("s_tr"); s_dve = sem("s_dve"); s_cnt = sem("s_cnt")
        s_wg = sem("s_wg"); s_next = sem("s_next"); s_dstb = sem("s_dstb")
        s_st = sem("s_st"); s_var = sem("s_var"); s_sq = sem("s_sq"); s_n = sem("s_n"); s_xn = sem("s_xn")
        s_hi = sem("s_hi"); s_rs = sem("s_rs"); s_lo = sem("s_lo")

        def chain(eng, s):
            n = [0]

            def link(ins):
                n[0] += 1
                ins.then_inc(s, 1)
                eng.wait_ge(s, n[0])
            link.count = n
            return link

        dst_a = view(arena, 2048, [NE // P], P).bitcast(i32)
        dst_b = view(arena, 2560, [NE // P], P).bitcast(i32)
        dst_f = view(arena, 3072, [NE // P], P)
        lt = view(arena, 6144, [2, NE // P], P)
        cols = view(arena, 4096, [T + 2 + NL], P)
        dst_16 = view(arena, 7680, [NE // P + 1], P, half=True)[:, 0:NE // P]
        lt16 = view(arena, 7936, [2, NE // P + 1], P, half=True)[:, :, 0:NE // P]

        with nc.Block() as block:
            @block.sync
            def _(sp):
                sp.dma_start(dst_a, dst.rearrange("(p c) -> p c", p=P)).then_inc(s_dst, 16)
                sp.wait_ge(s_next, 1)
                sp.dma_start(dst_b[0:P - 1, :], dst[1:1 + (P - 1) * (NE // P)].rearrange("(p c) -> p c", p=P - 1)).then_inc(s_dstb, 16)
                sp.dma_start(dst_b[P - 1:P, 0:NE // P - 1], dst[1 + (P - 1) * (NE // P):NE].rearrange("(p c) -> p c", p=1)).then_inc(s_dstb, 16)
                sp.dma_start(xres[:, :, :], x.rearrange("(t p) d -> p t d", p=P)).then_inc(s_x, 16)
                sp.dma_start(dst_pad[0:NE].rearrange("(p c) -> p c", p=P), dst.rearrange("(p c) -> p c", p=P)).then_inc(s_pad, 16)
                sp.dma_start(src_pad[0:NE].rearrange("(p c) -> p c", p=P), src.rearrange("(p c) -> p c", p=P)).then_inc(s_pad, 16)
                sp.dma_start(ew_pad[0:NE].rearrange("(p c) -> p c", p=P), edge_weight.rearrange("(p c) -> p c", p=P)).then_inc(s_pad, 16)
                sp.wait_ge(s_const, 2)
                tail = lambda a: a[NE:NE_PAD].rearrange("(p c) -> p c", p=25)
                sp.dma_start(tail(dst_pad), pad_i[:, :]).then_inc(s_pad, 16)
                sp.dma_start(tail(src_pad), pad_z[:, :].bitcast(i32)).then_inc(s_pad, 16)
                sp.dma_start(tail(ew_pad), pad_z[:, :]).then_inc(s_pad, 16)
                xn_rows = xn16_dram.rearrange("(t p) d -> p t d", p=P)
                for b in range(T // U):
                    sp.wait_ge(s_lo, (b + 1) * U)
                    sp.dma_start(xn_rows[:, b * U:(b + 1) * U, :], x16[:, b * U:(b + 1) * U, :]).then_inc(s_xn, 16)
                sp.wait_ge(s_pad, 16 * 6)
                sp.wait_ge(s_xn, 16 * (T // U))

            @block.scalar
            def _(act):
                act.dma_start(vec_rows[0:HC, :], L0_gnn_b1.rearrange("(m p) -> m p", p=128)).then_inc(s_w, 16)
                act.dma_start(vec_rows[HC:2 * HC, :], L0_gnn_gamma.rearrange("(m p) -> m p", p=128)).then_inc(s_w, 16)
                act.dma_start(vec_rows[2 * HC:3 * HC, :], L0_gnn_beta.rearrange("(m p) -> m p", p=128)).then_inc(s_w, 16)
                act.dma_start(vec_rows[EB0:EB1, :], L0_ffn_b1.rearrange("e (c p) -> (e c) p", p=128)).then_inc(s_w, 16)
                act.dma_start(vec_rows[EB1:VROWS, :], L1_ffn_b1.rearrange("e (c p) -> (e c) p", p=128)).then_inc(s_w, 16)
                act.dma_start(router[:, :], L0_ffn_router_w).then_inc(s_w, 16)
                act.dma_start(w1g, L0_gnn_W1.rearrange("(c p) h -> p c h", p=128)).then_inc(s_wg, 16)
                act.dma_start(gateT[1][:, :, :], L1_ffn_gate_w.rearrange("(c p) e -> p c e", p=128)).then_inc(s_wg, 16)
                act.dma_start(gateb_bc[:, :], L1_ffn_gate_b.partition_broadcast(128)).then_inc(s_wg, 16)
                act.dma_start(i_first[:, :], src[0:1].rearrange("(a n) -> a n", a=1)).then_inc(s_wg, 16)
                act.wait_ge(s_var, T)
                nc.scalar.activation(mean_v[:, :], mv[:, :, 1], ACT.Sqrt, bias=eps[0:P, :]).then_inc(s_sq, 1)
                for t in range(T):
                    act.wait_ge(s_n, t + 1)
                    nc.scalar.copy(x16[:, t, 0:D], tok[:, t, :]).then_inc(s_hi, 1)
                act.wait_ge(s_wg, 16 * 4)

            @block.gpsimd
            def _(pool):
                pool.memset(dst_b, NO_NODE).then_inc(s_next, 1)
                pool.memset(pad_i[:, :], NO_NODE).then_inc(s_const, 1)
                pool.memset(pad_z[:, :], 0.0).then_inc(s_const, 1)
                pool.memset(ident[:, :], 0.0).then_inc(s_const, 1)
                pool.memset(ones[:, :], 1.0).then_inc(s_const, 1)
                pool.memset(before[:, :], 1.0).then_inc(s_const, 1)
                pool.memset(eps[:, :], LN_EPS).then_inc(s_const, 1)
                pool.iota(node_row[:, :], [[1, P]], base=0, channel_multiplier=0,
                          allow_small_or_imprecise_dtypes=True).then_inc(s_const, 1)
                pool.iota(node_base[:, :], [[P, T]], base=0, channel_multiplier=0,
                          allow_small_or_imprecise_dtypes=True).then_inc(s_const, 1)
                pool.iota(expert_row[:, :], [[1, 16]], base=0, channel_multiplier=0,
                          allow_small_or_imprecise_dtypes=True).then_inc(s_const, 1)
                pool.iota(region_row[:, :], [[REGION, 16]], base=0, channel_multiplier=0,
                          allow_small_or_imprecise_dtypes=True).then_inc(s_const, 1)
                pool.iota(tile_start[:, :], [[128, MOST_TILES]], base=0, channel_multiplier=0,
                          allow_small_or_imprecise_dtypes=True).then_inc(s_const, 1)
                pool.memset(degree[:, :], 0.0).then_inc(s_const, 1)
                for k in range(4):
                    pool.memset(nibble_row.rearrange("p (n k) -> p n k", k=4)[:, :, k], float(16 ** k)).then_inc(s_const, 1)
                pool.iota(col_row, [[1, T * SUB]], base=0, channel_multiplier=0,
                          allow_small_or_imprecise_dtypes=True).then_inc(s_const, 1)
                pool.iota(sub_base[:, :], [[SUB, SUBS]], base=0, channel_multiplier=0,
                          allow_small_or_imprecise_dtypes=True).then_inc(s_const, 1)
                pool.wait_ge(s_const, 18)
                pool.affine_select(out=ident[:, :], in_=ident[:, :], compare_op=ALU.not_equal, fill=1.0,
                                   base=0, pattern=[[-1, 128]], channel_multiplier=1).then_inc(s_const, 1)
                pool.affine_select(out=before[:, :], in_=before[:, :], compare_op=ALU.is_gt, fill=0.0,
                                   base=0, pattern=[[1, P]], channel_multiplier=-1).then_inc(s_const, 1)
                for t in range(T):
                    pool.wait_ge(s_hi, t + 1)
                    pool.tensor_tensor(x16[:, t, D:2 * D], tok[:, t, :], x16[:, t, 0:D], ALU.subtract).then_inc(s_lo, 1)

            @block.tensor
            def _(pe):
                pe.wait_ge(s_const, 20)
                pe.wait_ge(s_w, 16 * 6)
                nc.tensor.transpose(psum[0][:, 0:VROWS], vec_rows[:, :], ident[0:VROWS, 0:VROWS])
                for c in range(DC):
                    last = nc.tensor.transpose(psum[1][:, c * E0:(c + 1) * E0], router[:, c * 128:(c + 1) * 128], ident[0:E0, 0:E0])
                last.then_inc(s_tr, 1)
                pe.wait_ge(s_cnt, 1)
                nc.tensor.matmul(psum[4][0:1, 0:T + 2 + NL], ones[0:P, 0:1], cols, start=True, stop=True).then_inc(s_tr, 1)

            @block.vector
            def _(dve):
                link = chain(dve, s_dve)
                dve.wait_ge(s_const, 20)
                link(nc.vector.memset(cols, 0.0))
                dve.wait_ge(s_dst, 16)
                link(nc.vector.tensor_copy(dst_f, dst_a))
                link(nc.vector.tensor_scalar(dst_16, dst_f, float(N // 2), None, ALU.subtract))
                firsts = {t: t * P for t in range(1, T)}
                for i in range(NL):
                    b, w, k = i // (len(DENSE) * SUBS), DENSE[i // SUBS % len(DENSE)], i % SUBS
                    if k:
                        firsts[T + 2 + i] = (b * U + w) * P + k * SUB
                for n, (column, node) in enumerate(firsts.items()):
                    dve.wait_ge(s_dve, max(link.count[0] - 1, 3))
                    nc.vector.tensor_scalar(lt16[:, n % 2, :], dst_16, float(node - N // 2), 0.0, ALU.is_lt, ALU.add,
                                            accum_out=cols[:, column:column + 1]).then_inc(s_dve, 1)
                    link.count[0] += 1
                dve.wait_ge(s_dstb, 32)
                dve.wait_ge(s_dve, link.count[0])
                link(nc.vector.tensor_copy(lt[:, 0, :], dst_b))
                link(nc.vector.tensor_tensor(lt[:, 1, :], lt[:, 0, :], dst_f, ALU.is_lt))
                nc.vector.tensor_reduce(cols[:, T + 1:T + 2], lt[:, 1, :], AX.X, ALU.add).then_inc(s_cnt, 1)
                dve.wait_ge(s_x, 16)
                for t in range(T):
                    nc.vector.bn_stats(st6[:, t, :], xres[:, t, :]).then_inc(s_st, 1)
                for t in range(T):
                    dve.wait_ge(s_st, t + 1)
                    nc.vector.bn_aggr(mv[:, t, :], st6[:, t, :]).then_inc(s_var, 1)
                dve.wait_ge(s_sq, 1)
                nc.vector.reciprocal(rstd[:, :], mean_v[:, :]).then_inc(s_rs, 1)
                dve.wait_ge(s_rs, 1)
                for t in range(T):
                    nc.vector.tensor_scalar(tok[:, t, :], xres[:, t, :], mv[:, t, 0:1], rstd[:, t:t + 1],
                                            ALU.subtract, ALU.mult).then_inc(s_n, 1)
                dve.wait_ge(s_tr, 2)
                nc.vector.tensor_copy(vecs[:, :], psum[0][:, 0:VROWS])
                nc.vector.tensor_copy(gateT[0][:, :, :], psum[1][:, 0:DC * E0].rearrange("p (c e) -> p c e", c=DC))
                link(nc.vector.tensor_copy(table, psum[4][0:1, 0:T + 2 + NL]))
                lists = table[:, T + 2:T + 2 + NL].rearrange("p (b w k) -> p b w k", b=T // U, k=SUBS)
                list_gaps = gaps[:, T:T + NL].rearrange("p (b w k) -> p b w k", b=T // U, k=SUBS)
                for w in range(len(DENSE)):
                    link(nc.vector.tensor_copy(lists[:, :, w, 0], table[:, 0:T].rearrange("p (b w) -> p b w", w=U)[:, :, DENSE[w]]))
                link(nc.vector.memset(table[:, T:T + 1], float(NE)))
                link(nc.vector.tensor_tensor(gaps[:, 0:T], table[:, 1:T + 1], table[:, 0:T], ALU.subtract))
                for w in range(len(DENSE)):
                    link(nc.vector.tensor_tensor(list_gaps[:, :, w, 0:SUBS - 1], lists[:, :, w, 1:SUBS], lists[:, :, w, 0:SUBS - 1], ALU.subtract))
                    nexts = table[:, 1:T + 1].rearrange("p (b w) -> p b w", w=U)[:, :, DENSE[w]]
                    link(nc.vector.tensor_tensor(list_gaps[:, :, w, SUBS - 1], nexts, lists[:, :, w, SUBS - 1], ALU.subtract))
                link(nc.vector.tensor_reduce(scal[:, 0:1], gaps[:, 0:T], AX.X, ALU.max))
                link(nc.vector.tensor_scalar(scal[:, 0:1], scal[:, 0:1], float(WIN), None, ALU.is_gt))
                link(nc.vector.tensor_scalar(scal[:, 1:2], table[:, T + 1:T + 2], 0.0, None, ALU.is_gt))
                link(nc.vector.tensor_reduce(scal[:, 2:3], gaps[:, T:T + NL], AX.X, ALU.max))
                link(nc.vector.tensor_scalar(scal[:, 2:3], scal[:, 2:3], float(SUB_TILES * 128), None, ALU.is_gt))
                link(nc.vector.tensor_tensor(scal[:, 0:1], scal[:, 0:1], scal[:, 1:2], ALU.max))
                link(nc.vector.tensor_tensor(scal[:, 2:3], scal[:, 0:1], scal[:, 2:3], ALU.max))
                link(nc.vector.tensor_scalar(rounds[:, 0:1], scal[:, 2:3], float(ROUNDS - 1), 1.0, ALU.mult, ALU.add))
                link(nc.vector.tensor_scalar(scal[:, 3:4], scal[:, 2:3], -1.0, 1.0, ALU.mult, ALU.add))
                link(nc.vector.tensor_copy(rounds[:, 1:2], scal[:, 3:4]))
                link(nc.vector.tensor_scalar(rounds[:, 2:3], scal[:, 2:3], float(ROUNDS), None, ALU.mult))
                link(nc.vector.tensor_scalar(starts[:, :], table[:, 0:T + 2], scal[:, 3:4], None, ALU.mult))
                link(nc.vector.tensor_copy(dense_starts[:, :], table[:, T + 2:T + 2 + NL]))

        def first_graph(dense):
            kinds = "".join("D" if dense and w in DENSE else "G" for w in range(U))
            assert DENSE == (1, 3) and U == 5
            G_SLOT = [kinds[:w].count("G") for w in range(U)]
            D_SLOT = [kinds[:w].count("D") for w in range(U)]
            NG, ND = kinds.count("G"), kinds.count("D")
            GROUP = 3
            KG = KS // GROUP
            RING = 3
            s_meta = [sem(f"s_meta{w}") for w in range(U)]
            s_row = [sem(f"s_row{j}") for j in range(KS)]
            s_local = sem("s_local"); s_mask = sem("s_mask"); s_used = sem("s_used"); s_sum = sem("s_sum")
            s_kept = sem("s_kept"); s_t = sem("s_t"); s_ht = sem("s_ht"); s_proj = sem("s_proj"); s_post = sem("s_post")
            s_one = sem("s_one"); s_went = sem("s_went"); s_went_sp = sem("s_went_sp")
            s_calc = sem("s_calc"); s_taken = sem("s_taken"); s_hot = sem("s_hot"); s_tile = sem("s_tile")
            s_evac = sem("s_evac"); s_dense = sem("s_dense")
            FREE = NG * KG
            TILES = 4
            HALVES = 3
            with nc.Block() as block:
                def windows(eng, body):
                    n = eng.value_load(rounds[0:1, 1:2] if dense else rounds[0:1, 2:3], min_val=0, max_val=1 if dense else ROUNDS)
                    with eng.If(n > 0):
                        with eng.Fori(0, n) as r:
                            with eng.Fori(0, T // U) as b:
                                body(r, b, r * (T // U) + b)

                @block.sync
                def _(sp):
                    def body(r, b, rb):
                        for w in range(U):
                            t = b * U + w
                            if kinds[w] == "G":
                                sp.wait_ge(s_used, (rb * NG + G_SLOT[w] + 1) * KG)
                                sp.sem_inc(s_went_sp, 1)
                                at = sp.value_load(starts[0:1, ds(t, 1)], min_val=0, max_val=NE)
                                if not dense:
                                    at = sp.snap(at + r * WIN)
                                for to, frm in ((meta_src, src_pad), (meta_dst, dst_pad)):
                                    sp.dma_start(to[:, w, :], frm[ds(at, WIN)].rearrange("(p j) -> p j", j=KS)).then_inc(s_meta[w], 16)
                            else:
                                sp.wait_ge(s_taken, rb * ND + D_SLOT[w] + 1)
                                sp.sem_inc(s_went_sp, 1)
                                for s in range(SUBS):
                                    at = sp.value_load(dense_starts[0:1, ds((b * ND + D_SLOT[w]) * SUBS + s, 1)], min_val=0, max_val=NE)
                                    for i, frm in enumerate((src_pad, dst_pad)):
                                        sp.dma_start(dense_meta[:, D_SLOT[w], i, s, :],
                                                     frm[ds(at, SUB_TILES * 128)].rearrange("(p j) -> p j", j=SUB_TILES)).then_inc(s_meta[w], 16)
                    windows(sp, body)

                @block.gpsimd
                def _(pool):
                    nc.gpsimd.memset(rows16[:, :, 2 * D:2 * D + 1], 1.0).then_inc(s_one, 1)

                    def body(r, b, rb):
                        for w in range(U):
                            if kinds[w] == "G":
                                x = rb * NG + G_SLOT[w]
                                pool.wait_ge(s_meta[w], (rb + 1) * 32)
                                pool.sem_inc(s_went, 1)
                                for j in range(KS):
                                    if j % GROUP == 0:
                                        pool.wait_ge(s_used, FREE + (x - 1) * KG + j // GROUP + 1)
                                        pool.sem_inc(s_went, 1)
                                    nc.gpsimd.indirect_dma_start(
                                        out=rows16[:, j, 0:2 * D], out_offset=None, in_=xn16_dram[:, :],
                                        in_offset=bass.IndirectOffsetOnAxis(ap=meta_src[:, w, j:j + 1], axis=0)).then_inc(s_row[j], 16)
                    windows(pool, body)

                @block.vector
                def _(dve):
                    dve.sem_inc(s_sum, 1)
                    dve.sem_inc(s_post, 1)
                    if dense:
                        dve.sem_inc(s_taken, ND)

                    def body(r, b, rb):
                        def masks(w, q):
                            x = rb * NG + G_SLOT[w]
                            if q == 0:
                                dve.wait_ge(s_meta[w], (rb + 1) * 32)
                                nc.vector.tensor_scalar(dst_local[:, w, :], meta_dst[:, w, :], node_base[:, ds(b * U + w, 1)], None,
                                                        ALU.subtract).then_inc(s_local, 1)
                                dve.wait_ge(s_local, x + 1)
                            dve.wait_ge(s_used, FREE + x * KG + q - RING + 1)
                            for j in range(q * GROUP, (q + 1) * GROUP):
                                m = nc.vector.tensor_scalar(masks16[:, j % (RING * GROUP), :], col_row[:, 0:P],
                                                            dst_local[:, w, j:j + 1], None, ALU.is_equal)
                            m.then_inc(s_mask, 1)

                        def columns(w):
                            d = rb * ND + D_SLOT[w]
                            n = [0]

                            def link(ins):
                                n[0] += 1
                                ins.then_inc(s_calc, 1)
                                dve.wait_ge(s_calc, d * 8 + n[0])
                            dve.wait_ge(s_meta[w], (rb + 1) * 16 * 2 * SUBS)
                            nc.vector.tensor_copy(meta_f, dense_meta[:, D_SLOT[w], :, :, :]).then_inc(s_taken, 1)
                            dve.wait_ge(s_taken, ND + d + 1)
                            link(nc.vector.tensor_scalar(block_of, meta_f[:, 0, :, :], 1.0 / P, -(P // 2) / P, ALU.mult, ALU.add))
                            link(nc.vector.tensor_scalar(block_of, block_of, float(3 << 22), None, ALU.add))
                            link(nc.vector.tensor_scalar(block_of, block_of, float(3 << 22), None, ALU.subtract))
                            link(nc.vector.scalar_tensor_tensor(row_of[D_SLOT[w]], block_of, -float(P), meta_f[:, 0, :, :], ALU.mult, ALU.add))
                            link(nc.vector.scalar_tensor_tensor(col_of[D_SLOT[w]], meta_f[:, 1, :, :], node_base[:, ds(b * U + w, 1)],
                                                                sub_base[:, :].unsqueeze(2).broadcast_to([128, SUBS, SUB_TILES]),
                                                                ALU.subtract, ALU.subtract))
                            link(nc.vector.tensor_scalar(beyond, col_of[D_SLOT[w]], float(SUB), float(1 << 16), ALU.is_ge, ALU.mult))
                            link(nc.vector.scalar_tensor_tensor(col_of[D_SLOT[w]], block_of, float(SUB), col_of[D_SLOT[w]], ALU.mult, ALU.add))
                            link(nc.vector.tensor_tensor(col_of[D_SLOT[w]], col_of[D_SLOT[w]], beyond, ALU.add))

                        def hots(w, lo, hi):
                            d = rb * ND + D_SLOT[w]
                            for k in range(lo, hi):
                                dve.wait_ge(s_tile, TILES + d * (SUBS * SUB_TILES) + (k - 2 if k >= 3 else 0))
                                at = (slice(None), k // SUB_TILES, slice(k % SUB_TILES, k % SUB_TILES + 1))
                                nc.vector.tensor_scalar(row_hot[:, k % 4, :], col_row[:, 0:P], row_of[D_SLOT[w]][at], None, ALU.is_equal)
                                nc.vector.tensor_scalar(col_hot[:, k % 3, :], col_row[:, :], col_of[D_SLOT[w]][at], None, ALU.is_equal).then_inc(s_hot, 1)

                        def add(w):
                            g = rb * U + w
                            acc = psum[w % 2]
                            if kinds[w] == "G":
                                dve.wait_ge(s_used, FREE + (rb * NG + G_SLOT[w] + 1) * KG)
                            else:
                                dve.wait_ge(s_dense, rb * ND + D_SLOT[w] + 1)
                            last_use = g - 1 if w else g
                            if not dense:
                                dve.wait_ge(s_kept, 1 + last_use)
                            dve.wait_ge(s_t, 1 + last_use)
                            nc.vector.tensor_tensor(summed[:, w % 2, 0:D], acc[0:P, 0:D], tok[:, ds(b * U + w, 1), :],
                                                    ALU.add).then_inc(s_sum, 1)
                            nc.vector.tensor_tensor(degree[:, ds(b * U + w, 1)], acc[0:P, D:D + 1], degree[:, ds(b * U + w, 1)],
                                                    ALU.add).then_inc(s_sum, 1)

                        def bias(w, halves=(0, 1)):
                            g = rb * U + w
                            for q in halves:
                                dve.wait_ge(s_proj, 2 * g + q + 1)
                                nc.vector.tensor_tensor(
                                    h1T[:, 4 * q:4 * q + 4, ds((b * U + w) * P, P)],
                                    psum[4 + q][:, 0:4 * P].rearrange("p (m n) -> p m n", m=4),
                                    b1g[:, 4 * q:4 * q + 4].unsqueeze(2).broadcast_to([128, 4, P]), ALU.add).then_inc(s_post, 1)

                        def statistics(w, halves=(0, 1)):
                            for q in halves:
                                dve.wait_ge(s_post, 1 + 2 * (rb * U + w) + q + 1)
                                for m in range(4 * q, 4 * q + 4):
                                    nc.vector.bn_stats(bn6[:, m, ds(b * U + w, 1), :], h1T[:, m, ds((b * U + w) * P, P)])

                        if not dense:
                            for w in range(U):
                                for q in range(KG):
                                    masks(w, q)
                                add(w)
                                bias(w)
                                statistics(w)
                            return
                        masks(0, 0)
                        masks(0, 1)
                        columns(1)
                        for k in range(SUBS):
                            hots(1, k * SUB_TILES, (k + 1) * SUB_TILES)
                            if k + 2 < KG:
                                masks(0, k + 2)
                        columns(3)
                        add(0)
                        hots(3, 0, 3)
                        masks(2, 0)
                        add(1)
                        masks(2, 1)
                        bias(0)
                        hots(3, 3, 7)
                        masks(2, 2)
                        statistics(0)
                        bias(1)
                        hots(3, 7, 8)
                        masks(2, 3)
                        hots(3, 8, 12)
                        statistics(1)
                        masks(2, 4)
                        hots(3, 12, 16)
                        masks(2, 5)
                        hots(3, 16, 20)
                        add(2)
                        masks(4, 0)
                        masks(4, 1)
                        add(3)
                        masks(4, 2)
                        bias(2)
                        for q in range(3, KG):
                            masks(4, q)
                        statistics(2)
                        add(4)
                        bias(3)
                        statistics(3)
                        for q in range(2):
                            bias(4, (q,))
                            statistics(4, (q,))
                    windows(dve, body)

                @block.tensor
                def _(pe):
                    pe.sem_inc(s_used, FREE)
                    pe.sem_inc(s_t, 1)
                    if dense:
                        pe.sem_inc(s_tile, TILES)
                    pe.wait_ge(s_one, 1)

                    def body(r, b, rb):
                        def bank_free(w):
                            g = rb * U + w
                            pe.wait_ge(s_sum, 1 + ((g - 1) * 2 if w else g * 2))

                        def gathered(w, q):
                            x = rb * NG + G_SLOT[w]
                            if q == 0:
                                bank_free(w)
                            pe.wait_ge(s_mask, x * KG + q + 1)
                            for j in range(q * GROUP, (q + 1) * GROUP):
                                pe.wait_ge(s_row[j], (x + 1) * 16)
                                mask = masks16[:, j % (RING * GROUP), :]
                                nc.tensor.matmul(psum[w % 2][0:P, 0:D + 1], mask, rows16[:, j, D:2 * D + 1], start=(j == 0), stop=False)
                                last = nc.tensor.matmul(psum[w % 2][0:P, 0:D], mask, rows16[:, j, 0:D], start=False, stop=(j == KS - 1))
                            last.then_inc(s_used, 1)

                        def build(w, s):
                            d = rb * ND + D_SLOT[w]
                            first = 2 * s
                            for k in range(SUB_TILES):
                                pe.wait_ge(s_hot, d * (SUBS * SUB_TILES) + s * SUB_TILES + k + 1)
                                for half in range(2):
                                    if k == 0:
                                        pe.wait_ge(s_evac, HALVES + d * (2 * SUBS) + (first + half - 2 if s else 0))
                                    lo, hi = HALF[half] * SUB, HALF[half + 1] * SUB
                                    n = s * SUB_TILES + k
                                    last = nc.tensor.matmul(psum[BUILD[(first + half) % 3]][0:P, 0:hi - lo], row_hot[:, n % 4, :],
                                                            col_hot[:, n % 3, lo:hi], start=(k == 0), stop=(k == SUB_TILES - 1))
                                last.then_inc(s_tile, 1)

                        def multiply(w, lo, hi):
                            if lo == 0:
                                bank_free(w)
                                pe.wait_ge(s_evac, HALVES + (rb * ND + D_SLOT[w] + 1) * (2 * SUBS))
                            for k in range(lo, hi):
                                for part in range(2):
                                    nc.tensor.matmul(psum[w % 2][0:P, 0:D], adjacency[:, k, :], x16[:, k, part * D:(part + 1) * D],
                                                     start=(k == 0 and part == 0), stop=(k == T - 1 and part == 1))
                            if hi == T:
                                for k in range(T):
                                    last = nc.tensor.matmul(psum[w % 2][0:P, D:D + 1], adjacency[:, k, :], rows16[0:P, 0, 2 * D:2 * D + 1],
                                                            start=(k == 0), stop=(k == T - 1))
                                last.then_inc(s_dense, 1)

                        def turn(w):
                            g = rb * U + w
                            pe.wait_ge(s_sum, 1 + (g + 1) * 2)
                            for c in range(DC):
                                last = nc.tensor.transpose(psum[2][:, c * P:(c + 1) * P], summed[:, w % 2, c * 128:(c + 1) * 128],
                                                           ident[0:P, 0:P])
                            last.then_inc(s_t, 1)

                        def project(w):
                            g = rb * U + w
                            pe.wait_ge(s_ht, g + 1)
                            pe.wait_ge(s_post, 1 + 2 * g)
                            for q in range(2):
                                for m in range(4):
                                    for c in range(DC):
                                        last = nc.tensor.matmul(psum[4 + q][:, m * P:(m + 1) * P],
                                                                w1g[:, c, (4 * q + m) * 128:(4 * q + m + 1) * 128],
                                                                hT[:, c, :], start=(c == 0), stop=(c == DC - 1))
                                last.then_inc(s_proj, 1)

                        if not dense:
                            for w in range(U):
                                for q in range(KG):
                                    gathered(w, q)
                                turn(w)
                                project(w)
                            return
                        for w in (0, 2):
                            gathered(w, 0)
                            if w == 0:
                                gathered(w, 1)
                            build(w + 1, 0)
                            if w:
                                project(w - 1)
                                gathered(w, 1)
                            for k in range(1, SUBS):
                                if w:
                                    build(w + 1, k)
                                    gathered(w, k + 1)
                                else:
                                    gathered(w, k + 1)
                                    build(w + 1, k)
                            multiply(w + 1, 0, T // 2)
                            turn(w)
                            multiply(w + 1, T // 2, T)
                            project(w)
                            turn(w + 1)
                        for q in range(KG):
                            gathered(4, q)
                        project(3)
                        turn(4)
                        project(4)
                    windows(pe, body)

                @block.scalar
                def _(act):
                    if dense:
                        act.sem_inc(s_evac, HALVES)
                    else:
                        act.sem_inc(s_kept, 1)

                    def body(r, b, rb):
                        def copies(w):
                            g = rb * U + w
                            if not dense:
                                act.wait_ge(s_sum, 1 + (g + 1) * 2)
                                nc.scalar.copy(tok[:, ds(b * U + w, 1), :], summed[:, w % 2:w % 2 + 1, 0:D]).then_inc(s_kept, 1)
                            act.wait_ge(s_t, 1 + g + 1)
                            nc.scalar.copy(hT[:, 0:DC, :], psum[2][:, 0:DC * P].rearrange("p (c n) -> p c n", c=DC)).then_inc(s_ht, 1)

                        def matrix(w):
                            d = rb * ND + D_SLOT[w]
                            for s in range(SUBS):
                                act.wait_ge(s_tile, TILES + d * (SUBS * SUB_TILES) + (s + 1) * SUB_TILES)
                                for half in range(2):
                                    lo, hi = HALF[half], HALF[half + 1]
                                    nc.scalar.copy(adjacency[:, lo:hi, s * SUB:(s + 1) * SUB],
                                                   psum[BUILD[(2 * s + half) % 3]][0:P, 0:(hi - lo) * SUB].rearrange(
                                                       "p (k n) -> p k n", n=SUB)).then_inc(s_evac, 1)

                        if not dense:
                            for w in range(U):
                                copies(w)
                            return
                        for w in (0, 2):
                            matrix(w + 1)
                            copies(w)
                            copies(w + 1)
                        copies(4)
                    windows(act, body)

        def second_graph():
            s_meta = [sem(f"s_meta{w}") for w in range(U)]
            s_row = [sem(f"s_row{j}") for j in range(KS)]
            s_local = sem("s_local"); s_mask = sem("s_mask"); s_used = sem("s_used"); s_sum = sem("s_sum")
            s_kept = sem("s_kept"); s_mean = sem("s_mean"); s_t = sem("s_t"); s_ht = sem("s_ht"); s_proj = sem("s_proj")
            s_relu = sem("s_relu"); s_zeroed = sem("s_zeroed"); s_first = sem("s_first")
            s_went_pool = sem("s_went_pool"); s_went_sp = sem("s_went_sp")
            META = 4 * 16
            FREE = U * GROUPS
            TURNED = U
            fbuf = view(work, 0, [U, D], P)
            hm = view(work, U * D, [2, D], P)
            relu_in = view(work, (U + 2) * D, [2, D], P)
            with nc.Block() as block:
                def windows(eng, body):
                    n = eng.value_load(rounds[0:1, 0:1], min_val=1, max_val=ROUNDS)
                    with eng.Fori(0, n) as r:
                        with eng.Fori(0, T // U) as b:
                            for w in range(U):
                                body(r, r * T + b * U + w, b * U + w, w, r * (T // U) + b)

                @block.sync
                def _(sp):
                    def body(r, g, t, w, rb):
                        sp.wait_ge(s_used, FREE + (g - U + 1) * GROUPS)
                        sp.sem_inc(s_went_sp, 1)
                        sp.wait_ge(s_t, TURNED + g - U + 1)
                        sp.sem_inc(s_went_sp, 1)
                        at = sp.value_load(starts[0:1, ds(t, 1)], min_val=0, max_val=NE)
                        at = sp.snap(at + r * WIN)
                        for to, frm in ((meta_src, src_pad), (meta_dst, dst_pad), (meta_ew, ew_pad)):
                            sp.dma_start(to[:, w, :], frm[ds(at, WIN)].rearrange("(p j) -> p j", j=KS)).then_inc(s_meta[w], 16)
                        sp.dma_start(fbuf[:, w, :], xn_dram[ds(t * P, P), :]).then_inc(s_meta[w], 16)
                    windows(sp, body)

                @block.gpsimd
                def _(pool):
                    def body(r, g, t, w, rb):
                        pool.wait_ge(s_meta[w], (rb + 1) * META)
                        pool.sem_inc(s_went_pool, 1)
                        for j in range(KS):
                            if j % GROUP == 0:
                                pool.wait_ge(s_used, FREE + (g - 1) * GROUPS + j // GROUP + 1)
                                pool.sem_inc(s_went_pool, 1)
                            nc.gpsimd.indirect_dma_start(
                                out=rows[:, j, :], out_offset=None, in_=xn_dram[:, :],
                                in_offset=bass.IndirectOffsetOnAxis(ap=meta_src[:, w, j:j + 1], axis=0)).then_inc(s_row[j], 16)
                    windows(pool, body)

                @block.vector
                def _(dve):
                    nc.vector.memset(tok[:, :, :], 0.0).then_inc(s_zeroed, 1)
                    dve.wait_ge(s_zeroed, 1)
                    dve.sem_inc(s_sum, 1)
                    dve.sem_inc(s_relu, 1)

                    def body(r, g, t, w, rb):
                        dve.wait_ge(s_meta[w], (rb + 1) * META)
                        nc.vector.tensor_scalar(dst_local[:, w, :], meta_dst[:, w, :], node_base[:, ds(t, 1)], None,
                                                ALU.subtract).then_inc(s_local, 1)
                        dve.wait_ge(s_local, g + 1)
                        for j in range(KS):
                            if j % GROUP == 0:
                                dve.wait_ge(s_used, FREE + (g - 1) * GROUPS + j // GROUP + 1)
                            mask = nc.vector.tensor_scalar(masks[:, j, :], node_row[:, :], dst_local[:, w, j:j + 1],
                                                           meta_ew[:, w, j:j + 1], ALU.is_equal, ALU.mult)
                            if j % GROUP == GROUP - 1:
                                mask.then_inc(s_mask, 1)
                        dve.wait_ge(s_used, FREE + (g + 1) * GROUPS)
                        last_use = g - 1 if w else g
                        dve.wait_ge(s_kept, 1 + last_use)
                        dve.wait_ge(s_t, TURNED + last_use)
                        nc.vector.tensor_tensor(summed[:, w % 2, 0:D], psum[w % 2][0:P, 0:D], tok[:, ds(t, 1), :],
                                                ALU.add).then_inc(s_sum, 1)
                        dve.wait_ge(s_sum, 1 + g + 1)
                        nc.vector.tensor_scalar(hm[:, w % 2, :], summed[:, w % 2, 0:D], rdegree[:, ds(t, 1)], None,
                                                ALU.mult).then_inc(s_mean, 1)
                        dve.wait_ge(s_proj, g + 1)
                        nc.vector.tensor_tensor(relu_in[:, w % 2, :], psum[4 + w % 2][0:P, 0:D], gb_bc[0:P, :],
                                                ALU.add).then_inc(s_relu, 1)
                        dve.wait_ge(s_relu, 1 + g + 1)
                        nc.vector.scalar_tensor_tensor(x3[:, ds(t, 1), :], relu_in[:, w % 2:w % 2 + 1, :], 0.0,
                                                       xres[:, ds(t, 1), :], ALU.max, ALU.add)
                    windows(dve, body)

                @block.tensor
                def _(pe):
                    pe.sem_inc(s_used, FREE)
                    pe.sem_inc(s_t, TURNED)

                    def body(r, g, t, w, rb):
                        pe.wait_ge(s_sum, 1 + (g - 1 if w else g))
                        for j in range(KS):
                            if j % GROUP == 0:
                                pe.wait_ge(s_mask, g * GROUPS + j // GROUP + 1)
                            pe.wait_ge(s_row[j], (g + 1) * 16)
                            product = nc.tensor.matmul(psum[w % 2][0:P, 0:D], masks[:, j, :], rows[:, j, :], start=(j == 0), stop=(j == KS - 1))
                            if j % GROUP == GROUP - 1:
                                product.then_inc(s_used, 1)
                        pe.wait_ge(s_mean, g + 1)
                        pe.wait_ge(s_meta[w], (rb + 1) * META)
                        for c in range(2 * DC):
                            frm = fbuf[:, w, c * 128:(c + 1) * 128] if c < DC else hm[:, w % 2, (c - DC) * 128:(c - DC + 1) * 128]
                            last = nc.tensor.transpose(psum[2][:, c * P:(c + 1) * P], frm, ident[0:P, 0:P])
                        last.then_inc(s_t, 1)
                        pe.wait_ge(s_ht, g + 1)
                        pe.wait_ge(s_relu, 1 + (g - 1 if w else g))
                        for c in range(2 * DC):
                            last = nc.tensor.matmul(psum[4 + w % 2][0:P, 0:D], hT[:, c, :], wT[:, c, :],
                                                    start=(c == 0), stop=(c == 2 * DC - 1))
                        last.then_inc(s_proj, 1)
                    windows(pe, body)

                @block.scalar
                def _(act):
                    source = act.value_load(i_first[0:1, 0:1], min_val=0, max_val=N - 1)
                    act.dma_start(g_col[:, :], xn_dram[ds(source, 1), :].rearrange("a (c p) -> p (a c)", p=128),
                                  allow_slow_non_contiguous=True).then_inc(s_first, 16)
                    act.wait_ge(s_first, 16)
                    act.sem_inc(s_kept, 1)

                    def body(r, g, t, w, rb):
                        act.wait_ge(s_sum, 1 + g + 1)
                        nc.scalar.copy(tok[:, ds(t, 1), :], summed[:, w % 2:w % 2 + 1, 0:D]).then_inc(s_kept, 1)
                        act.wait_ge(s_t, TURNED + g + 1)
                        nc.scalar.copy(hT[:, 0:DC, :], psum[2][:, 0:DC * P].rearrange("p (c n) -> p c n", c=DC))
                        for c in range(DC):
                            scaled = nc.scalar.activation(hT[:, DC + c, :], psum[2][:, (DC + c) * P:(DC + c + 1) * P], ACT.Copy,
                                                          scale=g_col[:, c:c + 1])
                        scaled.then_inc(s_ht, 1)
                    windows(act, body)

        def dispatch(layer, E, F, w1, w2, softmax_first):
            NT = moe_tiles(E)
            FC = F // 128
            B = T // U
            first = layer == 0
            w1s, w2s, early = expert_weights(layer, E, F)
            pools = [[work, 1600, 4096], [arena, 31400, 32768]] if first else [[arena, 26624, 32768]]

            def small(dims, parts=P, dt=fp32):
                size = 1
                for d in dims:
                    size *= d
                size += size % 2
                pool = next(p for p in pools if p[1] + size <= p[2])
                v = view(pool[0], pool[1], dims, parts)
                pool[1] += size
                return v if dt is fp32 else v.bitcast(dt)

            ysum = view(work, 0, [2, D], P)
            tT = view(work, 2 * D, [4, DC, P])
            lg = small([T, E]); v8 = small([T, 8]); i8 = small([T, 8], dt=u32); ex = small([T, 8]); zs = small([T])
            idf = small([T, 2]); sel = small([T, 2, E]); both = small([T, E]); rank = small([T, E])
            picked = small([T, 2, E]); posf = small([T, E]); place = small([T, 2])
            cum = small([T + 1, E]); cf = small([E]); ci = small([E], dt=i32); padded = small([E])
            ends = [small([E]), small([E])]; base = small([E]); adj = small([E], 1)
            tcmp = small([NT, E], 1); tcount = small([NT], 1); valid = small([NT], 1)
            nibble = small([NT], 1); word = small([NT // 4], 1); filled = small([1], 1)
            wts, pos, pos_in, comb, tile_word, tile_row, pad_row = routing(E)

            def over(a, n=T, p=P):
                return a.unsqueeze(1).broadcast_to([p, n, E])

            s_w2 = sem("s_w2"); s_wl = sem("s_wl"); s_bn = sem("s_bn"); s_bns = sem("s_bns"); s_norm = sem("s_norm")
            s_y = sem("s_y"); s_ycopy = sem("s_ycopy"); s_x = sem("s_x"); s_st = sem("s_st"); s_var = sem("s_var")
            s_sq = sem("s_sq"); s_rs = sem("s_rs"); s_tok = sem("s_tok"); s_lt = sem("s_lt"); s_lc = sem("s_lc")
            s_lg = sem("s_lg"); s_lgr = sem("s_lgr"); s_both = sem("s_both"); s_rank = sem("s_rank"); s_rkr = sem("s_rkr")
            s_pos = sem("s_pos"); s_total = sem("s_total"); s_own = sem("s_own"); s_top = sem("s_top"); s_shift = sem("s_shift")
            s_ex = sem("s_ex"); s_sc = sem("s_sc"); s_pad = sem("s_pad"); s_padrow = sem("s_padrow"); s_cum = sem("s_cum"); s_xl = sem("s_xl"); s_zero = sem("s_zero"); s_zeros = sem("s_zeros")

            with nc.Block() as block:
                @block.sync
                def _(sp):
                    if first:
                        sp.dma_start(w2g, L0_gnn_W2.rearrange("(m p) d -> p m d", p=128)).then_inc(s_w2, 16)
                        sp.dma_start(b2g_bc, L0_gnn_b2.partition_broadcast(128)).then_inc(s_w2, 16)
                        sp.dma_start(xres[:, :, :], x.rearrange("(t p) d -> p t d", p=P)).then_inc(s_xl, 16)
                        sp.wait_ge(s_w2, 32)
                    for e in range(E):
                        sp.dma_start(w1s[:, e * DC * F:(e + 1) * DC * F].rearrange("p (c f) -> p c f", c=DC),
                                     w1[e].rearrange("(c p) f -> p c f", p=128)).then_inc(s_wl, 16)
                    if not first:
                        sp.wait_ge(s_x, T)
                    for e in range(early):
                        sp.dma_start(w2s[:, e * FC * D:(e + 1) * FC * D].rearrange("p (c d) -> p c d", c=FC),
                                     w2[e].rearrange("(c p) d -> p c d", p=128)).then_inc(s_wl, 16)
                    sp.wait_ge(s_wl, 16 * (E + early))
                    if first:
                        sp.wait_ge(s_xl, 16)
                        sp.wait_ge(s_zero, 1)
                        behind = 2 * N // 128 * 128
                        sp.dma_start(slots_out[behind:SLOTS, :].rearrange("(n p) d -> p n d", p=128),
                                     zero_rows[:, :].unsqueeze(1).broadcast_to([128, (SLOTS - behind) // 128, D])).then_inc(s_zeros, 16)
                        sp.wait_ge(s_zeros, 16)
                    sp.wait_ge(s_padrow, 1)
                    for e in range(E):
                        row = sp.value_load(pad_row[0:1, e:e + 1], min_val=e * REGION, max_val=e * REGION + N)
                        sp.dma_start(slots_in[ds(row, 128), :], zero_rows[:, :]).then_inc(s_pad, 16)
                    sp.wait_ge(s_pad, 16 * E)

                @block.scalar
                def _(act):
                    def batch_norm(b):
                        for m in range(HC):
                            part = h1T[:, m, b * U * P:(b + 1) * U * P]
                            nc.scalar.activation(part, part, ACT.Relu, bias=bn_shift[:, m:m + 1],
                                                 scale=bn_scale[:, m:m + 1]).then_inc(s_norm, 1)

                    if first:
                        act.wait_ge(s_bn, HC)
                        nc.scalar.activation(bn_shift[:, :], bnmv[:, :, 1], ACT.Sqrt, bias=eps[:, :]).then_inc(s_bns, 1)
                        act.wait_ge(s_bn, HC + 4)
                        batch_norm(0)
                        batch_norm(1)
                    else:
                        for t in range(T):
                            nc.scalar.copy(xres[:, t, :], x3[:, t, :]).then_inc(s_x, 1)
                    def roots(b):
                        act.wait_ge(s_var, (b + 1) * U)
                        nc.scalar.activation(mean_v[:, b * U:(b + 1) * U], mv[:, b * U:(b + 1) * U, 1], ACT.Sqrt,
                                             bias=eps[0:P, :]).then_inc(s_sq, 1)

                    def copies(b):
                        for t in range(b * U, (b + 1) * U):
                            act.wait_ge(s_lt, t + 1)
                            if t >= 4:
                                act.wait_ge(s_lg, t - 3)
                            nc.scalar.copy(tT[:, t % 4, :, :], psum[2 + t % 2][:, 0:DC * P].rearrange("p (c n) -> p c n", c=DC)).then_inc(s_lc, 1)

                    if first:
                        for b in range(B):
                            roots(b)
                            if b + 2 < B:
                                batch_norm(b + 2)
                            copies(b)
                    else:
                        roots(0)
                        roots(1)
                        for b in range(B):
                            copies(b)
                            if b + 2 < B:
                                roots(b + 2)
                    n = 8 if softmax_first else 2
                    act.wait_ge(s_shift, 1)
                    nc.scalar.activation(ex[:, :, 0:n], ex[:, :, 0:n], ACT.Exp).then_inc(s_ex, 1)

                @block.gpsimd
                def _(pool):
                    if first:
                        pool.memset(zero_rows[:, :], 0.0).then_inc(s_zero, 1)
                    for t in range(T):
                        if t % U == 0:
                            pool.wait_ge(s_pos, t // U + 1)
                        for k in range(2):
                            nc.gpsimd.indirect_dma_start(
                                out=slots_in[:, :], out_offset=bass.IndirectOffsetOnAxis(ap=pos_in[:, t, k:k + 1], axis=0),
                                in_=tok[:, t, :], in_offset=None).then_inc(s_sc, 16)
                    pool.wait_ge(s_sc, 16 * 2 * T)

                @block.tensor
                def _(pe):
                    def product(t):
                        if t >= 2:
                            pe.wait_ge(s_ycopy, t - 1)
                        for m in range(HC):
                            if t % U == 0:
                                pe.wait_ge(s_norm, t // U * HC + m + 1)
                            last = nc.tensor.matmul(psum[t % 2][0:P, 0:D], h1T[:, m, t * P:(t + 1) * P], w2g[:, m, :],
                                                    start=(m == 0), stop=(m == HC - 1))
                        last.then_inc(s_y, 1)

                    def logits(t):
                        b = t // U
                        pe.wait_ge(s_lc, t + 1)
                        if t % U == 0 and b >= 2:
                            pe.wait_ge(s_lgr, b - 1)
                        for c in range(DC):
                            last = nc.tensor.matmul(psum[4 + b % 2][0:P, (t % U) * E:(t % U + 1) * E], tT[:, t % 4, c, :],
                                                    gateT[layer][:, c, :], start=(c == 0), stop=(c == DC - 1))
                        last.then_inc(s_lg, 1)

                    def transposes_and_logits(b):
                        for t in range(b * U, (b + 1) * U):
                            pe.wait_ge(s_tok, t + 1)
                            if t >= 2:
                                pe.wait_ge(s_lc, t - 1)
                            for c in range(DC):
                                last = nc.tensor.transpose(psum[2 + t % 2][:, c * P:(c + 1) * P], tok[:, t, c * 128:(c + 1) * 128],
                                                           ident[0:P, 0:P])
                            last.then_inc(s_lt, 1)
                            if t % U:
                                logits(t - 1)
                        logits((b + 1) * U - 1)

                    def ranks(b):
                        pe.wait_ge(s_cum, (b + 1) * U)
                        if b >= 2:
                            pe.wait_ge(s_rkr, b - 1)
                        to = psum[6 + b % 2][0:P, 0:U * E]
                        nc.tensor.matmul(to, before[:, :], both[:, b * U:(b + 1) * U, :].rearrange("p t e -> p (t e)"), start=True, stop=False)
                        last = nc.tensor.matmul(to, ones[0:P, 0:P], cum[:, b * U:(b + 1) * U, :].rearrange("p t e -> p (t e)"), start=False, stop=True)
                        last.then_inc(s_rank, 1)

                    if first:
                        pe.wait_ge(s_w2, 32)
                    if first:
                        for b in range(B + 2):
                            if b < B:
                                product(b * U)
                                product(b * U + 1)
                            if b >= 2:
                                ranks(b - 2)
                            if b < B:
                                for t in range(b * U + 2, (b + 1) * U):
                                    product(t)
                            if 1 <= b <= B:
                                transposes_and_logits(b - 1)
                    else:
                        transposes_and_logits(0)
                        transposes_and_logits(1)
                        for b in range(B):
                            ranks(b)
                            if b + 2 < B:
                                transposes_and_logits(b + 2)
                    pe.wait_ge(s_cum, T)
                    nc.tensor.matmul(psum[0][0:P, 0:E], ones[0:P, 0:P], cum[:, T, :], start=True, stop=True).then_inc(s_total, 1)

                @block.vector
                def _(dve):
                    link = chain(dve, s_own)

                    def residual(t):
                        if first:
                            dve.wait_ge(s_y, t + 1)
                            nc.vector.tensor_tensor(ysum[:, t % 2, :], psum[t % 2][0:P, 0:D], b2g_bc[0:P, :], ALU.add).then_inc(s_ycopy, 1)
                            dve.wait_ge(s_ycopy, t + 1)
                            nc.vector.scalar_tensor_tensor(xres[:, t, :], ysum[:, t % 2, :], 0.0, xres[:, t, :],
                                                           ALU.max, ALU.add).then_inc(s_x, 1)
                        dve.wait_ge(s_x, t + 1)
                        nc.vector.bn_stats(st6[:, t, :], xres[:, t, :]).then_inc(s_st, 1)

                    def variances(b):
                        for t in range(b * U, (b + 1) * U):
                            dve.wait_ge(s_st, t + 1)
                            nc.vector.bn_aggr(mv[:, t, :], st6[:, t, :]).then_inc(s_var, 1)

                    def normalise(b):
                        dve.wait_ge(s_sq, b + 1)
                        nc.vector.reciprocal(rstd[:, b * U:(b + 1) * U], mean_v[:, b * U:(b + 1) * U]).then_inc(s_rs, 1)
                        dve.wait_ge(s_rs, b + 1)
                        for t in range(b * U, (b + 1) * U):
                            nc.vector.tensor_scalar(tok[:, t, :], xres[:, t, :], mv[:, t, 0:1], rstd[:, t:t + 1],
                                                    ALU.subtract, ALU.mult).then_inc(s_tok, 1)

                    def choose(b):
                        r = slice(b * U, (b + 1) * U)
                        dve.wait_ge(s_lg, (b + 1) * U)
                        pt = psum[4 + b % 2][0:P, 0:U * E].rearrange("p (t e) -> p t e", e=E)
                        if first:
                            nc.vector.tensor_copy(lg[:, r, :], pt).then_inc(s_lgr, 1)
                        else:
                            nc.vector.tensor_tensor(lg[:, r, :], pt, over(gateb_bc[0:P, 0:E], U), ALU.add).then_inc(s_lgr, 1)
                        dve.wait_ge(s_lgr, b + 1)
                        for t in range(b * U, (b + 1) * U):
                            nc.vector.max(v8[:, t, :], lg[:, t, :]).then_inc(s_top, 1)
                        for n, t in enumerate(range(b * U, (b + 1) * U)):
                            dve.wait_ge(s_top, 2 * b * U + n + 1)
                            nc.vector.max_index(i8[:, t, :], v8[:, t, :], lg[:, t, :]).then_inc(s_top, 1)
                        dve.wait_ge(s_top, 2 * (b + 1) * U)
                        link(nc.vector.tensor_copy(idf[:, r, :], i8[:, r, 0:2]))
                        link(nc.vector.tensor_tensor(sel[:, r, :, :], expert_row[0:P, 0:E].unsqueeze(1).unsqueeze(1).broadcast_to([P, U, 2, E]),
                                                     idf[:, r, :].unsqueeze(3).broadcast_to([P, U, 2, E]), ALU.is_equal))
                        nc.vector.tensor_tensor(both[:, r, :], sel[:, r, 0, :], sel[:, r, 1, :], ALU.add).then_inc(s_both, 1)
                        dve.wait_ge(s_both, b + 1)
                        for t in range(b * U, (b + 1) * U):
                            nc.vector.tensor_tensor(cum[:, t + 1, :], cum[:, t, :], both[:, t, :], ALU.add).then_inc(s_cum, 1)
                            dve.wait_ge(s_cum, t + 1)

                    def places(b):
                        r = slice(b * U, (b + 1) * U)
                        dve.wait_ge(s_rank, b + 1)
                        nc.vector.tensor_copy(rank[:, r, :], psum[6 + b % 2][0:P, 0:U * E].rearrange("p (t e) -> p t e", e=E)).then_inc(s_rkr, 1)
                        dve.wait_ge(s_rkr, b + 1)
                        link(nc.vector.tensor_tensor(posf[:, r, :], rank[:, r, :], over(region_row[0:P, 0:E], U), ALU.add))
                        link(nc.vector.tensor_tensor(picked[:, r, :, :], sel[:, r, :, :],
                                                     posf[:, r, :].unsqueeze(2).broadcast_to([P, U, 2, E]), ALU.mult))
                        link(nc.vector.tensor_reduce(place[:, r, :], picked[:, r, :, :], AX.X, ALU.add))
                        nc.vector.tensor_copy(pos_in[:, r, :], place[:, r, :]).then_inc(s_pos, 1)

                    if first:
                        for m in range(HC):
                            nc.vector.bn_aggr(bnmv[:, m, :], bn6[:, m, :, :].rearrange("p t s -> p (t s)")).then_inc(s_bn, 1)
                        dve.wait_ge(s_bns, 1)
                        scale = chain(dve, s_bn)
                        scale.count[0] = HC
                        scale(nc.vector.reciprocal(bn_scale[:, :], bn_shift[:, :]))
                        scale(nc.vector.tensor_tensor(bn_scale[:, :], bn_scale[:, :], gam, ALU.mult))
                        scale(nc.vector.tensor_tensor(bn_shift[:, :], bnmv[:, :, 0], bn_scale[:, :], ALU.mult))
                        scale(nc.vector.tensor_tensor(bn_shift[:, :], bet, bn_shift[:, :], ALU.subtract))
                        dve.wait_ge(s_w2, 32)
                        dve.wait_ge(s_xl, 16)
                    link(nc.vector.memset(cum[:, 0, :], 0.0))
                    if first:
                        for b in range(B + 2):
                            if b < B:
                                for t in range(b * U, b * U + 3):
                                    residual(t)
                            if b >= 2:
                                places(b - 2)
                            if b < B:
                                for t in range(b * U + 3, (b + 1) * U):
                                    residual(t)
                                variances(b)
                                if b:
                                    choose(b - 1)
                                normalise(b)
                            elif b == B:
                                choose(b - 1)
                    else:
                        def statistics(b):
                            if b < B:
                                for t in range(b * U, (b + 1) * U):
                                    residual(t)
                                variances(b)

                        statistics(0)
                        statistics(1)
                        normalise(0)
                        statistics(2)
                        normalise(1)
                        for b in range(B):
                            choose(b)
                            statistics(b + 3)
                            places(b)
                            if b + 2 < B:
                                normalise(b + 2)

                    dve.wait_ge(s_total, 1)
                    total = psum[0][0:P, 0:E]
                    nc.vector.tensor_tensor(pad_row[0:1, 0:E], total[0:1, :], region_row[0:1, 0:E], ALU.add).then_inc(s_padrow, 1)
                    link(nc.vector.tensor_scalar(cf, total, 127.0, None, ALU.add))
                    link(nc.vector.tensor_copy(ci, cf))
                    link(nc.vector.tensor_scalar(ci, ci, 7, 7, ALU.logical_shift_right, ALU.logical_shift_left))
                    link(nc.vector.tensor_copy(padded, ci))
                    n = 8 if softmax_first else 2
                    nc.vector.tensor_tensor(ex[:, :, 0:n], v8[:, :, 0:n], v8[:, :, 0:1].broadcast_to([P, T, n]), ALU.subtract).then_inc(s_shift, 1)
                    q = padded
                    s = 1
                    while s < E:
                        to = ends[s.bit_length() % 2]
                        nc.vector.tensor_copy(to[:, 0:s], q[:, 0:s]).then_inc(s_own, 1)
                        link.count[0] += 1
                        link(nc.vector.tensor_tensor(to[:, s:E], q[:, s:E], q[:, 0:E - s], ALU.add))
                        q = to
                        s *= 2
                    link(nc.vector.tensor_tensor(base, q, padded, ALU.subtract))
                    link(nc.vector.tensor_scalar(filled, q[0:1, E - 1:E], float((GROUP_TILES - 1 - tail_tiles(E)) * 128), None, ALU.add))
                    link(nc.vector.tensor_copy(tile_groups[:, :], filled))
                    link(nc.vector.tensor_scalar(tile_groups[:, :], tile_groups[:, :], 7 + GROUP_TILES.bit_length() - 1, 0,
                                                 ALU.logical_shift_right, ALU.logical_shift_left))
                    link(nc.vector.tensor_tensor(posf, rank, over(base), ALU.add))
                    link(nc.vector.tensor_tensor(picked, sel, posf.unsqueeze(2).broadcast_to([P, T, 2, E]), ALU.mult))
                    link(nc.vector.tensor_reduce(place, picked, AX.X, ALU.add))
                    link(nc.vector.tensor_copy(pos[:, :, :], place))
                    link(nc.vector.tensor_tensor(adj, region_row[0:1, 0:E], base[0:1, :], ALU.subtract))
                    link(nc.vector.tensor_tensor(tcmp, over(q[0:1, :], NT, 1),
                                                 tile_start[:, 0:NT].unsqueeze(2).broadcast_to([1, NT, E]), ALU.is_le))
                    link(nc.vector.tensor_reduce(tcount, tcmp, AX.X, ALU.add))
                    link(nc.vector.tensor_scalar(nibble, tcount, float(E - 1), None, ALU.min))
                    link(nc.vector.tensor_tensor(nibble, nibble, nibble_row[:, 0:NT], ALU.mult))
                    link(nc.vector.tensor_reduce(word, nibble.rearrange("p (n k) -> p n k", k=4), AX.X, ALU.add))
                    link(nc.vector.tensor_copy(tile_word[:, 0:NT // 4], word))
                    link(nc.vector.tensor_tensor(tcmp, over(expert_row[0:1, 0:E], NT, 1), tcount.unsqueeze(2).broadcast_to([1, NT, E]), ALU.is_equal))
                    link(nc.vector.tensor_tensor(tcmp, tcmp, over(adj, NT, 1), ALU.mult))
                    link(nc.vector.tensor_scalar(valid, tcount, float(E), None, ALU.is_lt))
                    link(nc.vector.tensor_reduce(tcount, tcmp, AX.X, ALU.add))
                    link(nc.vector.tensor_tensor(tcount, tcount, tile_start[:, 0:NT], ALU.add))
                    link(nc.vector.tensor_tensor(tile_row[:, 0:NT], tcount, valid, ALU.mult))
                    dve.wait_ge(s_ex, 1)
                    if softmax_first:
                        link(nc.vector.tensor_reduce(zs, ex, AX.X, ALU.add))
                        link(nc.vector.reciprocal(zs, zs))
                        link(nc.vector.tensor_tensor(ex[:, :, 0:2], ex[:, :, 0:2], zs.unsqueeze(2).broadcast_to([P, T, 2]), ALU.mult))
                    link(nc.vector.tensor_tensor(zs, ex[:, :, 0], ex[:, :, 1], ALU.add))
                    if softmax_first:
                        link(nc.vector.tensor_scalar(zs, zs, 1e-12, None, ALU.max))
                    link(nc.vector.reciprocal(zs, zs))
                    link(nc.vector.tensor_tensor(wts[:, :, :], ex[:, :, 0:2], zs.unsqueeze(2).broadcast_to([P, T, 2]), ALU.mult))
                    link(nc.vector.tensor_tensor(picked, sel, wts[:, :, :].unsqueeze(3).broadcast_to([P, T, 2, E]), ALU.mult))
                    link(nc.vector.tensor_tensor(comb, picked[:, :, 0, :], picked[:, :, 1, :], ALU.add))

        def experts_stage(layer, E, F, w1, w2, act_fn):
            NT = moe_tiles(E)
            FC = F // 128
            eb = EB0 if layer == 0 else EB1
            w1s, w2s, early = expert_weights(layer, E, F)
            _, _, _, _, tile_word, tile_row, _ = routing(E)
            G = GROUP_TILES
            TAIL = tail_tiles(E)
            S = 4
            assert G % S == 0 and TAIL % S == 0
            xin = view(work, 0, [S, D])
            xT = view(work, 1024, [S, D])
            hN = view(work, 2048, [2, 512])
            hTt = view(work, 3072, [2, 512])
            s_xi = [sem(f"s_xi_{w}") for w in range(S)]
            s_yo = [sem(f"s_yo_{q}") for q in range(2)]
            s_xt = sem("s_xt"); s_xc = sem("s_xc"); s_h = sem("s_h"); s_hc = sem("s_hc")
            s_g = sem("s_g"); s_gc = sem("s_gc"); s_o2 = sem("s_o2"); s_oc = sem("s_oc")
            s_gb = sem("s_gb"); s_table = sem("s_table"); s_w2l = sem("s_w2l"); s_went = sem("s_went"); s_stored = sem("s_stored")
            with nc.Block() as block:
                def groups(eng, body, engine=None):
                    def step(i, count, more):
                        experts = []
                        if engine is not None:
                            _, words = nc.values_load_multi_w_load_instructions(
                                tile_word[0:1, ds(i * (G // 4), count // 4)], engines=(engine,), min_val=0, max_val=(1 << 16) - 1)
                            experts = [eng.snap((words[w // 4] >> 4 * (w % 4)) & (E - 1)) for w in range(count)]
                        body(i, experts, count, more)

                    n = eng.value_load(tile_groups[0:1, 0:1], min_val=1, max_val=(NT - TAIL) // G)
                    with eng.Fori(0, n) as i:
                        step(i, G, True)
                    step(n, TAIL, False)

                @block.sync
                def _(sp):
                    def load(n, slot):
                        row = sp.value_load(tile_row[0:1, ds(n, 1)], min_val=0, max_val=E * REGION - 128)
                        sp.dma_start(xin[:, slot, :], slots_in[ds(row, 128), :]).then_inc(s_xi[slot], 16)

                    for w in range(S):
                        load(w, w)
                    if layer == 1:
                        sp.dma_start(fbet_bc, L1_ffn_beta.partition_broadcast(128)).then_inc(s_gb, 16)
                        sp.dma_start(fgam_bc[:, :], L1_ffn_gamma.partition_broadcast(128)).then_inc(s_gb, 16)
                    for e in range(early, E):
                        sp.dma_start(w2s[:, e * FC * D:(e + 1) * FC * D].rearrange("p (c d) -> p c d", c=FC),
                                     w2[e].rearrange("(c p) d -> p c d", p=128)).then_inc(s_w2l, 16)

                    def body(i, experts, count, more):
                        for w in range(count):
                            if more or w + S < count:
                                sp.wait_ge(s_xt, i * G + w + 1)
                                sp.sem_inc(s_went, 1)
                                load(i * G + w + S, w % S)
                    groups(sp, body)
                    sp.wait_ge(s_w2l, 16 * (E - early))
                    if layer == 1:
                        sp.wait_ge(s_gb, 32)

                @block.tensor
                def _(pe):
                    def x_transposes(i, w):
                        pe.wait_ge(s_xi[w % S], (i * (G // S) + w // S + 1) * 16)
                        for c in range(DC):
                            at = (w % 2) * D + c * 128
                            last = nc.tensor.transpose(psum[4 + w % S // 2][:, at:at + 128], xin[:, w % S, c * 128:(c + 1) * 128], ident[:, :])
                        last.then_inc(s_xt, 1)

                    pe.sem_inc(s_h, S)
                    pe.sem_inc(s_g, 2)
                    pe.sem_inc(s_o2, 2)
                    for w in range(S):
                        x_transposes(0, w)

                    def body(i, experts, count, more):
                        def first_product(w):
                            pe.wait_ge(s_xc, i * (G // 2) + w // 2 + 1)
                            pe.wait_ge(s_gc, i * G + w + 1)
                            for c in range(DC):
                                last = nc.tensor.matmul(psum[w % S][:, 0:F], xT[:, w % S, c * 128:(c + 1) * 128],
                                                        w1s[:, ds(experts[w] * (DC * F) + c * F, F)], start=(c == 0), stop=(c == DC - 1))
                            last.then_inc(s_h, 1)

                        def hidden_transposes(w):
                            pe.wait_ge(s_hc, i * G + w + 1)
                            for c in range(FC):
                                last = nc.tensor.transpose(psum[w % S][:, c * 128:(c + 1) * 128], hN[:, w % 2, c * 128:(c + 1) * 128], ident[:, :])
                            last.then_inc(s_g, 1)

                        def second_product(w):
                            pe.wait_ge(s_gc, S + i * G + w + 1)
                            pe.wait_ge(s_oc, i * (G // 2) + w // 2 + 1)
                            for c in range(FC):
                                last = nc.tensor.matmul(psum[6 + w % S // 2][:, (w % 2) * D:(w % 2) * D + D],
                                                        hTt[:, w % 2, c * 128:(c + 1) * 128],
                                                        w2s[:, ds(experts[w] * (FC * D) + c * D, D)], start=(c == 0), stop=(c == FC - 1))
                            last.then_inc(s_o2, 1)

                        first_product(0)
                        first_product(1)
                        hidden_transposes(0)
                        for w in range(count):
                            if w + 2 < count:
                                first_product(w + 2)
                            if w + 1 < count:
                                hidden_transposes(w + 1)
                            if w == 0:
                                pe.wait_ge(s_w2l, 16 * (E - early))
                            second_product(w)
                            if w % 2 == 0 and (more or w + S < count):
                                x_transposes(i, w + S)
                                x_transposes(i, w + S + 1)
                    groups(pe, body, mybir.EngineType.PE)

                @block.scalar
                def _(act):
                    act.sem_inc(s_gc, S)

                    def body(i, experts, count, more):
                        if act_fn is ACT.Gelu:
                            nc.scalar.activation(scal[:, 0:1], eps[0:1, :], act_fn).then_inc(s_table, 1)
                            act.wait_ge(s_table, i + 1)
                        for w in range(count):
                            act.wait_ge(s_g, 2 + i * G + w + 1)
                            act.wait_ge(s_o2, i * G + w + 1)
                            for c in range(FC):
                                last = nc.scalar.activation(hTt[:, w % 2, c * 128:(c + 1) * 128], psum[w % S][:, c * 128:(c + 1) * 128], act_fn,
                                                            bias=vecs[:, ds(experts[w] * FC + (eb + c), 1)])
                            last.then_inc(s_gc, 1)
                    groups(act, body, mybir.EngineType.Activation)

                @block.vector
                def _(dve):
                    dve.sem_inc(s_oc, 2)
                    if layer == 1:
                        dve.wait_ge(s_gb, 32)
                        nc.vector.tensor_tensor(xres[:, :, :], xres[:, :, :], fbet_bc[0:P, :].unsqueeze(1).broadcast_to([P, T, D]), ALU.add)

                    def xT_copy(i, w):
                        dve.wait_ge(s_xt, i * G + w + 2)
                        dve.wait_ge(s_h, i * G + w + 2)
                        nc.vector.tensor_copy(xT[:, w % S:w % S + 2, :],
                                              psum[4 + w % S // 2][:, :].rearrange("p (w d) -> p w d", w=2)).then_inc(s_xc, 1)

                    for w in range(0, S, 2):
                        xT_copy(0, w)

                    def body(i, experts, count, more):
                        def hidden_copy(w):
                            dve.wait_ge(s_h, S + i * G + w + 1)
                            dve.wait_ge(s_g, i * G + w + 1)
                            nc.vector.tensor_copy(hN[:, w % 2, 0:F], psum[w % S][:, 0:F]).then_inc(s_hc, 1)

                        def result_copy(q):
                            dve.wait_ge(s_o2, 2 + i * G + 2 * q + 2)
                            dve.wait_ge(s_stored, i * (G // 2) + q + 1)
                            nc.vector.tensor_copy(y_out[:, q % 2, :, :], psum[6 + q % 2][:, :].rearrange("p (w d) -> p w d", w=2)).then_inc(s_oc, 1)

                        hidden_copy(0)
                        hidden_copy(1)
                        for w in range(count):
                            if w + 2 < count:
                                hidden_copy(w + 2)
                            if w % 2:
                                result_copy(w // 2)
                            elif more or w + S < count:
                                xT_copy(i, w + S)
                    groups(dve, body)

                @block.gpsimd
                def _(pool):
                    pool.sem_inc(s_stored, 2)

                    def body(i, experts, count, more):
                        for q in range(count // 2):
                            pool.wait_ge(s_oc, 2 + i * (G // 2) + q + 1)
                            pool.sem_inc(s_went, 1)
                            pool.dma_start(slots_out[ds((i * (G // 2) + q) * 256, 256), :].rearrange("(w p) d -> p w d", w=2),
                                           y_out[:, q % 2, :, :]).then_inc(s_yo[q % 2], 16)
                            if q:
                                pool.wait_ge(s_yo[(q - 1) % 2], (i * (G // 4) + (q - 1) // 2 + 1) * 16)
                                pool.sem_inc(s_stored, 1)
                        pool.wait_ge(s_yo[1], (i * (G // 4) + count // 4) * 16)
                        pool.sem_inc(s_stored, 1)
                    groups(pool, body)

        def combine(layer, E, NT, b2):
            NQ = 10
            BATCH = [0, 5, 10, 15, 20, 23, T]
            B = len(BATCH) - 1
            first = layer == 0
            ygath = view(arena, 0, [NQ, D], P)
            part = view(arena, NQ * D, [4, D], P)
            b2e = view(work, 0, [D], E)
            combT = view(work, D, [4, P], 16)
            wts, pos, _, comb, _, _, _ = routing(E)
            s_b2 = sem("s_b2"); s_yg = [sem(f"s_yg{n}") for n in range(NQ)]
            s_ct = sem("s_ct"); s_cc = sem("s_cc"); s_bb = sem("s_bb"); s_part = sem("s_part"); s_first = sem("s_first"); s_c = sem("s_c")
            s_st = sem("s_st"); s_var = sem("s_var"); s_sq = sem("s_sq"); s_rs = sem("s_rs")
            s_n = sem("s_n"); s_gain = sem("s_gain"); s_io = sem("s_io")
            s_v = sem("s_v"); s_vt = sem("s_vt"); s_vd = sem("s_vd")
            result = xres if first else tok
            with nc.Block() as block:
                @block.sync
                def _(sp):
                    sp.dma_start(b2e, b2).then_inc(s_b2, 16)
                    if first:
                        sp.dma_start(wraw, L1_gnn_W.rearrange("(o p) i -> p o i", p=128)).then_inc(s_v, 16)
                        sp.dma_start(gb_bc, L1_gnn_b.partition_broadcast(128)).then_inc(s_v, 16)
                        sp.wait_ge(s_v, 32)
                    sp.wait_ge(s_b2, 16)
                    to = (xn_dram if first else out).rearrange("(t p) d -> p t d", p=P)
                    for b in range(B):
                        sp.wait_ge(s_n, BATCH[b + 1])
                        sp.dma_start(to[:, BATCH[b]:BATCH[b + 1], :], tok[:, BATCH[b]:BATCH[b + 1], :]).then_inc(s_io, 16)
                    sp.wait_ge(s_io, 16 * B)

                @block.gpsimd
                def _(pool):
                    for t in range(T):
                        for k in range(2):
                            n = 2 * t + k
                            if n >= NQ:
                                pool.wait_ge(s_c if k else s_part, t - NQ // 2 + 1)
                            nc.gpsimd.indirect_dma_start(
                                out=ygath[:, n % NQ, :], out_offset=None, in_=slots_out[0:NT * 128, :],
                                in_offset=bass.IndirectOffsetOnAxis(ap=pos[:, t, k:k + 1], axis=0)).then_inc(s_yg[n % NQ], 16)

                @block.tensor
                def _(pe):
                    if first:
                        pe.wait_ge(s_v, 32)
                        for i in range(2 * DC):
                            for o in range(DC):
                                at = (i % 2) * D + o * 128
                                last = nc.tensor.transpose(psum[6 + i // 2][:, at:at + 128], wraw[:, o, i * 128:(i + 1) * 128], ident[:, :])
                        last.then_inc(s_vt, 1)
                    pe.wait_ge(s_b2, 16)

                    def first_rows(t):
                        pe.wait_ge(s_part, t + 1)
                        nc.tensor.matmul(psum[2 + t % 4][0:P, 0:D], ident[0:P, 0:P], part[:, t % 4, :], start=False, stop=True).then_inc(s_first, 1)

                    for t in range(T):
                        if t >= 2:
                            pe.wait_ge(s_cc, t - 1)
                        nc.tensor.transpose(psum[t % 2][0:E, 0:P], comb[:, t, :], ident[0:P, 0:P]).then_inc(s_ct, 1)
                        if t >= 4:
                            pe.wait_ge(s_c, t - 3)
                        to = psum[2 + t % 4][0:P, 0:D]
                        nc.tensor.matmul(to, ident[0:P, 0:P], tok[:, t, :], start=True, stop=False)
                        if first:
                            nc.tensor.matmul(to, ident[0:P, 0:P], xres[:, t, :], start=False, stop=False)
                        pe.wait_ge(s_cc, t + 1)
                        nc.tensor.matmul(to, combT[0:E, t % 4, :], b2e, start=False, stop=False).then_inc(s_bb, 1)
                        if t:
                            first_rows(t - 1)
                    first_rows(T - 1)

                @block.scalar
                def _(act):
                    def weighted(t):
                        act.wait_ge(s_ct, t + 1)
                        if t >= 4:
                            act.wait_ge(s_bb, t - 3)
                        nc.scalar.copy(combT[0:E, t % 4, :], psum[t % 2][0:E, 0:P]).then_inc(s_cc, 1)
                        n = 2 * t
                        act.wait_ge(s_yg[n % NQ], 16 * (n // NQ + 1))
                        if t >= 4:
                            act.wait_ge(s_first, t - 3)
                        nc.scalar.activation(part[:, t % 4, :], ygath[:, n % NQ, :], ACT.Copy, scale=wts[:, t, 0:1]).then_inc(s_part, 1)

                    def roots(b):
                        act.wait_ge(s_var, BATCH[b + 1])
                        nc.scalar.activation(mean_v[:, BATCH[b]:BATCH[b + 1]], mv[:, BATCH[b]:BATCH[b + 1], 1], ACT.Sqrt,
                                             bias=eps[0:P, :]).then_inc(s_sq, 1)

                    for t in range(T):
                        weighted(t)
                        if t - 1 in BATCH[1:]:
                            roots(BATCH.index(t - 1) - 1)
                    roots(B - 1)

                @block.vector
                def _(dve):
                    def add_rows(t, other):
                        n = 2 * t + 1
                        dve.wait_ge(s_yg[n % NQ], 16 * (n // NQ + 1))
                        dve.wait_ge(s_first, t + 1)
                        nc.vector.scalar_tensor_tensor(result[:, t, :], ygath[:, n % NQ, :], wts[:, t, 1:2], psum[2 + t % 4][0:P, 0:D],
                                                       ALU.mult, ALU.add).then_inc(s_c, 1)
                        if other is not None:
                            normalise(other, 0)
                        dve.wait_ge(s_c, t + 1)
                        nc.vector.bn_stats(st6[:, t, :], result[:, t, :]).then_inc(s_st, 1)
                        if other is not None:
                            normalise(other, 1)
                        dve.wait_ge(s_st, t + 1)
                        nc.vector.bn_aggr(mv[:, t, :], st6[:, t, :]).then_inc(s_var, 1)

                    def reciprocals(b):
                        dve.wait_ge(s_sq, b + 1)
                        nc.vector.reciprocal(rstd[:, BATCH[b]:BATCH[b + 1]], mean_v[:, BATCH[b]:BATCH[b + 1]]).then_inc(s_rs, 1)
                        dve.wait_ge(s_rs, b + 1)

                    def normalise(t, step):
                        if first and step == 0:
                            nc.vector.tensor_scalar(tok[:, t, :], xres[:, t, :], mv[:, t, 0:1], rstd[:, t:t + 1],
                                                    ALU.subtract, ALU.mult).then_inc(s_n, 1)
                        elif step == 0:
                            nc.vector.scalar_tensor_tensor(tok[:, t, :], tok[:, t, :], mv[:, t, 0:1], fgam_bc[0:P, :],
                                                           ALU.subtract, ALU.mult).then_inc(s_gain, 1)
                        elif not first:
                            dve.wait_ge(s_gain, t + 1)
                            nc.vector.scalar_tensor_tensor(tok[:, t, :], tok[:, t, :], rstd[:, t:t + 1], xres[:, t, :],
                                                           ALU.mult, ALU.add).then_inc(s_n, 1)

                    if first:
                        nc.vector.tensor_scalar(rdegree[:, :], degree[:, :], 1.0, None, ALU.max).then_inc(s_vd, 1)
                        dve.wait_ge(s_vd, 1)
                        nc.vector.reciprocal(rdegree[:, :], rdegree[:, :])
                        dve.wait_ge(s_vt, 1)
                        for i in range(DC):
                            nc.vector.tensor_copy(wT[:, 2 * i:2 * i + 2, :], psum[6 + i][:, :].rearrange("p (i o) -> p i o", i=2))
                    done = 0
                    ready = 0
                    for t in range(T):
                        add_rows(t, done if done < ready else None)
                        done += done < ready
                        if t - 1 in BATCH[1:]:
                            reciprocals(BATCH.index(t - 1) - 1)
                            ready = t - 1
                    for b in range(B):
                        if BATCH[b + 1] > ready:
                            reciprocals(b)
                    for t in range(done, T + 1):
                        if t < T:
                            normalise(t, 0)
                        if t > done:
                            normalise(t - 1, 1)

        wts_all = sb("wts", [P, T, 2]); pos_all = sb("pos", [P, T, 2], i32); pos_in_all = sb("pos_in", [P, T, 2], i32)
        tile_word_all = sb("tile_word", [1, MOST_TILES // 4], i32); tile_row_all = sb("tile_row", [1, MOST_TILES], i32)
        tile_groups = sb("tile_groups", [1, 1], i32)
        pad_row_all = sb("pad_row", [1, 16], i32)

        def routing(E):
            return (wts_all, pos_all, pos_in_all, comb_all[0:P, 0:T * E].rearrange("p (t e) -> p t e", e=E),
                    tile_word_all, tile_row_all, pad_row_all)

        def expert_weights(layer, E, F):
            if layer == 0:
                return view(arena, 27304, [E * DC * F]), view(arena, 0, [E * (F // 128) * D]), 0
            return view(arena, 0, [E * DC * F]), view(arena, E * DC * F, [E * (F // 128) * D]), 10

        end_stage()
        first_graph(True)
        end_stage()
        first_graph(False)
        end_stage()
        dispatch(0, E0, F0, L0_ffn_w1, L0_ffn_w2, True)
        end_stage()
        experts_stage(0, E0, F0, L0_ffn_w1, L0_ffn_w2, ACT.Gelu)
        end_stage()
        combine(0, E0, moe_tiles(E0), L0_ffn_b2)
        end_stage()
        second_graph()
        end_stage()
        dispatch(1, E1, F1, L1_ffn_w1, L1_ffn_w2, False)
        end_stage()
        experts_stage(1, E1, F1, L1_ffn_w1, L1_ffn_w2, ACT.Relu)
        end_stage()
        combine(1, E1, moe_tiles(E1), L1_ffn_b2)
        end_stage()


_INS = ['x', 'src', 'dst', 'edge_weight', 'L0_gnn_W1', 'L0_gnn_b1', 'L0_gnn_gamma', 'L0_gnn_beta', 'L0_gnn_W2', 'L0_gnn_b2',
        'L0_ffn_router_w', 'L0_ffn_w1', 'L0_ffn_b1', 'L0_ffn_w2', 'L0_ffn_b2', 'L1_gnn_W', 'L1_gnn_b', 'L1_ffn_gate_w',
        'L1_ffn_gate_b', 'L1_ffn_w1', 'L1_ffn_b1', 'L1_ffn_w2', 'L1_ffn_b2', 'L1_ffn_gamma', 'L1_ffn_beta']


def kernel(**inputs):
    import numpy as _np
    import concourse.bacc as _bacc
    from concourse import mybir as _mybir
    from concourse.bass_utils import run_bass_kernel_spmd as _run

    nc = _bacc.Bacc("TRN2", target_bir_lowering=False, num_devices=1)
    arrays, args = {}, []
    for name in _INS:
        a = _np.ascontiguousarray(inputs[name])
        arrays[f"in_{name}_dram"] = a
        args.append(nc.dram_tensor(f"in_{name}_dram", a.shape, _mybir.dt.from_np(a.dtype), kind="ExternalInput").ap())
    args.append(nc.dram_tensor("out_0_dram", (N, D), _mybir.dt.float32, kind="ExternalOutput").ap())
    gnn_moe(nc, *args)
    r = _run(nc, [arrays], core_ids=[0])
    return r.results[0]["out_0_dram"]
```
